# Optimizing a Trainium2 kernel written in Bass

```python
import numpy as np
import jax
import jax.numpy as jnp

def _softmax(x, axis=-1):
    return jax.nn.softmax(x, axis=axis)

def _gelu(x):
    return jax.nn.gelu(x, approximate=True)

def _silu(x):
    return jax.nn.silu(x)

def _sigmoid(x):
    return jax.nn.sigmoid(x)

def _layernorm(x, axis=-1, eps=1e-05):
    m = jnp.mean(x, axis=axis, keepdims=True)
    v = jnp.var(x, axis=axis, keepdims=True)
    return (x - m) / jnp.sqrt(v + eps)

def _scatter_add(tgt, idx, src, axis=0):
    return tgt.at[idx].add(src)

def _segment_sum(src, seg, n):
    return jax.ops.segment_sum(src, seg, n)
kernel_name = 'mk_decoder_postln_d1_seqx_r8_305cf8'

def setup_inputs(seed: int=0):
    np.random.seed(seed)
    _w = jnp.asarray

    def _rec_inputs():
        import jax
        import jax.numpy as jnp
        _rk = jax.random.key(seed)
        x = 7.22e-05 + 1 * jax.random.normal(jax.random.fold_in(_rk, 1), (2, 512, 128), jnp.float32)
        _lenS = 512 - jax.random.randint(jax.random.fold_in(_rk, 7), (2,), 0, max(1, 512 // 4) + 1, jnp.int32)
        _lenS2 = 154 - jax.random.randint(jax.random.fold_in(_rk, 8), (2,), 0, max(1, 154 // 4) + 1, jnp.int32)
        _ctx_1024P = jax.random.normal(jax.random.fold_in(_rk, 11), (2, 16, 128), jnp.float32)
        _ctx_1024c = jax.random.dirichlet(jax.random.fold_in(_rk, 511), 0.3 * jnp.ones((16,), jnp.float32), (2, 154))
        _ctx_1024t = jnp.einsum('bsk,bkd->bsd', _ctx_1024c, _ctx_1024P)
        _ctx_1024t = _ctx_1024t * jax.lax.rsqrt(jnp.mean(jnp.square(_ctx_1024t)) + 1e-12) * 0.953939
        ctx_1024 = 4.13588e-05 + 0.999923 * (_ctx_1024t + 0.3 * jax.random.normal(jax.random.fold_in(_rk, 611), (2, 154, 128), jnp.float32))
        return (x, ctx_1024)
    x, ctx_1024 = _rec_inputs()

    def _L0_attn_setup():
        import jax, jax.numpy as jnp
        import numpy as np
        EPS = 1e-06
        H = 16

        def _phi(x):
            return jax.nn.elu(x) + 1.0
        key = jax.random.key(seed)
        ks = jax.random.split(key, 6)
        B, N, D = (4, 1024, 128)
        s = 1.0 / np.sqrt(D)
        return {'x': jax.random.normal(ks[0], (B, N, D), dtype=jnp.float32), 'Wq': jax.random.normal(ks[1], (D, D), dtype=jnp.float32) * s, 'Wk': jax.random.normal(ks[2], (D, D), dtype=jnp.float32) * s, 'Wv': jax.random.normal(ks[3], (D, D), dtype=jnp.float32) * s, 'Wo': jax.random.normal(ks[4], (D, D), dtype=jnp.float32) * s, 'bo': jnp.zeros((D,), dtype=jnp.float32)}
    _L0_attn_all = _L0_attn_setup()
    _L0_attn_in = {k: v for k, v in _L0_attn_all.items() if k in ('Wq', 'Wk', 'Wv', 'Wo', 'bo')}
    del _L0_attn_all

    def _L0_xattn_setup():
        import jax, jax.numpy as jnp
        import numpy as np
        B, S, D, H = (4, 256, 128, 16)
        DEPTH = D // H
        NEG = 10000000000.0

        def _split_heads(x):
            b, s, _ = x.shape
            return x.reshape(b, s, H, DEPTH).transpose(0, 2, 1, 3)
        key = jax.random.key(seed)
        ks = jax.random.split(key, 11)
        sc = 0.02
        return {'q': jax.random.normal(ks[0], (B, S, D), jnp.float32), 'v': jax.random.normal(ks[1], (B, S, D), jnp.float32), 'k': jax.random.normal(ks[2], (B, S, D), jnp.float32), 'Wq': jax.random.normal(ks[3], (D, D), jnp.float32) * sc, 'bq': jnp.zeros((D,), jnp.float32), 'Wk': jax.random.normal(ks[4], (D, D), jnp.float32) * sc, 'bk': jnp.zeros((D,), jnp.float32), 'Wv': jax.random.normal(ks[5], (D, D), jnp.float32) * sc, 'bv': jnp.zeros((D,), jnp.float32), 'Wo': jax.random.normal(ks[6], (D, D), jnp.float32) * sc, 'bo': jnp.zeros((D,), jnp.float32), 'mask': 1}
    _L0_xattn_all = _L0_xattn_setup()
    _L0_xattn_in = {k: v for k, v in _L0_xattn_all.items() if k in ('Wq', 'bq', 'Wk', 'bk', 'Wv', 'bv', 'Wo', 'bo')}
    del _L0_xattn_all

    def _L0_ffn_setup():
        import jax, jax.numpy as jnp
        import numpy as np
        S, B, D = (128, 2, 128)
        E, TOPK = (15, 3)
        F = 128
        FS = 256

        def _uinit(k, shape, out_dim):
            std = out_dim ** (-0.5)
            return jax.random.uniform(k, shape, jnp.float32, -std, std)
        key = jax.random.key(seed)
        ks = jax.random.split(key, 10)
        return {'x': jax.random.normal(ks[0], (S, B, D), jnp.float32), 'gate_w': jax.random.normal(ks[1], (E, D), jnp.float32) * D ** (-0.5), 'fc1_w': _uinit(ks[2], (E, 2 * F, D), 2 * F), 'fc1_b': _uinit(ks[3], (E, 2 * F), 2 * F), 'geglu_mult': jnp.ones((E, F), jnp.float32), 'fc2_w': _uinit(ks[4], (E, D, F), D), 'fc2_b': _uinit(ks[5], (E, D), D), 's_fc1_w': _uinit(ks[6], (2 * FS, D), 2 * FS), 's_fc1_b': _uinit(ks[7], (2 * FS,), 2 * FS), 's_geglu_mult': jnp.ones((FS,), jnp.float32), 's_fc2_w': _uinit(ks[8], (D, FS), D), 's_fc2_b': _uinit(ks[9], (D,), D)}
    _L0_ffn_all = _L0_ffn_setup()
    _L0_ffn_in = {k: v for k, v in _L0_ffn_all.items() if k in ('gate_w', 'fc1_w', 'fc1_b', 'geglu_mult', 'fc2_w', 'fc2_b', 's_fc1_w', 's_fc1_b', 's_geglu_mult', 's_fc2_w', 's_fc2_b')}
    del _L0_ffn_all
    return {'x': x, 'ctx_1024': ctx_1024, 'L0_attn_Wq': _L0_attn_in['Wq'], 'L0_attn_Wk': _L0_attn_in['Wk'], 'L0_attn_Wv': _L0_attn_in['Wv'], 'L0_attn_Wo': _L0_attn_in['Wo'], 'L0_attn_bo': _L0_attn_in['bo'], 'L0_xattn_Wq': _L0_xattn_in['Wq'], 'L0_xattn_bq': _L0_xattn_in['bq'], 'L0_xattn_Wk': _L0_xattn_in['Wk'], 'L0_xattn_bk': _L0_xattn_in['bk'], 'L0_xattn_Wv': _L0_xattn_in['Wv'], 'L0_xattn_bv': _L0_xattn_in['bv'], 'L0_xattn_Wo': _L0_xattn_in['Wo'], 'L0_xattn_bo': _L0_xattn_in['bo'], 'L0_ffn_gate_w': _L0_ffn_in['gate_w'], 'L0_ffn_fc1_w': _L0_ffn_in['fc1_w'], 'L0_ffn_fc1_b': _L0_ffn_in['fc1_b'], 'L0_ffn_geglu_mult': _L0_ffn_in['geglu_mult'], 'L0_ffn_fc2_w': _L0_ffn_in['fc2_w'], 'L0_ffn_fc2_b': _L0_ffn_in['fc2_b'], 'L0_ffn_s_fc1_w': _L0_ffn_in['s_fc1_w'], 'L0_ffn_s_fc1_b': _L0_ffn_in['s_fc1_b'], 'L0_ffn_s_geglu_mult': _L0_ffn_in['s_geglu_mult'], 'L0_ffn_s_fc2_w': _L0_ffn_in['s_fc2_w'], 'L0_ffn_s_fc2_b': _L0_ffn_in['s_fc2_b']}

def reference(x, ctx_1024, L0_attn_Wq, L0_attn_Wk, L0_attn_Wv, L0_attn_Wo, L0_attn_bo, L0_xattn_Wq, L0_xattn_bq, L0_xattn_Wk, L0_xattn_bk, L0_xattn_Wv, L0_xattn_bv, L0_xattn_Wo, L0_xattn_bo, L0_ffn_gate_w, L0_ffn_fc1_w, L0_ffn_fc1_b, L0_ffn_geglu_mult, L0_ffn_fc2_w, L0_ffn_fc2_b, L0_ffn_s_fc1_w, L0_ffn_s_fc1_b, L0_ffn_s_geglu_mult, L0_ffn_s_fc2_w, L0_ffn_s_fc2_b):
    import jax
    import jax.numpy as jnp

    def _L0_attn_ref(x, Wq, Wk, Wv, Wo, bo):
        import jax, jax.numpy as jnp
        import numpy as np
        EPS = 1e-06
        H = 16

        def _phi(x):
            return jax.nn.elu(x) + 1.0
        B, N, D = x.shape
        d = D // H

        def proj(W):
            return (x @ W.T).reshape(B, N, H, d).transpose(0, 2, 1, 3)
        q = _phi(proj(Wq))
        k = _phi(proj(Wk))
        v = proj(Wv)
        kv = jnp.einsum('bhnd,bhne->bhde', k, v)
        numerator = jnp.einsum('bhnd,bhde->bhne', q, kv)
        k_sum = k.sum(axis=2)
        denominator = jnp.einsum('bhnd,bhd->bhn', q, k_sum)[..., None] + EPS
        out = numerator / denominator
        out = out.transpose(0, 2, 1, 3).reshape(B, N, D)
        return out @ Wo.T + bo

    def _L0_xattn_ref(q, v, k, Wq, bq, Wk, bk, Wv, bv, Wo, bo, mask):
        import jax, jax.numpy as jnp
        import numpy as np
        B, S, D, H = (4, 256, 128, 16)
        DEPTH = D // H
        NEG = 10000000000.0

        def _split_heads(x):
            b, s, _ = x.shape
            return x.reshape(b, s, H, DEPTH).transpose(0, 2, 1, 3)
        qh = _split_heads(q @ Wq + bq)
        kh = _split_heads(k @ Wk + bk)
        vh = _split_heads(v @ Wv + bv)
        scale = 1.0 / jnp.sqrt(jnp.asarray(DEPTH, jnp.float32))
        logits = jnp.einsum('bhqd,bhkd->bhqk', qh, kh) * scale
        if mask:
            nd, ns = (logits.shape[-2], logits.shape[-1])
            i = jnp.arange(nd)[:, None]
            j = jnp.arange(ns)[None, :]
            b = (i >= j - ns + nd).astype(logits.dtype)
            logits = logits * b - NEG * (1.0 - b)
        attn = jax.nn.softmax(logits, axis=-1)
        out = jnp.einsum('bhqk,bhkd->bhqd', attn, vh)
        out = out.transpose(0, 2, 1, 3).reshape(q.shape[0], -1, D)
        return out @ Wo + bo

    def _L0_ffn_ref(x, gate_w, fc1_w, fc1_b, geglu_mult, fc2_w, fc2_b, s_fc1_w, s_fc1_b, s_geglu_mult, s_fc2_w, s_fc2_b):
        import jax, jax.numpy as jnp
        import numpy as np
        S, B, D = (128, 2, 128)
        E, TOPK = (15, 3)
        F = 128
        FS = 256

        def _uinit(k, shape, out_dim):
            std = out_dim ** (-0.5)
            return jax.random.uniform(k, shape, jnp.float32, -std, std)
        s, b, d = x.shape
        xt = x.reshape(-1, d)
        T = xt.shape[0]
        logits = xt @ gate_w.T
        scores = jax.nn.softmax(logits, axis=-1)
        topk_w, topk_idx = jax.lax.top_k(scores, TOPK)
        topk_w = topk_w / (jnp.sum(topk_w, axis=-1, keepdims=True) + 1e-20)
        comb = jnp.zeros((T, E), xt.dtype).at[jnp.arange(T)[:, None], topk_idx].add(topk_w)
        h = jnp.einsum('td,efd->etf', xt, fc1_w) + fc1_b[:, None, :]
        xh, g = (h[..., :F], h[..., F:])
        a = jax.nn.gelu(g, approximate=False) * xh * geglu_mult[:, None, :]
        yexp = jnp.einsum('etf,edf->etd', a, fc2_w) + fc2_b[:, None, :]
        y = jnp.einsum('etd,te->td', yexp, comb)
        hs = xt @ s_fc1_w.T + s_fc1_b
        xs, gs = (hs[..., :FS], hs[..., FS:])
        as_ = jax.nn.gelu(gs, approximate=False) * xs * s_geglu_mult
        ys = as_ @ s_fc2_w.T + s_fc2_b
        return (y + ys).reshape(s, b, d)
    x = _layernorm(x + _L0_attn_ref(x, L0_attn_Wq, L0_attn_Wk, L0_attn_Wv, L0_attn_Wo, L0_attn_bo), axis=-1)
    x = _layernorm(x + _L0_xattn_ref(x, ctx_1024, ctx_1024, L0_xattn_Wq, L0_xattn_bq, L0_xattn_Wk, L0_xattn_bk, L0_xattn_Wv, L0_xattn_bv, L0_xattn_Wo, L0_xattn_bo, 1), axis=-1)
    x = _layernorm(x + _L0_ffn_ref(x, L0_ffn_gate_w, L0_ffn_fc1_w, L0_ffn_fc1_b, L0_ffn_geglu_mult, L0_ffn_fc2_w, L0_ffn_fc2_b, L0_ffn_s_fc1_w, L0_ffn_s_fc1_b, L0_ffn_s_geglu_mult, L0_ffn_s_fc2_w, L0_ffn_s_fc2_b), axis=-1)
    return x

_drawn_inputs = setup_inputs


def setup_inputs(seed=0):
    import zlib

    import numpy as np

    out = dict(_drawn_inputs(seed))
    spreads = {'L0_attn_bo': (0.0, 0.1),
     'L0_xattn_bq': (0.0, 2.0),
     'L0_xattn_bk': (0.0, 2.0),
     'L0_xattn_bv': (0.0, 0.352),
     'L0_xattn_bo': (0.0, 0.1),
     'L0_ffn_geglu_mult': (1.0, 0.6),
     'L0_ffn_s_geglu_mult': (1.0, 0.6)}
    factors = {'L0_attn_Wq': 3.654,
     'L0_xattn_Wq': 26.58,
     'L0_xattn_Wk': 24.8,
     'L0_ffn_fc1_b': 8.0,
     'L0_ffn_s_fc1_b': 8.0}
    for name, (base, spread) in spreads.items():
        noise = np.random.default_rng([zlib.crc32(name.encode()), seed]).standard_normal(out[name].shape)
        drawn = base * np.exp(spread * noise) if base else spread * noise
        out[name] = jnp.asarray(drawn.astype(out[name].dtype))
    for name, factor in factors.items():
        out[name] = (out[name] * factor).astype(out[name].dtype)
    return out
```

```python
from contextlib import ExitStack

import concourse.bass as bass
from concourse import mybir

F32 = mybir.dt.float32
F32R = mybir.dt.float32r
BF16 = mybir.dt.bfloat16
ALU = mybir.AluOpType
ACT = mybir.ActivationFunctionType
AX = mybir.AxisListType

P = 128
D = 128
B, N = 2, 512
NT = B * N // P
TPB = N // P
H, DH = 16, 8
NS = 154
C2 = NS - P
QA = N - NS
QB0 = QA - 2 * P
QB = P - QB0
G = 4
E = 15
U = 17
LNEPS = 1e-5
EPS = 1e-6
NEG = -1e10
PAD = -3e38
SCALE = DH ** -0.5
UPL = 4
assert QB == C2 and QB0 + QB == P and U == 1 + UPL * 4


def build(nc, x, xT, ctxT, wA, boA, wqs, wks, bqs, bks, wv, bv, wo, wop, boX, gateT, w1T, b1, mult,
          w2T, b2, comb_dram, out):
    with ExitStack() as ctx:
        def sb(name, shape, dt=F32):
            return ctx.enter_context(nc.sbuf_tensor(name, shape, dt))

        def sem(name):
            return ctx.enter_context(nc.semaphore(name))

        bank = [ctx.enter_context(nc.psum_tensor(f"bank{i}", [P, 512], F32)) for i in range(8)]

        ident = sb("ident", [P, P])
        ident16 = sb("ident16", [P, P], BF16)
        identr = sb("identr", [P, P], F32R)
        headmask = sb("headmask", [P, P])
        onehot = sb("onehot", [P, H])
        selM = sb("selM", [P, H, P], F32R)
        selD = sb("selD", [P, P])
        maskf = sb("maskf", [P, 2, P])
        maskS = sb("maskS", [P, P], BF16)
        maskT = sb("maskT", [P, P], BF16)
        lomask = sb("lomask", [P, 2])
        mcol = sb("mcol", [P, 1])

        x_sb = sb("x_sb", [P, NT, D])
        xT_sb = sb("xT_sb", [P, NT * P])
        wA_sb = sb("wA_sb", [P, 4 * D])
        ctx_sb = sb("ctx_sb", [P, B * NS])
        bo_bc = sb("bo_bc", [P, 3, D])
        wqs_sb = sb("wqs_sb", [P, G, P])
        wks_sb = sb("wks_sb", [P, G, P])
        bqk_sb = sb("bqk_sb", [P, 2, G])
        wv_sb = sb("wv_sb", [P, D])
        wo_sb = sb("wo_sb", [P, D])
        wop_sb = sb("wop_sb", [P, G, D])
        gate_sb = sb("gate_sb", [P, 16])
        w1_sb = sb("w1_sb", [P, U + 1, 2 * P])
        b1_sb = sb("b1_sb", [P, U + 1, 2])
        b1g = sb("b1g", [P, 2])
        mult_sb = sb("mult_sb", [P, U])
        w2_sb = sb("w2_sb", [P, U, D])
        b2_sb = sb("b2_sb", [16, D])

        ek = sb("ek", [P, 4, 2, P])
        ksb = sb("ksb", [P, NT, P])
        vsb = sb("vsb", [P, NT, P + 1])
        eq = sb("eq", [P, B, N])
        qT = sb("qT", [P, B, N])
        bd = sb("bd", [P, B, P + H])
        rden = sb("rden", [P, 4, 2, H])
        osb = sb("osb", [P, 4, 2, P])
        oT = sb("oT", [P, 2, 4, P])
        xb = sb("xb", [P, NT, D])
        y = sb("y", [P, NT, D])
        st = sb("st", [P, NT, 6])
        mv = sb("mv", [P, NT, 2])
        lnv = sb("lnv", [P, NT])
        rstd = sb("rstd", [P, NT])
        x1 = sb("x1", [P, NT, D])
        x1b = osb[:].rearrange("p i t d -> p (i t) d")
        epsc = sb("epsc", [P, 1])

        vx = sb("vx", [P, B, 2, D])
        va = sb("va", [P, B, 2, H, 32])
        mvT = sb("mvT", [P, B])
        mv_bc = sb("mv_bc", [P, B, P])
        mv_t2 = sb("mv_t2", [P, B, P])
        cb = sb("cb", [P, B, D])
        fullk = sb("fullk", [P, G, B * NS])
        fullq = fullk
        hisk = sb("hisk", [P, G, B * NS], F32R)
        hisq = hisk
        ks = sb("ks", [P, G, B * NS], F32R)
        qs = sb("qs", [P, G, B * NS], F32R)
        x1T = sb("x1T", [P, B, NS])
        mA = sb("mA", [P, B, H])
        mB = sb("mB", [P, B, H])
        mmA = sb("mmA", [P, B, P])
        mmB = sb("mmB", [P, B, P])
        mT = sb("mT", [P, B, NS], F32R)
        pT1 = sb("pT1", [P, B, H, NS])
        pT2 = sb("pT2", [P, B, H, C2])
        oraw = sb("oraw", [P, B, G, NS])
        rdx = fullk[:].rearrange("p g (b n) -> p (g b n)", b=B).rearrange("p (b g n) -> p b g n", b=B, g=G)
        on = sb("on", [P, B, G, 2 * P])
        st2 = sb("st2", [P, NT, 6])
        mv2 = sb("mv2", [P, NT, 2])
        lnv2 = sb("lnv2", [P, NT])
        rstd2 = sb("rstd2", [P, NT])
        y2 = x_sb
        x2 = xb

        x2hi = sb("x2hi", [P, B, N], F32R)
        x2lo = sb("x2lo", [P, B, N], F32R)
        ghi = sb("ghi", [P, 16], F32R)
        glo = sb("glo", [P, 16], F32R)
        LG = E + 5
        lg = sb("lg", [P, NT, LG])
        top = sb("top", [P, NT, 8])
        vals = sb("vals", [P, NT, 8])
        rep = sb("rep", [P, NT, LG])
        sel = sb("sel", [P, NT, E])
        dl = sb("dl", [P, NT, E])
        el = sb("el", [P, NT, E])
        em = sb("em", [P, NT, E])
        zs = sb("zs", [P, NT])
        s3 = sb("s3", [P, NT])
        dn = sb("dn", [P, NT])
        rd = sb("rd", [P, NT])
        comb = sb("comb", [P, NT, 16])
        combT = sb("combT", [16, B, N])
        comb_bc = pT1[:].rearrange("p b h n -> p (b h n)")[:, 0:UPL * B * N].rearrange("p (j b n) -> p j b n", j=UPL, b=B)
        w1hi = sb("w1hi", [P, 2 * 2 * P], F32R)
        w1lo = sb("w1lo", [P, 2 * 2 * P], F32R)
        w2hi = sb("w2hi", [P, 2 * D], F32R)
        w2lo = sb("w2lo", [P, 2 * D], F32R)
        gl = ek[:].rearrange("p i t n -> p (i t n)").rearrange("p (s n) -> p s n", s=2)
        a = eq
        ahi = sb("ahi", [P, 2 * N], F32R)
        alo = sb("alo", [P, 2 * N], F32R)
        yT = qT
        st3 = sb("st3", [P, NT, 6])
        mv3 = sb("mv3", [P, NT, 2])
        lnv3 = sb("lnv3", [P, NT])
        rstd3 = sb("rstd3", [P, NT])
        res = ksb

        names = ("ld_xT0 ld_xT1 ld_wA ld_x ld_ctx ld_wks ld_wqs ld_bias ld_wv ld_wo ld_wop ld_gate ld_w1 ld_w2 ld_small "
                 "b1g_ready c_mm0 c_mvt0 c_on0 c_gate0 c_lg0 c_comb0 c_w1pad c_selD0 lomask_ready y2a_ready yT0_ready yT1_ready c_ident c_ident16 c_headmask c_onehot c_selM c_selD c_maskf c_mask16 c_misc c_va0 c_zero "
                 "kv_mm q_mm ek_done ekmin_done k_ready v_ready eq_done eqmin_done q_ready kvs_mm bd_ready bdk_ready "
                 "num_mm den_ready rden_ready o_ready oT_mm oT_ready wo_mm xb_ready y_ready st_done mv_ready lnv_done "
                 "rstd_ready x1_ready x1b_ready vx_mm vx_ready va_ready mean_mm mean_ready mvbc_ready cb_mm cb_ready "
                 "kst_mm kst_full kst_his ks_ready qst_mm qst_full qst_his qs_ready x1T_mm x1T_ready "
                 "s_mm m_ready mhi_ready mlo_ready mmhi_ready mt_mm mT_ready sT_mm p_ready pv_mm oraw_ready db_mm rdx_ready "
                 "on_ready wox_mm y2_ready st2_done mv2_ready lnv2_done rstd2_ready x2_ready x2T_mm x2hi_ready x2lo_ready "
                 "g_hi g_lo lg_mm lg_ready top_ready vals_ready rep_ready sel_ready dl_ready el_ready em_ready zs_ready s3_ready dn_ready "
                 "rd_ready comb_ready cT_mm cT_ready comb_stored "
                 "w1hi_ready w1lo_ready w2hi_ready w2lo_ready g_mm h_mm gelu_done gc_ready a_ready ahi_ready alo_ready fc2_mm "
                 "ybias_mm yT_ready yt_mm y3_ready st3_done mv3_ready lnv3_done rstd3_ready res_ready stored").split()
        S = {n: sem(n) for n in names}
        slot_filled = [sem(f"slot_filled{j}") for j in range(UPL)]

        block = ctx.enter_context(nc.Block())

        PAIRS = [(2, 3), (6, 7), (0, 1), (4, 5)]
        POS = {t: 2 * i + j for i, pr in enumerate(PAIRS) for j, t in enumerate(pr)}
        NUMBANK = [4, 5, 0, 1]
        KSTBANK = [7, 2, 3, 6]
        WOBANK = [6, 7]

        ORDER2 = [0, 1, 4, 5, 2, 3, 6, 7]

        def slot(k):
            return k // G, k % G

        @block.sync
        def _(sp):
            sp.dma_start(wA_sb[:], wA).then_inc(S["ld_wA"], 16)
            sp.dma_start(ctx_sb[:], ctxT).then_inc(S["ld_ctx"], 16)
            sp.dma_start(wv_sb[:], wv).then_inc(S["ld_wv"], 16)
            sp.dma_start(wks_sb[:], wks).then_inc(S["ld_wks"], 16)
            sp.dma_start(bqk_sb[:, 0, :], bqs).then_inc(S["ld_bias"], 16)
            sp.dma_start(bqk_sb[:, 1, :], bks).then_inc(S["ld_bias"], 16)
            for i, v in enumerate((boA, bv, boX)):
                sp.dma_start(bo_bc[:, i, :], v.partition_broadcast(P)).then_inc(S["ld_bias"], 16)
            sp.dma_start(x_sb[:], x.rearrange("b (k p) d -> p (b k) d", p=P)).then_inc(S["ld_x"], 16)
            sp.dma_start(wqs_sb[:], wqs).then_inc(S["ld_wqs"], 16)
            sp.dma_start(wo_sb[:], wo).then_inc(S["ld_wo"], 16)
            sp.dma_start(wop_sb[:], wop).then_inc(S["ld_wop"], 16)
            sp.dma_start(gate_sb[:, 0:E], gateT).then_inc(S["ld_gate"], 16)
            sp.dma_start(b1_sb[:, 0:U, :], b1).then_inc(S["ld_small"], 16)
            sp.dma_start(mult_sb[:], mult).then_inc(S["ld_small"], 16)
            sp.dma_start(b2_sb[:], b2).then_inc(S["ld_small"], 16)
            sp.dma_start(w1_sb[:, 0:U, :], w1T).then_inc(S["ld_w1"], 16)
            sp.dma_start(w2_sb[:], w2T).then_inc(S["ld_w2"], 16)

            sp.wait_ge(S["cT_ready"], B)
            sp.dma_start(comb_dram, combT[0:E, :, :]).then_inc(S["comb_stored"], 16)
            sp.wait_ge(S["comb_stored"], 16)
            sp.wait_ge(S["pv_mm"], 8)
            for j in range(1, UPL):
                sp.dma_start(comb_bc[:, j, :, :], comb_dram[j - 1, :, :].partition_broadcast(P)).then_inc(slot_filled[j], 16)
            with sp.Fori(0, (U - 1) // UPL - 1) as i:
                for j in range(UPL):
                    sp.wait_ge(S["gc_ready"], 8 * i + 2 * (j + 2))
                    sp.dma_start(comb_bc[:, j, :, :], comb_dram[bass.ds(4 * i + (UPL + j - 1), 1), :, :].rearrange("a b n -> (a b) n").partition_broadcast(P)).then_inc(slot_filled[j], 16)

            for i in range(4):
                sp.wait_ge(S["res_ready"], 2 * (i + 1))
                sp.dma_start(out.rearrange("b (k p) d -> p (b k) d", p=P)[:, 2 * i:2 * i + 2, :],
                             res[:, 2 * i:2 * i + 2, :]).then_inc(S["stored"], 16)
            sp.wait_ge(S["stored"], 64)

        @block.tensor
        def _(pe):
            mm = nc.tensor.matmul

            pe.wait_ge(S["ld_wA"], 16)
            pe.wait_ge(S["ld_xT0"], 16)
            for t in range(NT):
                if t == TPB:
                    pe.wait_ge(S["ld_xT1"], 16)
                i = mm(bank[t // 2][:, (t % 2) * 256:(t % 2) * 256 + 256], xT_sb[:, t * P:(t + 1) * P],
                       wA_sb[:, D:3 * D], start=True, stop=True)
                if t % 2:
                    i.then_inc(S["kv_mm"], 1)
            for b in range(B):
                mm(bank[4 + b][:], wA_sb[:, 0:D], xT_sb[:, b * N:(b + 1) * N], start=True, stop=True).then_inc(S["q_mm"], 1)
            pe.wait_ge(S["ld_ctx"], 16)
            pe.wait_ge(S["ld_wv"], 16)
            for b in range(B):
                for c, (k0, n) in enumerate(((0, P), (P, C2))):
                    i = mm(bank[6][0:n, (2 * b + c) * D:(2 * b + c + 1) * D], ctx_sb[:, b * NS + k0:b * NS + k0 + n],
                           wv_sb[:], start=True, stop=True)
            i.then_inc(S["vx_mm"], 1)

            def kstack(g):
                mm(bank[KSTBANK[g]][:, 0:B * NS], wks_sb[:, g, :], ctx_sb[:], start=True, stop=True).then_inc(S["kst_mm"], 1)

            pe.wait_ge(S["ld_wks"], 16)
            kstack(0)
            for b in range(B):
                pe.wait_ge(S["k_ready"], 2 * b + 2)
                pe.wait_ge(S["v_ready"], 2 * b + 2)
                pe.wait_ge(S["c_misc"], 1)
                for k in range(TPB):
                    i = mm(bank[b][:, 0:P + 1], ksb[:, b * TPB + k, :], vsb[:, b * TPB + k, :],
                           start=(k == 0), stop=(k == TPB - 1))
                i.then_inc(S["kvs_mm"], 1)
            kstack(1)
            kstack(2)
            def num(i):
                b = PAIRS[i][0] // TPB
                pe.wait_ge(S["q_ready"], b + 1)
                pe.wait_ge(S["bdk_ready"], b + 1)
                if i == 2:
                    pe.wait_ge(S["bdk_ready"], B)
                if i < 2:
                    pe.wait_ge(S["q_ready"], i + 1)
                for j, t in enumerate(PAIRS[i]):
                    r = mm(bank[NUMBANK[i]][:, j * 256:j * 256 + P + H], qT[:, b, (t % TPB) * P:(t % TPB + 1) * P],
                           bd[:, b, :], start=True, stop=True)
                r.then_inc(S["num_mm"], 1)

            def o_transposes(i):
                pe.wait_ge(S["o_ready"], i + 1)
                if i == 0:
                    pe.wait_ge(S["c_ident"], 1)
                    pe.wait_ge(S["kst_full"], 2)
                if i == 2:
                    pe.wait_ge(S["kst_full"], 3)
                for j in range(2):
                    c = (i % 2) * 2 + j
                    r = nc.tensor.transpose(bank[2 + i // 2][:, c * P:(c + 1) * P], osb[:, i, j, :], ident[:])
                if i % 2:
                    r.then_inc(S["oT_mm"], 1)

            def wo_a(h):
                pe.wait_ge(S["oT_ready"], h + 1)
                if h == 0:
                    pe.wait_ge(S["kst_full"], 4)
                else:
                    pe.wait_ge(S["cb_ready"], 1)
                for c in range(4):
                    r = mm(bank[WOBANK[h]][:, c * P:(c + 1) * P], oT[:, h, c, :], wA_sb[:, 3 * D:4 * D], start=True, stop=True)
                r.then_inc(S["wo_mm"], 1)

            num(0)
            num(1)
            o_transposes(0)
            pe.wait_ge(S["vx_ready"], 2)
            kstack(3)
            pe.wait_ge(S["kst_full"], 1)
            for b in range(B):
                mm(bank[7][:, b:b + 1], vx[:, b, 0, :], mcol[:], start=True, stop=False)
                i = mm(bank[7][:, b:b + 1], vx[0:C2, b, 1, :], mcol[0:C2, :], start=False, stop=True)
            i.then_inc(S["mean_mm"], 1)
            o_transposes(1)
            num(2)
            num(3)
            wo_a(0)
            o_transposes(2)
            pe.wait_ge(S["mvbc_ready"], 2 * B)
            pe.wait_ge(S["ld_wo"], 16)
            for b in range(B):
                i = mm(bank[7][:, 128 + b * P:128 + (b + 1) * P], mv_bc[:, b, :], wo_sb[:], start=True, stop=True)
            i.then_inc(S["cb_mm"], 1)
            o_transposes(3)
            wo_a(1)
            for b in range(B):
                pe.wait_ge(S["x1_ready"], 2 * b + 2)
                for j in range(2):
                    r = nc.tensor.transpose(bank[4 + b][:, j * P:(j + 1) * P], x1[:, b * TPB + 2 + j, :], ident[:])
                r.then_inc(S["x1T_mm"], 1)
            pe.wait_ge(S["x1T_ready"], B)
            pe.wait_ge(S["ld_wqs"], 16)
            pe.wait_ge(S["o_ready"], 4)
            pe.wait_ge(S["oT_ready"], 2)
            for g in range(G):
                mm(bank[g][:, 0:B * NS], wqs_sb[:, g, :], x1T[:].rearrange("p b n -> p (b n)"), start=True, stop=True)\
                    .then_inc(S["qst_mm"], 1)

            pe.wait_ge(S["qs_ready"], G)
            pe.wait_ge(S["ks_ready"], G)
            pe.wait_ge(S["c_mask16"], 2)
            pe.wait_ge(S["c_ident16"], 1)

            def scores(n):
                b, c = divmod(n, 8)
                bk = bank[n % 2]
                if n >= 2:
                    pe.wait_ge(S["m_ready"], 2 * (n - 1))
                for j in range(2):
                    v, g = slot(2 * c + j)
                    a0 = j * NS
                    b0 = 2 * NS + j * C2
                    rows = slice(32 * v, 32 * v + 32)
                    q0 = b * NS
                    mm(bk[:, a0:a0 + NS], qs[rows, g, q0 + QB:q0 + NS], ks[rows, g, q0:q0 + NS],
                       start=(j == 0), stop=False, skip_group_check=True, tile_position=(32 * v, 0))
                    mm(bk[0:QB, b0:b0 + C2], qs[rows, g, q0:q0 + QB], ks[rows, g, q0:q0 + C2],
                       start=False, stop=False, skip_group_check=True, tile_position=(32 * v, 0))
                for j in range(2):
                    mm(bk[:, j * NS + C2:(j + 1) * NS], ident16[:], maskS[:],
                       start=False, stop=False, skip_group_check=True)
                    r = mm(bk[0:QB, 2 * NS + j * C2:2 * NS + (j + 1) * C2], ident16[0:QB, 0:QB], maskS[0:QB, 0:C2],
                           start=False, stop=(j == 1), skip_group_check=True)
                r.then_inc(S["s_mm"], 1)

            def max_transposes(b):
                pe.wait_ge(S["mlo_ready"], 2 * (b + 1))
                nc.tensor.transpose(bank[6 + b][:, 0:QB], mmB[0:QB, b, :], ident[0:QB, 0:QB])
                nc.tensor.transpose(bank[6 + b][:, QB:NS], mmA[:, b, :], ident[:]).then_inc(S["mt_mm"], 1)

            def scores_T(n):
                b, c = divmod(n, 8)
                bk = bank[2 + n % 2]
                pe.wait_ge(S["mT_ready"], b + 1)
                if n == 0:
                    pe.wait_ge(S["c_selM"], 1)
                if n >= 2:
                    pe.wait_ge(S["p_ready"], 2 * (n - 1))
                q0 = b * NS
                for j in range(2):
                    k = 2 * c + j
                    a0 = j * NS
                    b0 = 2 * NS + j * C2
                    mm(bk[:, a0:a0 + NS], selM[:, k, :], mT[:, b, :], start=(j == 0), stop=False, skip_group_check=True)
                    mm(bk[0:C2, b0:b0 + C2], selM[:, k, 0:C2], mT[:, b, P:NS], start=False, stop=False, skip_group_check=True)
                    mm(bk[:, a0:a0 + P], ident16[:], maskT[:], start=False, stop=False, skip_group_check=True)
                    mm(bk[0:C2, b0:b0 + C2], ident16[0:C2, 0:C2], maskT[0:C2, 0:C2], start=False, stop=False,
                       skip_group_check=True)
                for j in range(2):
                    v, g = slot(2 * c + j)
                    a0 = j * NS
                    b0 = 2 * NS + j * C2
                    rows = slice(32 * v, 32 * v + 32)
                    mm(bk[:, a0:a0 + NS], ks[rows, g, q0:q0 + P], qs[rows, g, q0:q0 + NS],
                       start=False, stop=False, skip_group_check=True, tile_position=(32 * v, 0))
                    r = mm(bk[0:C2, b0:b0 + C2], ks[rows, g, q0 + P:q0 + NS], qs[rows, g, q0 + P:q0 + NS],
                           start=False, stop=(j == 1), skip_group_check=True, tile_position=(32 * v, 0))
                r.then_inc(S["sT_mm"], 1)

            def pv(b, u):
                pe.wait_ge(S["p_ready"], 2 * (8 * b + 2 * u + 2))
                pe.wait_ge(S["va_ready"], 1 + 2 * B)
                if b == 1 and u == 0:
                    pe.wait_ge(S["oraw_ready"], 2)
                o = bank[4 + u // 2][:, (u % 2) * NS:(u % 2 + 1) * NS]
                for w in range(G):
                    k = G * u + w
                    mm(o[32 * w:32 * w + 32, :], va[:, b, 0, k, :], pT1[:, b, k, :], start=(u % 2 == 0), stop=False,
                       skip_group_check=True, tile_position=(0, 32 * w))
                for w in range(G):
                    k = G * u + w
                    r = mm(o[32 * w:32 * w + 32, P:NS], va[0:C2, b, 1, k, :], pT2[0:C2, b, k, :], start=False, stop=True,
                           skip_group_check=True, tile_position=(0, 32 * w))
                r.then_inc(S["pv_mm"], 1)

            for n in range(8):
                scores(n)
            max_transposes(0)
            for c in range(8):
                scores_T(c)
                scores(8 + c)
                if c >= 3 and c % 2:
                    pv(0, (c - 3) // 2)
            max_transposes(1)

            def den_bc(b):
                pe.wait_ge(S["c_selD"], 1)
                for hf in range(2):
                    pe.wait_ge(S["oraw_ready"], 2 * b + hf + 1)
                    if b:
                        pe.wait_ge(S["rdx_ready"], 2)
                    mm(bank[6 + hf][:, 0:2 * NS], selD[:], oraw[:, b, 2 * hf:2 * hf + 2, :].rearrange("p u n -> p (u n)"),
                       start=True, stop=True).then_inc(S["db_mm"], 1)

            def wo_x(b):
                pe.wait_ge(S["on_ready"], 2 * (b + 1))
                pe.wait_ge(S["ld_wop"], 16)
                pe.wait_ge(S["m_ready"], 32)
                for j in range(2):
                    o = bank[b][:, j * P:(j + 1) * P]
                    if j == 0:
                        mm(o, mv_t2[:, b, :], wo_sb[:], start=True, stop=False)
                    for u in range(G):
                        r = mm(o, on[:, b, u, j * P:(j + 1) * P], wop_sb[:, u, :], start=(u == 0 and j == 1),
                               stop=(u == G - 1))
                r.then_inc(S["wox_mm"], 1)

            for c in range(8):
                scores_T(8 + c)
                if c == 1:
                    pv(0, 3)
                if c == 4:
                    den_bc(0)
                if c >= 3 and c % 2:
                    pv(1, (c - 3) // 2)
            pv(1, 3)
            wo_x(0)

            def x2_transposes(b):
                pe.wait_ge(S["p_ready"], 32)
                for k in range(TPB):
                    pe.wait_ge(S["x2_ready"], ORDER2.index(b * TPB + k) + 1)
                    r = nc.tensor.transpose(bank[2 + b][:, k * P:(k + 1) * P], x2[:, b * TPB + k, :], ident[:])
                r.then_inc(S["x2T_mm"], 1)

            def router(b):
                pe.wait_ge(S["x2hi_ready"], b + 1)
                pe.wait_ge(S["x2lo_ready"], b + 1)
                pe.wait_ge(S["g_lo"], 1)
                pe.wait_ge(S["rdx_ready"], 4)
                for k in range(TPB):
                    o = bank[6 + b][:, k * 16:(k + 1) * 16]
                    c = slice(k * P, (k + 1) * P)
                    mm(o, x2hi[:, b, c], ghi[:], start=True, stop=False)
                    mm(o, x2hi[:, b, c], glo[:], start=False, stop=False)
                    r = mm(o, x2lo[:, b, c], ghi[:], start=False, stop=True)
                r.then_inc(S["lg_mm"], 1)

            x2_transposes(0)
            den_bc(1)
            router(0)
            wo_x(1)
            x2_transposes(1)
            router(1)

            def fc1(u, s, i=None):
                w = slice(u * 256 + P, u * 256 + 256), slice(u * 256, u * 256 + P)
                for part, (bk, signal) in enumerate(((bank[s], "g_mm"), (bank[2 + s], "h_mm"))):
                    c = w[part]
                    if i is not None:
                        n = i(0, s)
                        pe.wait_ge(S["gelu_done" if part == 0 else "a_ready"], n - 1)
                    mm(bk[:], w1hi[:, c], x2hi[:, s, :], start=True, stop=False)
                    mm(bk[:], w1hi[:, c], x2lo[:, s, :], start=False, stop=False)
                    mm(bk[:], w1lo[:, c], x2hi[:, s, :], start=False, stop=True).then_inc(S[signal], 1)

            def fc2(u, s, n):
                pe.wait_ge(S["alo_ready"], n + 1)
                hi, lo = ahi[:, s * N:(s + 1) * N], alo[:, s * N:(s + 1) * N]
                c = slice(u * D, (u + 1) * D)
                mm(bank[4 + s][:], w2hi[:, c], hi, start=False, stop=False, skip_group_check=True)
                mm(bank[4 + s][:], w2hi[:, c], lo, start=False, stop=False, skip_group_check=True)
                mm(bank[4 + s][:], w2lo[:, c], hi, start=False, stop=False, skip_group_check=True).then_inc(S["fc2_mm"], 1)

            pe.wait_ge(S["w1hi_ready"], 1)
            pe.wait_ge(S["w1lo_ready"], 1)
            pe.wait_ge(S["y2_ready"], B)
            for s in range(B):
                fc1(0, s)
            pe.wait_ge(S["c_ident16"], 2)
            for s in range(B):
                mm(bank[4 + s][:], identr[:], x2hi[:, s, :], start=True, stop=False, skip_group_check=True)
                mm(bank[4 + s][:], identr[:], x2lo[:, s, :], start=False, stop=False, skip_group_check=True)\
                    .then_inc(S["fc2_mm"], 1)

            for b in range(B):
                pe.wait_ge(S["comb_ready"], b + 1)
                for k in range(TPB):
                    r = nc.tensor.transpose(bank[6 + b][0:16, k * P:(k + 1) * P], comb[:, b * TPB + k, :], ident[:])
                r.then_inc(S["cT_mm"], 1)

            with pe.Fori(0, (U - 1) // UPL) as i:
                for j in range(UPL):
                    par = (1 + j) % 2
                    pe.wait_ge(S["w1hi_ready"], UPL * i + (j + 2))
                    pe.wait_ge(S["w1lo_ready"], UPL * i + (j + 2))
                    for s in range(B):
                        fc1(par, s, lambda _, s: 2 * UPL * i + (2 * (1 + j) + s))
                        if s == 0:
                            pe.wait_ge(S["w2hi_ready"], UPL * i + (j + 1))
                            pe.wait_ge(S["w2lo_ready"], UPL * i + (j + 1))
                        fc2(1 - par, s, 2 * UPL * i + (2 * j + s))
            for s in range(B):
                fc2((U - 1) % 2, s, 2 * (U - 1) + s)
                if s == 0:
                    pe.wait_ge(S["cT_ready"], B)
                    pe.wait_ge(S["ld_small"], 48)
                mm(bank[4 + s][:], b2_sb[:], combT[:, s, :], start=False, stop=True, skip_group_check=True)\
                    .then_inc(S["ybias_mm"], 1)
            for s in range(B):
                pe.wait_ge(S[f"yT{s}_ready"], 1)
                for k in range(TPB):
                    r = nc.tensor.transpose(bank[s][:, k * P:(k + 1) * P], yT[:, s, k * P:(k + 1) * P], ident[:])
                r.then_inc(S["yt_mm"], 1)

        @block.gpsimd
        def _(pool):
            pool.memset(vsb[:, :, P:P + 1], 1.0).then_inc(S["c_misc"], 1)
            pool.memset(mcol[:], 1.0 / NS).then_inc(S["c_misc"], 1)
            pool.memset(epsc[:], LNEPS).then_inc(S["c_misc"], 1)
            pool.memset(headmask[:], 1.0).then_inc(S["c_headmask"], 1)
            pool.memset(ident[:], 0.0).then_inc(S["c_zero"], 1)
            pool.wait_ge(S["c_headmask"], 1)
            hm = headmask[:].rearrange("p (h d) -> p h d", d=DH)
            pool.affine_select(out=hm, in_=hm, compare_op=ALU.is_ge, fill=0.0, base=0,
                               pattern=[[-DH, H], [0, DH]], channel_multiplier=1).then_inc(S["c_headmask"], 1)
            pool.wait_ge(S["c_headmask"], 2)
            pool.affine_select(out=hm, in_=hm, compare_op=ALU.is_ge, fill=0.0, base=DH - 1,
                               pattern=[[DH, H], [0, DH]], channel_multiplier=-1).then_inc(S["c_headmask"], 1)
            pool.wait_ge(S["c_zero"], 1)
            pool.affine_select(out=ident[:], in_=ident[:], compare_op=ALU.not_equal, fill=1.0, base=0,
                               pattern=[[-1, P]], channel_multiplier=1).then_inc(S["c_ident"], 1)
            pool.wait_ge(S["ld_x"], 16)
            pool.wait_ge(S["ld_bias"], 80)
            for t0, t1 in PAIRS:
                pool.tensor_tensor(xb[:, t0:t1 + 1, :], x_sb[:, t0:t1 + 1, :],
                                   bo_bc[:, 0:1, :].broadcast_to([P, 2, D]), ALU.add).then_inc(S["xb_ready"], 1)
            pool.memset(maskf[:], 0.0).then_inc(S["c_maskf"], 1)
            pool.memset(selD[:], 0.0).then_inc(S["c_selD0"], 1)
            pool.memset(onehot[:], 0.0).then_inc(S["c_onehot"], 1)
            pool.wait_ge(S["c_onehot"], 1)
            for n, base in enumerate((0, -H)):
                pool.wait_ge(S["c_onehot"], n + 1)
                pool.affine_select(out=onehot[:], in_=onehot[:], compare_op=ALU.not_equal, fill=1.0, base=base,
                                   pattern=[[-1, H]], channel_multiplier=1).then_inc(S["c_onehot"], 1)
            pool.wait_ge(S["c_maskf"], 1)
            pool.affine_select(out=maskf[:, 0, :], in_=maskf[:, 0, :], compare_op=ALU.is_ge, fill=NEG, base=0,
                               pattern=[[-1, P]], channel_multiplier=1).then_inc(S["c_maskf"], 1)
            pool.affine_select(out=maskf[:, 1, :], in_=maskf[:, 1, :], compare_op=ALU.is_ge, fill=NEG, base=0,
                               pattern=[[1, P]], channel_multiplier=-1).then_inc(S["c_maskf"], 1)
            pool.wait_ge(S["c_selD0"], 1)
            sd = selD[:].rearrange("p (w c) -> p w c", c=32)
            pool.affine_select(out=sd, in_=sd, compare_op=ALU.not_equal, fill=1.0, base=-DH,
                               pattern=[[-32, G], [0, 32]], channel_multiplier=1).then_inc(S["c_selD"], 1)
            pool.memset(mmA[:], 0.0).then_inc(S["c_mm0"], 1)
            pool.memset(mmB[:], 0.0).then_inc(S["c_mm0"], 1)
            pool.memset(va[:], 0.0).then_inc(S["c_va0"], 1)
            pool.wait_ge(S["c_va0"], 1)
            pool.memset(va[:, :, :, :, DH:DH + 1], 1.0).then_inc(S["va_ready"], 1)
            pool.wait_ge(S["vx_ready"], 2)
            for b in range(B):
                for c, n in enumerate((P, C2)):
                    pool.tensor_copy(va[0:n, b, c, :, 0:DH].rearrange("p (v g) d -> p v g d", v=G),
                                     vx[0:n, b, c, :].rearrange("p (g v d) -> p v g d", g=G, v=G))                        .then_inc(S["va_ready"], 1)
            for g in range(G):
                pool.wait_ge(S["kst_full"], g + 1)
                pool.wait_ge(S["lomask_ready"], 2)
                pool.tensor_scalar(hisk[:, g, :], fullk[:, g, :], lomask[:, 1:2], None, ALU.mult).then_inc(S["kst_his"], 1)
                pool.wait_ge(S["kst_his"], g + 1)
                pool.tensor_tensor(ks[:, g, :], fullk[:, g, :], hisk[:, g, :].bitcast(F32), ALU.subtract)                    .then_inc(S["ks_ready"], 1)
            pool.memset(mv_t2[:], 0.0).then_inc(S["c_mvt0"], 1)
            pool.memset(on[:], 0.0).then_inc(S["c_on0"], 1)
            pool.memset(gate_sb[:, E:16], 0.0).then_inc(S["c_gate0"], 1)
            pool.memset(lg[:], PAD).then_inc(S["c_lg0"], 1)
            pool.memset(vals[:], PAD).then_inc(S["c_lg0"], 1)
            pool.memset(comb[:, :, E:16], 1.0).then_inc(S["c_comb0"], 1)
            pool.memset(w1_sb[:, U, :], 0.0).then_inc(S["c_w1pad"], 1)
            pool.memset(b1_sb[:, U, :], 0.0).then_inc(S["c_w1pad"], 1)

            for t in (0, 1, 4, 5):
                pool.wait_ge(S["cb_ready"], 1)
                pool.wait_ge(S["x1_ready"], POS[t] + 1)
                pool.tensor_tensor(y2[:, t, :], x1[:, t, :], cb[:, t // TPB, :], ALU.add).then_inc(S["y2a_ready"], 1)
            for n, t in enumerate((2, 3, 6, 7)):
                pool.wait_ge(S["x1_ready"], POS[t] + 1)
                pool.tensor_tensor(x1b[:, t, :], x1[:, t, :], bo_bc[:, 2, :], ALU.add).then_inc(S["x1b_ready"], 1)

            pool.wait_ge(S["pv_mm"], 8)
            pool.memset(comb_bc[:, 0, :, :], 1.0).then_inc(slot_filled[0], 16)

            def w1lo_stage(u, par):
                pool.wait_ge(S["w1hi_ready"], u + 1)
                pool.wait_ge(S["ld_w1"], 16)
                pool.tensor_tensor(w1lo[:, par * 256:par * 256 + 256], w1_sb[:, bass.ds(u, 1), :].rearrange("p a n -> p (a n)"),
                                   w1hi[:, par * 256:par * 256 + 256].bitcast(F32), ALU.subtract).then_inc(S["w1lo_ready"], 1)

            def gate_product(n, s, slot_):
                pool.wait_ge(S["gelu_done"], n + 1)
                pool.tensor_tensor(gl[:, s, :], gl[:, s, :], comb_bc[:, slot_, s, :], ALU.mult).then_inc(S["gc_ready"], 1)

            pool.wait_ge(S["c_w1pad"], 1)
            w1lo_stage(0, 0)
            w1lo_stage(1, 1)
            pool.wait_ge(slot_filled[0], 16)
            for s in range(B):
                gate_product(s, s, 0)
            with pool.Fori(0, (U - 1) // UPL) as i:
                for j in range(UPL):
                    u = UPL * i + (1 + j)
                    w1lo_stage(UPL * i + (2 + j), (2 + j) % 2)
                    pool.wait_ge(slot_filled[j], 16 * i + 16)
                    for s in range(B):
                        gate_product(2 * UPL * i + (2 * (1 + j) + s), s, j)

        @block.vector
        def _(dve):
            sub_, add_, mul_ = ALU.subtract, ALU.add, ALU.mult
            for i in range(4):
                dve.wait_ge(S["ek_done"], i + 1)
                dve.tensor_scalar(ek[:, i, :, :], ek[:, i, :, :], 1.0, None, ALU.min).then_inc(S["ekmin_done"], 1)
                dve.wait_ge(S["ekmin_done"], i + 1)
                dve.wait_ge(S["v_ready"], i + 1)
                dve.scalar_tensor_tensor(out=ksb[:, 2 * i:2 * i + 2, :],
                                         in0=bank[i][:].rearrange("p (t n) -> p t n", t=2)[:, :, 0:P], scalar=0.0,
                                         in1=ek[:, i, :, :], op0=ALU.max, op1=add_).then_inc(S["k_ready"], 1)
            for b in range(B):
                dve.wait_ge(S["eq_done"], b + 1)
                dve.tensor_scalar(eq[:, b, :], eq[:, b, :], 1.0, None, ALU.min).then_inc(S["eqmin_done"], 1)
                dve.wait_ge(S["eqmin_done"], b + 1)
                dve.scalar_tensor_tensor(out=qT[:, b, :], in0=bank[4 + b][:], scalar=0.0, in1=eq[:, b, :],
                                         op0=ALU.max, op1=add_).then_inc(S["q_ready"], 1)
            dve.wait_ge(S["c_headmask"], 3)
            for b in range(B):
                dve.wait_ge(S["kvs_mm"], b + 1)
                dve.tensor_tensor(bd[:, b, 0:P], bank[b][:, 0:P], headmask[:], mul_).then_inc(S["bd_ready"], 1)
                dve.tensor_scalar(bd[:, b, P:P + H], headmask[:, 0:P:DH], bank[b][:, P:P + 1], None, mul_)                    .then_inc(S["bdk_ready"], 1)
            dve.wait_ge(S["vx_mm"], 1)
            dve.wait_ge(S["ld_bias"], 80)
            v6 = bank[6][:].rearrange("p (b c d) -> p b c d", b=B, c=2)
            for c, n in enumerate((P, C2)):
                dve.tensor_tensor(vx[0:n, :, c, :], v6[0:n, :, c, :], bo_bc[0:n, 1:2, :].broadcast_to([n, B, D]), add_)                    .then_inc(S["vx_ready"], 1)
            hw = headmask[:].rearrange("p (w c d) -> p w c d", w=G, c=4)
            dve.tensor_reduce(lomask[:, 0:1], hw[:, :, 2:4, 0], AX.XY, add_).then_inc(S["lomask_ready"], 1)
            dve.tensor_reduce(lomask[:, 1:2], headmask[:, DH:P:2 * DH], AX.X, add_).then_inc(S["lomask_ready"], 1)

            def kfull(g):
                dve.wait_ge(S["kst_mm"], g + 1)
                dve.tensor_scalar(fullk[:, g, :], bank[KSTBANK[g]][:, 0:B * NS], bqk_sb[:, 1, g:g + 1], None, add_)                    .then_inc(S["kst_full"], 1)

            def normalise(i):
                dve.wait_ge(S["num_mm"], i + 1)
                o = bank[NUMBANK[i]][:].rearrange("p (t n) -> p t n", t=2)
                dve.tensor_scalar(rden[:, i, :, :], o[:, :, P:P + H], EPS, None, add_).then_inc(S["den_ready"], 1)
                dve.wait_ge(S["den_ready"], i + 1)
                dve.reciprocal(rden[:, i, :, :], rden[:, i, :, :]).then_inc(S["rden_ready"], 1)
                dve.wait_ge(S["rden_ready"], i + 1)
                dve.tensor_tensor(osb[:, i, :, :].rearrange("p t (h d) -> p t h d", h=H),
                                  o[:, :, 0:P].rearrange("p t (h d) -> p t h d", h=H),
                                  rden[:, i, :, :].unsqueeze(3).broadcast_to([P, 2, H, DH]), mul_).then_inc(S["o_ready"], 1)

            kfull(0)
            kfull(1)
            normalise(0)
            kfull(2)
            normalise(1)
            kfull(3)
            dve.wait_ge(S["mean_mm"], 1)
            dve.wait_ge(S["c_mvt0"], 1)
            for b in range(B):
                dve.tensor_copy(mv_bc[:, b, :], bank[7][:, b:b + 1].broadcast_to([P, P])).then_inc(S["mvbc_ready"], 1)
                dve.tensor_copy(mv_t2[:, b, 0:QB0], bank[7][:, b:b + 1].broadcast_to([P, QB0])).then_inc(S["mvbc_ready"], 1)
            normalise(2)
            normalise(3)
            dve.wait_ge(S["cb_mm"], 1)
            dve.tensor_tensor(cb[:], bank[7][:, P:P + B * D].rearrange("p (b d) -> p b d", b=B),
                              bo_bc[:, 2:3, :].broadcast_to([P, B, D]), add_).then_inc(S["cb_ready"], 1)

            def stats(src, st_, mv_, tiles, n0, s_st, s_mv):
                for t in tiles:
                    dve.bn_stats(st_[:, t, :], src(t)).then_inc(S[s_st], 1)
                for n, t in enumerate(tiles):
                    dve.wait_ge(S[s_st], n0 + n + 1)
                    dve.bn_aggr(mv_[:, t, :], st_[:, t, :]).then_inc(S[s_mv], 1)

            def apply(dst, src, mv_, rs, tiles, signal):
                for t in tiles:
                    dve.tensor_scalar(dst[:, t, :], src(t), mv_[:, t, 0:1], rs[:, t:t + 1], sub_, mul_).then_inc(S[signal], 1)

            def first_norm(h):
                dve.wait_ge(S["wo_mm"], h + 1)
                for q in range(2):
                    i = 2 * h + q
                    t = PAIRS[i][0]
                    dve.wait_ge(S["xb_ready"], i + 1)
                    dve.tensor_tensor(y[:, t:t + 2, :], bank[WOBANK[h]][:, q * 256:(q + 1) * 256].rearrange("p (t d) -> p t d", t=2),
                                      xb[:, t:t + 2, :], add_).then_inc(S["y_ready"], 1)
                dve.wait_ge(S["y_ready"], 2 * h + 2)
                stats(lambda t: y[:, t, :], st, mv, PAIRS[2 * h] + PAIRS[2 * h + 1], 4 * h, "st_done", "mv_ready")

            def first_apply(h):
                dve.wait_ge(S["rstd_ready"], h + 1)
                apply(x1, lambda t: y[:, t, :], mv, rstd, PAIRS[2 * h] + PAIRS[2 * h + 1], "x1_ready")

            first_norm(0)
            first_apply(0)
            first_norm(1)
            dve.wait_ge(S["ks_ready"], G)
            for g in range(G):
                dve.wait_ge(S["qst_mm"], g + 1)
                dve.tensor_scalar(fullq[:, g, :], bank[g][:, 0:B * NS], bqk_sb[:, 0, g:g + 1], SCALE, add_, mul_)                    .then_inc(S["qst_full"], 1)
            for g in range(G):
                dve.wait_ge(S["qst_his"], g + 1)
                dve.tensor_tensor(qs[:, g, :], fullq[:, g, :], hisq[:, g, :].bitcast(F32), sub_).then_inc(S["qs_ready"], 1)
                if g == 0:
                    dve.wait_ge(S["c_ident"], 1)
                    dve.wait_ge(S["c_maskf"], 3)
                    dve.tensor_copy(ident16[:], ident[:]).then_inc(S["c_ident16"], 1)
                    dve.tensor_copy(maskS[:], maskf[:, 0, :]).then_inc(S["c_mask16"], 1)
                    dve.tensor_copy(maskT[:], maskf[:, 1, :]).then_inc(S["c_mask16"], 1)
            first_apply(1)

            def maxima(n):
                b, c = divmod(n, 8)
                bk = bank[n % 2]
                dve.wait_ge(S["s_mm"], n + 1)
                dve.tensor_reduce(mA[:, b, 2 * c:2 * c + 2], bk[:, 0:2 * NS].rearrange("p (h n) -> p h n", h=2), AX.X, ALU.max)                    .then_inc(S["m_ready"], 1)
                dve.tensor_reduce(mB[0:QB, b, 2 * c:2 * c + 2], bk[0:QB, 2 * NS:2 * NS + 2 * C2].rearrange("p (h n) -> p h n", h=2),
                                  AX.X, ALU.max).then_inc(S["m_ready"], 1)

            def maxima_split(b):
                dve.wait_ge(S["m_ready"], 16 * (b + 1))
                dve.wait_ge(S["c_mm0"], 2)
                for mm_, m_, r in ((mmA, mA, P), (mmB, mB, QB)):
                    dve.tensor_scalar(mm_[0:r, b, 0:H].bitcast(F32R), m_[0:r, b, :], -1.0, None, mul_).then_inc(S["mhi_ready"], 1)
                for n, (mm_, m_, r) in enumerate(((mmA, mA, P), (mmB, mB, QB))):
                    dve.wait_ge(S["mhi_ready"], 2 * b + n + 1)
                    dve.scalar_tensor_tensor(out=mm_[0:r, b, H:2 * H], in0=m_[0:r, b, :], scalar=-1.0, in1=mm_[0:r, b, 0:H],
                                             op0=mul_, op1=sub_).then_inc(S["mlo_ready"], 1)
                dve.wait_ge(S["mt_mm"], b + 1)
                dve.tensor_copy(mT[:, b, :], bank[6 + b][:, 0:NS]).then_inc(S["mT_ready"], 1)

            for n in range(8):
                maxima(n)
                if n == 3:
                    dve.wait_ge(S["c_onehot"], 3)
                    dve.tensor_copy(selM[:], onehot[:].unsqueeze(2).broadcast_to([P, H, P])).then_inc(S["c_selM"], 1)
            maxima_split(0)
            for n in range(8, 16):
                maxima(n)
            maxima_split(1)

            def second_norm(tiles, n0):
                stats(lambda t: y2[:, t, :], st2, mv2, tiles, n0, "st2_done", "mv2_ready")

            def second_apply(tiles, n):
                dve.wait_ge(S["rstd2_ready"], n)
                apply(x2, lambda t: y2[:, t, :], mv2, rstd2, tiles, "x2_ready")

            dve.wait_ge(S["y2a_ready"], 4)
            second_norm((0, 1, 4, 5), 0)
            second_apply((0, 1, 4, 5), 1)

            dve.wait_ge(S["ld_gate"], 16)
            dve.wait_ge(S["c_gate0"], 1)
            dve.tensor_copy(ghi[:], gate_sb[:]).then_inc(S["g_hi"], 1)
            dve.wait_ge(S["g_hi"], 1)
            dve.tensor_tensor(glo[:], gate_sb[:], ghi[:].bitcast(F32), sub_).then_inc(S["g_lo"], 1)
            dve.tensor_copy(identr[:], ident[:]).then_inc(S["c_ident16"], 1)

            def b1g_stage(u, par):
                dve.wait_ge(S["ld_small"], 48)
                dve.tensor_copy(b1g[:, par:par + 1], b1_sb[:, bass.ds(u, 1), 1:2].rearrange("p a b -> p (a b)"))\
                    .then_inc(S["b1g_ready"], 1)

            def w1hi_stage(u, par):
                dve.wait_ge(S["ld_w1"], 16)
                dve.tensor_copy(w1hi[:, par * 256:par * 256 + 256], w1_sb[:, bass.ds(u, 1), :].rearrange("p a n -> p (a n)"))                    .then_inc(S["w1hi_ready"], 1)

            w1hi_stage(0, 0)
            w1hi_stage(1, 1)
            dve.wait_ge(S["c_w1pad"], 2)
            b1g_stage(0, 0)
            b1g_stage(1, 1)

            def o_normalise(b):
                dve.wait_ge(S["c_on0"], 1)
                for hf in range(2):
                    dve.wait_ge(S["db_mm"], 2 * b + hf + 1)
                    dve.reciprocal(rdx[:, b, 2 * hf:2 * hf + 2, :], bank[6 + hf][:, 0:2 * NS].rearrange("p (u n) -> p u n", u=2))                        .then_inc(S["rdx_ready"], 1)
                    dve.wait_ge(S["rdx_ready"], 2 * b + hf + 1)
                    dve.tensor_tensor(on[:, b, 2 * hf:2 * hf + 2, QB0:2 * P], oraw[:, b, 2 * hf:2 * hf + 2, :],
                                      rdx[:, b, 2 * hf:2 * hf + 2, :], mul_).then_inc(S["on_ready"], 1)

            def attended(b):
                dve.wait_ge(S["wox_mm"], b + 1)
                dve.wait_ge(S["x1b_ready"], 2 * b + 2)
                t = b * TPB + 2
                dve.tensor_tensor(y2[:, t:t + 2, :], bank[b][:, 0:2 * P].rearrange("p (t d) -> p t d", t=2), x1b[:, t:t + 2, :], add_)                    .then_inc(S["y2_ready"], 1)
                dve.wait_ge(S["y2_ready"], b + 1)
                second_norm((t, t + 1), 4 + 2 * b)
                second_apply((t, t + 1), 2 + b)

            def x2_split(b):
                dve.wait_ge(S["x2hi_ready"], b + 1)
                dve.tensor_tensor(x2lo[:, b, :], bank[2 + b][:], x2hi[:, b, :].bitcast(F32), sub_).then_inc(S["x2lo_ready"], 1)

            def gates(b):
                T = slice(b * TPB, (b + 1) * TPB)
                dve.wait_ge(S["lg_mm"], b + 1)
                dve.wait_ge(S["c_lg0"], 2)
                dve.tensor_copy(lg[:, T, 0:E], bank[6 + b][:, 0:TPB * 16].rearrange("p (t e) -> p t e", e=16)[:, :, 0:E])                    .then_inc(S["lg_ready"], 1)
                dve.wait_ge(S["lg_ready"], b + 1)
                for t in range(b * TPB, (b + 1) * TPB):
                    dve.max(top[:, t, :], lg[:, t, 0:E]).then_inc(S["top_ready"], 1)
                dve.wait_ge(S["top_ready"], TPB * (b + 1))
                dve.tensor_copy(vals[:, T, 0:3], top[:, T, 0:3]).then_inc(S["vals_ready"], 1)
                dve.tensor_tensor(dl[:, T, :], lg[:, T, 0:E], top[:, T, 0:1].broadcast_to([P, TPB, E]), sub_).then_inc(S["dl_ready"], 1)
                dve.wait_ge(S["vals_ready"], b + 1)
                for t in range(b * TPB, (b + 1) * TPB):
                    dve.match_replace(rep[:, t, :], vals[:, t, :], lg[:, t, :], PAD).then_inc(S["rep_ready"], 1)
                dve.wait_ge(S["rep_ready"], TPB * (b + 1))
                dve.tensor_tensor(sel[:, T, :], rep[:, T, 0:E], lg[:, T, 0:E], ALU.not_equal).then_inc(S["sel_ready"], 1)
                dve.wait_ge(S["el_ready"], b + 1)
                dve.wait_ge(S["sel_ready"], b + 1)
                dve.tensor_tensor(em[:, T, :], el[:, T, :], sel[:, T, :], mul_).then_inc(S["em_ready"], 1)
                dve.tensor_reduce(zs[:, T], el[:, T, :], AX.X, add_).then_inc(S["zs_ready"], 1)
                dve.wait_ge(S["em_ready"], b + 1)
                dve.tensor_reduce(s3[:, T], em[:, T, :], AX.X, add_).then_inc(S["s3_ready"], 1)
                dve.wait_ge(S["s3_ready"], b + 1)
                dve.wait_ge(S["zs_ready"], b + 1)
                dve.scalar_tensor_tensor(out=dn[:, T], in0=zs[:, T], scalar=1e-20, in1=s3[:, T], op0=mul_, op1=add_)                    .then_inc(S["dn_ready"], 1)
                dve.wait_ge(S["dn_ready"], b + 1)
                dve.reciprocal(rd[:, T], dn[:, T]).then_inc(S["rd_ready"], 1)
                dve.wait_ge(S["rd_ready"], b + 1)
                dve.wait_ge(S["c_comb0"], 1)
                dve.tensor_tensor(comb[:, T, 0:E], em[:, T, :], rd[:, T].unsqueeze(2).broadcast_to([P, TPB, E]), mul_)                    .then_inc(S["comb_ready"], 1)

            o_normalise(0)
            attended(0)
            x2_split(0)
            o_normalise(1)
            gates(0)
            attended(1)
            x2_split(1)
            gates(1)

            def w2_stage(u, par):
                c = slice(par * D, (par + 1) * D)
                w = w2_sb[:, bass.ds(u, 1), :].rearrange("p a n -> p (a n)")
                m = mult_sb[:, bass.ds(u, 1)]
                dve.tensor_scalar(w2hi[:, c], w, m, None, mul_).then_inc(S["w2hi_ready"], 1)
                dve.wait_ge(S["w2hi_ready"], u + 1)
                dve.scalar_tensor_tensor(out=w2lo[:, c], in0=w, scalar=m, in1=w2hi[:, c].bitcast(F32), op0=mul_, op1=sub_)                    .then_inc(S["w2lo_ready"], 1)

            def act_product(n, s, u, first=False):
                dve.wait_ge(S["gc_ready"], n + 1)
                dve.wait_ge(S["h_mm"], n + 1)
                if not first:
                    dve.wait_ge(S["alo_ready"], n - 1)
                dve.scalar_tensor_tensor(out=a[:, s, :], in0=bank[2 + s][:], scalar=b1_sb[:, bass.ds(u, 1), 0:1].rearrange("p a b -> p (a b)"),
                                         in1=gl[:, s, :], op0=add_, op1=mul_).then_inc(S["a_ready"], 1)

            def act_lo(n, s):
                dve.wait_ge(S["ahi_ready"], n + 1)
                dve.tensor_tensor(alo[:, s * N:(s + 1) * N], a[:, s, :], ahi[:, s * N:(s + 1) * N].bitcast(F32), sub_)                    .then_inc(S["alo_ready"], 1)

            dve.wait_ge(S["ld_w2"], 16)
            dve.wait_ge(S["ld_small"], 48)
            w2_stage(0, 0)
            act_product(0, 0, 0, first=True)
            act_lo(0, 0)
            act_product(1, 1, 0, first=True)
            with dve.Fori(0, (U - 1) // UPL) as i:
                for j in range(UPL):
                    u = UPL * i + (1 + j)
                    par = (1 + j) % 2
                    dve.wait_ge(S["h_mm"], 2 * UPL * i + 2 * (1 + j))
                    w1hi_stage(UPL * i + (2 + j), 1 - par)
                    act_lo(2 * UPL * i + (2 * j + 1), 1)
                    b1g_stage(UPL * i + (2 + j), 1 - par)
                    act_product(2 * UPL * i + (2 * j + 2), 0, u)
                    dve.wait_ge(S["fc2_mm"], 2 * UPL * i + (2 * j + 2))
                    w2_stage(u, par)
                    act_lo(2 * UPL * i + (2 * j + 2), 0)
                    act_product(2 * UPL * i + (2 * j + 3), 1, u)
            act_lo(2 * U - 1, 1)

            dve.wait_ge(S["ybias_mm"], 2)
            dve.tensor_copy(yT[:, 1, :], bank[5][:]).then_inc(S["yT1_ready"], 1)
            for b in range(B):
                dve.wait_ge(S["yt_mm"], b + 1)
                T = range(b * TPB, (b + 1) * TPB)
                src = lambda t: bank[t // TPB][:, (t % TPB) * P:(t % TPB + 1) * P]
                stats(src, st3, mv3, T, 4 * b, "st3_done", "mv3_ready")
                dve.wait_ge(S["rstd3_ready"], b + 1)
                apply(res, src, mv3, rstd3, T, "res_ready")

        @block.scalar
        def _(act):
            def A(out, in_, f, **kw):
                return nc.scalar.activation(out, in_, f, **kw)

            for b in range(B):
                act.dma_start(xT_sb[:, b * N:(b + 1) * N], xT[:, b * N:(b + 1) * N]).then_inc(S[f"ld_xT{b}"], 16)
            for i in range(4):
                o = bank[i][:].rearrange("p (t n) -> p t n", t=2)
                act.wait_ge(S["kv_mm"], i + 1)
                A(ek[:, i, :, :], o[:, :, 0:P], ACT.Exp).then_inc(S["ek_done"], 1)
                A(vsb[:, 2 * i:2 * i + 2, 0:P], o[:, :, P:2 * P], ACT.Copy).then_inc(S["v_ready"], 1)
            for b in range(B):
                act.wait_ge(S["q_mm"], b + 1)
                A(eq[:, b, :], bank[4 + b][:], ACT.Exp).then_inc(S["eq_done"], 1)

            def rsqrt(mv_view, ln_view, rs_view, n, names):
                act.wait_ge(S["c_misc"], 3)
                A(ln_view, mv_view, ACT.Ln, bias=epsc[:, 0:1]).then_inc(S[names[0]], 1)
                act.wait_ge(S[names[0]], n)
                A(rs_view, ln_view, ACT.Exp, scale=-0.5).then_inc(S[names[1]], 1)

            def tiles_of(tensor, k0):
                return tensor[:].rearrange("p (b k) -> p b k", b=B)[:, :, k0:k0 + 2]

            def var_of(tensor, k0):
                return tensor[:].rearrange("p (b k) s -> p b k s", b=B)[:, :, k0:k0 + 2, 1]

            for h in range(2):
                act.wait_ge(S["oT_mm"], h + 1)
                A(oT[:, h, :, :].rearrange("p c n -> p (c n)"), bank[2 + h][:], ACT.Copy).then_inc(S["oT_ready"], 1)
            act.wait_ge(S["mv_ready"], 4)
            rsqrt(var_of(mv, 2), tiles_of(lnv, 2), tiles_of(rstd, 2), 1, ("lnv_done", "rstd_ready"))
            for b in range(B):
                act.wait_ge(S["x1T_mm"], b + 1)
                A(x1T[:, b, :], bank[4 + b][:, QB0:2 * P], ACT.Copy).then_inc(S["x1T_ready"], 1)
            act.wait_ge(S["mv_ready"], 8)
            rsqrt(var_of(mv, 0), tiles_of(lnv, 0), tiles_of(rstd, 0), 2, ("lnv_done", "rstd_ready"))
            act.wait_ge(S["lomask_ready"], 2)
            for g in range(G):
                act.wait_ge(S["qst_full"], g + 1)
                A(hisq[:, g, :], fullq[:, g, :], ACT.Copy, scale=lomask[:, 0:1]).then_inc(S["qst_his"], 1)

            def probabilities(n):
                b, c = divmod(n, 8)
                bk = bank[2 + n % 2]
                act.wait_ge(S["sT_mm"], n + 1)
                A(pT1[:, b, 2 * c:2 * c + 2, :], bk[:, 0:2 * NS].rearrange("p (h n) -> p h n", h=2), ACT.Exp).then_inc(S["p_ready"], 1)
                A(pT2[0:C2, b, 2 * c:2 * c + 2, :], bk[0:C2, 2 * NS:2 * NS + 2 * C2].rearrange("p (h n) -> p h n", h=2), ACT.Exp)                    .then_inc(S["p_ready"], 1)

            def o_copy(b, hf):
                act.wait_ge(S["pv_mm"], 4 * b + 2 * hf + 2)
                A(oraw[:, b, 2 * hf:2 * hf + 2, :], bank[4 + hf][:, 0:2 * NS].rearrange("p (u n) -> p u n", u=2), ACT.Copy)                    .then_inc(S["oraw_ready"], 1)

            for n in range(16):
                probabilities(n)
                if n == 7:
                    o_copy(0, 0)
                if n == 9:
                    o_copy(0, 1)
                if n == 11:
                    act.wait_ge(S["mv2_ready"], 4)
                    rsqrt(var_of(mv2, 0), tiles_of(lnv2, 0), tiles_of(rstd2, 0), 1, ("lnv2_done", "rstd2_ready"))
            o_copy(1, 0)
            o_copy(1, 1)

            def attended_rsqrt(b):
                t = slice(b * TPB + 2, b * TPB + 4)
                act.wait_ge(S["mv2_ready"], 6 + 2 * b)
                rsqrt(mv2[:, t, 1], lnv2[:, t], rstd2[:, t], 2 + b, ("lnv2_done", "rstd2_ready"))

            def x2_hi(b):
                act.wait_ge(S["x2T_mm"], b + 1)
                A(x2hi[:, b, :], bank[2 + b][:], ACT.Copy).then_inc(S["x2hi_ready"], 1)

            def gate_exp(b):
                T = slice(b * TPB, (b + 1) * TPB)
                act.wait_ge(S["dl_ready"], b + 1)
                A(el[:, T, :], dl[:, T, :], ACT.Exp).then_inc(S["el_ready"], 1)

            attended_rsqrt(0)
            x2_hi(0)
            gate_exp(0)
            attended_rsqrt(1)
            x2_hi(1)
            gate_exp(1)

            def gelu(n, s, u, par, first=False):
                act.wait_ge(S["g_mm"], n + 1)
                if not first:
                    act.wait_ge(S["a_ready"], n - 1)
                act.wait_ge(S["b1g_ready"], u + 1)
                A(gl[:, s, :], bank[s][:], ACT.Gelu, bias=b1g[:, par:par + 1])                    .then_inc(S["gelu_done"], 1)

            def act_hi(n, s, first=False):
                act.wait_ge(S["a_ready"], n + 1)
                if not first:
                    act.wait_ge(S["fc2_mm"], n + 1)
                A(ahi[:, s * N:(s + 1) * N], a[:, s, :], ACT.Copy).then_inc(S["ahi_ready"], 1)

            gelu(0, 0, 0, 0, first=True)
            for b in range(B):
                act.wait_ge(S["cT_mm"], b + 1)
                A(combT[:, b, :], bank[6 + b][0:16, :], ACT.Copy).then_inc(S["cT_ready"], 1)
            gelu(1, 1, 0, 0, first=True)
            act_hi(0, 0, first=True)
            with act.Fori(0, (U - 1) // UPL) as i:
                for j in range(UPL):
                    u = UPL * i + (1 + j)
                    gelu(2 * UPL * i + (2 * j + 2), 0, u, (1 + j) % 2)
                    act_hi(2 * UPL * i + (2 * j + 1), 1)
                    gelu(2 * UPL * i + (2 * j + 3), 1, u, (1 + j) % 2)
                    act_hi(2 * UPL * i + (2 * j + 2), 0)
            act_hi(2 * U - 1, 1)

            act.wait_ge(S["ybias_mm"], 1)
            A(yT[:, 0, :], bank[4][:], ACT.Copy).then_inc(S["yT0_ready"], 1)
            for b in range(B):
                t = slice(b * TPB, (b + 1) * TPB)
                act.wait_ge(S["mv3_ready"], 4 * b + 4)
                rsqrt(mv3[:, t, 1], lnv3[:, t], rstd3[:, t], b + 1, ("lnv3_done", "rstd3_ready"))


def kernel(**inputs):
    import numpy as np
    import concourse.bacc as bacc
    from concourse.bass_utils import run_bass_kernel_spmd as run

    I = {k: np.asarray(v) for k, v in inputs.items()}
    c = np.ascontiguousarray

    def stacked(w):
        w = w.reshape(w.shape[:-1] + (G, G, 1, DH))
        w = np.broadcast_to(w, w.shape[:-2] + (4, DH))
        return w.reshape(w.shape[:-4] + (G, P))

    wq, wk = I["L0_xattn_Wq"], I["L0_xattn_Wk"]
    wo = I["L0_xattn_Wo"]
    wop = np.zeros((G, 32, G, D), wo.dtype)
    wop[:, 0:DH, :, :] = wo.reshape(G, G, DH, D).transpose(0, 2, 1, 3)
    f1, s1 = I["L0_ffn_fc1_w"], I["L0_ffn_s_fc1_w"]
    s1 = s1.reshape(2, 2, P, D).transpose(1, 0, 2, 3).reshape(2, 2 * P, D)
    sb1 = I["L0_ffn_s_fc1_b"].reshape(2, 2, P).transpose(1, 0, 2)
    f2, s2 = I["L0_ffn_fc2_w"], I["L0_ffn_s_fc2_w"]
    s2 = s2.reshape(D, 2, P).transpose(1, 0, 2)
    arrays = {
        "x": c(I["x"]),
        "xT": c(I["x"].transpose(2, 0, 1).reshape(D, B * N)),
        "ctxT": c(I["ctx_1024"].transpose(2, 0, 1).reshape(D, B * NS)),
        "wA": c(np.concatenate([I["L0_attn_W" + n].T for n in "qkvo"], axis=1)),
        "boA": c(I["L0_attn_bo"]),
        "wqs": c(stacked(wq)),
        "wks": c(stacked(wk)),
        "bqs": c(stacked(I["L0_xattn_bq"]).T),
        "bks": c(stacked(I["L0_xattn_bk"]).T),
        "wv": c(I["L0_xattn_Wv"]),
        "bv": c(I["L0_xattn_bv"]),
        "wo": c(wo),
        "wop": c(wop.reshape(P, G, D)),
        "boX": c(I["L0_xattn_bo"]),
        "gateT": c(I["L0_ffn_gate_w"].T),
        "w1T": c(np.concatenate([s1, f1]).transpose(2, 0, 1)),
        "b1": c(np.concatenate([sb1, I["L0_ffn_fc1_b"].reshape(E, 2, P)]).transpose(2, 0, 1)),
        "mult": c(np.concatenate([I["L0_ffn_s_geglu_mult"].reshape(2, P), I["L0_ffn_geglu_mult"]]).T),
        "w2T": c(np.concatenate([s2, f2]).transpose(2, 0, 1)),
        "b2": c(np.concatenate([I["L0_ffn_fc2_b"], I["L0_ffn_s_fc2_b"][None]])),
    }
    nc = bacc.Bacc("TRN2", target_bir_lowering=False, num_devices=1)
    args = {n: nc.dram_tensor(n + "_d", v.shape, mybir.dt.from_np(v.dtype), kind="ExternalInput").ap() for n, v in arrays.items()}
    comb_dram = nc.dram_tensor("comb_d", (E, B, N), F32, kind="Internal").ap()
    out = nc.dram_tensor("out_d", (B, N, D), F32, kind="ExternalOutput").ap()
    build(nc, comb_dram=comb_dram, out=out, **args)
    r = run(nc, [{n + "_d": v for n, v in arrays.items()}], core_ids=[0])
    return r.results[0]["out_d"]
```

```python
from contextlib import ExitStack

import concourse.bass as bass
from concourse import mybir

F32 = mybir.dt.float32
F32R = mybir.dt.float32r
BF16 = mybir.dt.bfloat16
ALU = mybir.AluOpType
ACT = mybir.ActivationFunctionType
AX = mybir.AxisListType

P = 128
D = 128
B, N = 2, 512
NT = B * N // P
TPB = N // P
H, DH = 16, 8
NS = 154
C2 = NS - P
QA = N - NS
QB0 = QA - 2 * P
QB = P - QB0
G = 4
E = 15
U = 17
LNEPS = 1e-5
EPS = 1e-6
NEG = -1e10
PAD = -3e38
SCALE = DH ** -0.5
UPL = 4
assert QB == C2 and QB0 + QB == P and U == 1 + UPL * 4


def build(nc, x, xT, ctxT, wA, boA, wqs, wks, bqs, bks, wv, bv, wo, wop, boX, gateT, w1T, b1, mult,
          w2T, b2, comb_dram, out):
    with ExitStack() as ctx:
        def sb(name, shape, dt=F32):
            return ctx.enter_context(nc.sbuf_tensor(name, shape, dt))

        def sem(name):
            return ctx.enter_context(nc.semaphore(name))

        bank = [ctx.enter_context(nc.psum_tensor(f"bank{i}", [P, 512], F32)) for i in range(8)]

        ident = sb("ident", [P, P])
        ident16 = sb("ident16", [P, P], BF16)
        identr = sb("identr", [P, P], F32R)
        headmask = sb("headmask", [P, P])
        selD = sb("selD", [P, P])
        maskf = sb("maskf", [P, 2, P])
        maskS = sb("maskS", [P, P], BF16)
        maskT = sb("maskT", [P, P], BF16)
        lomask = sb("lomask", [P, 2])
        mcol = sb("mcol", [P, 1])

        x_sb = sb("x_sb", [P, NT, D])
        xT_sb = sb("xT_sb", [P, NT * P])
        wA_sb = sb("wA_sb", [P, 4 * D])
        ctx_sb = sb("ctx_sb", [P, B * NS])
        bo_bc = sb("bo_bc", [P, 3, D])
        wqs_sb = sb("wqs_sb", [P, G, P])
        wks_sb = sb("wks_sb", [P, G, P])
        bqk_sb = sb("bqk_sb", [P, 2, G])
        wv_sb = sb("wv_sb", [P, D])
        wo_sb = sb("wo_sb", [P, D])
        wop_sb = sb("wop_sb", [P, G, D])
        gate_sb = sb("gate_sb", [P, 16])
        w1_sb = sb("w1_sb", [P, U + 1, 2 * P])
        b1_sb = sb("b1_sb", [P, U + 1, 2])
        b1g = sb("b1g", [P, 2])
        mult_sb = sb("mult_sb", [P, U])
        w2_sb = sb("w2_sb", [P, U, D])
        b2_sb = sb("b2_sb", [16, D])

        ek = sb("ek", [P, 4, 2, P])
        ksb = sb("ksb", [P, NT, P])
        vsb = sb("vsb", [P, NT, P + 1])
        eq = sb("eq", [P, B, N])
        qT = sb("qT", [P, B, N])
        bd = sb("bd", [P, B, P + H])
        rden = sb("rden", [P, 4, 2, H])
        osb = sb("osb", [P, 4, 2, P])
        oT = sb("oT", [P, 2, 4, P])
        xb = sb("xb", [P, NT, D])
        y = sb("y", [P, NT, D])
        st = sb("st", [P, NT, 6])
        mv = sb("mv", [P, NT, 2])
        lnv = sb("lnv", [P, NT])
        rstd = sb("rstd", [P, NT])
        x1 = sb("x1", [P, NT, D])
        x1b = osb[:].rearrange("p i t d -> p (i t) d")
        epsc = sb("epsc", [P, 1])

        vx = sb("vx", [P, B, 2, D])
        va = sb("va", [P, B, 2, H, 32])
        mvT = sb("mvT", [P, B])
        mv_bc = sb("mv_bc", [P, B, P])
        mv_t2 = sb("mv_t2", [P, B, P])
        cb = sb("cb", [P, B, D])
        fullk = sb("fullk", [P, G, B * NS])
        fullq = fullk
        hisk = sb("hisk", [P, G, B * NS], F32R)
        hisq = hisk
        ks = sb("ks", [P, G, B * NS], F32R)
        qs = sb("qs", [P, G, B * NS], F32R)
        x1T = sb("x1T", [P, B, NS])
        mA = sb("mA", [P, B, H])
        mB = sb("mB", [P, B, H])
        mmA = sb("mmA", [P, G, P])
        mmB = sb("mmB", [P, G, P])
        pT1 = sb("pT1", [P, B, H, NS])
        pT2 = sb("pT2", [P, B, H, C2])
        oraw = sb("oraw", [P, B, G, NS])
        rdx = fullk[:].rearrange("p g (b n) -> p (g b n)", b=B).rearrange("p (b g n) -> p b g n", b=B, g=G)
        on = sb("on", [P, B, G, 2 * P])
        st2 = sb("st2", [P, NT, 6])
        mv2 = sb("mv2", [P, NT, 2])
        lnv2 = sb("lnv2", [P, NT])
        rstd2 = sb("rstd2", [P, NT])
        y2 = x_sb
        x2 = xb

        x2hi = sb("x2hi", [P, B, N], F32R)
        x2lo = sb("x2lo", [P, B, N], F32R)
        ghi = sb("ghi", [P, 16], F32R)
        glo = sb("glo", [P, 16], F32R)
        LG = E + 5
        lg = sb("lg", [P, NT, LG])
        top = sb("top", [P, NT, 8])
        vals = sb("vals", [P, NT, 8])
        rep = sb("rep", [P, NT, LG])
        sel = sb("sel", [P, NT, E])
        dl = sb("dl", [P, NT, E])
        el = sb("el", [P, NT, E])
        em = sb("em", [P, NT, E])
        zs = sb("zs", [P, NT])
        s3 = sb("s3", [P, NT])
        dn = sb("dn", [P, NT])
        rd = sb("rd", [P, NT])
        comb = sb("comb", [P, NT, 16])
        combT = sb("combT", [16, B, N])
        comb_bc = pT1[:].rearrange("p b h n -> p (b h n)")[:, 0:UPL * B * N].rearrange("p (j b n) -> p j b n", j=UPL, b=B)
        w1hi = sb("w1hi", [P, 2 * 2 * P], F32R)
        w1lo = sb("w1lo", [P, 2 * 2 * P], F32R)
        w2hi = sb("w2hi", [P, 2 * D], F32R)
        w2lo = sb("w2lo", [P, 2 * D], F32R)
        gl = ek[:].rearrange("p i t n -> p (i t n)").rearrange("p (s n) -> p s n", s=2)
        a = eq
        ahi = sb("ahi", [P, 2 * N], F32R)
        alo = sb("alo", [P, 2 * N], F32R)
        start = sb("start", [P, 2], F32)
        yT = qT
        st3 = sb("st3", [P, NT, 6])
        mv3 = sb("mv3", [P, NT, 2])
        lnv3 = sb("lnv3", [P, NT])
        rstd3 = sb("rstd3", [P, NT])
        res = ksb

        names = ("ld_xT0 ld_xT1 ld_wA ld_x ld_ctx ld_wks ld_wqs ld_bias ld_wv ld_wo ld_wop ld_gate ld_w1 ld_w2 ld_small "
                 "b1g_ready c_mm0 c_mvt0 c_on0 c_gate0 c_lg0 c_comb0 c_w1pad c_selD0 lomask_ready y2a_ready yT0_ready yT1_ready c_ident c_ident16 c_headmask qm_ready rln_ready c_selD c_maskf c_mask16 c_misc c_va0 c_zero "
                 "kv_mm q_mm ek_done ekmin_done k_ready v_ready eq_done eqmin_done q_ready kvs_mm bd_ready bdk_ready "
                 "num_mm den_ready rden_ready o_ready oT_mm oT_ready wo_mm xb_ready y_ready st_done mv_ready lnv_done "
                 "rstd_ready x1_ready x1b_ready vx_mm vx_ready va_ready mean_mm mean_ready mvbc_ready cb_mm cb_ready "
                 "kst_mm kst_full kst_his ks_ready qst_mm qst_full qst_his qs_ready x1T_mm x1T_ready "
                 "s_mm m_ready mhi_ready mlo_ready mt_mm sT_mm p_ready pv_mm oraw_ready db_mm rdx_ready "
                 "on_ready wox_mm y2_ready st2_done mv2_ready lnv2_done rstd2_ready x2_ready x2T_mm x2hi_ready x2lo_ready "
                 "g_hi g_lo lg_mm lg_ready top_ready vals_ready rep_ready sel_ready dl_ready el_ready em_ready zs_ready s3_ready dn_ready "
                 "rd_ready comb_ready cT_mm cT_ready comb_stored "
                 "w1hi_ready w1lo_ready w2hi_ready w2lo_ready g_mm h_mm gelu_done gc_ready a_ready ahi_ready alo_ready fc2_mm "
                 "ybias_mm yT_ready yt_mm y3_ready st3_done mv3_ready lnv3_done rstd3_ready res_ready stored").split()
        S = {n: sem(n) for n in names}
        slot_filled = [sem(f"slot_filled{j}") for j in range(UPL)]

        block = ctx.enter_context(nc.Block())

        PAIRS = [(2, 3), (6, 7), (0, 1), (4, 5)]
        POS = {t: 2 * i + j for i, pr in enumerate(PAIRS) for j, t in enumerate(pr)}
        NUMBANK = [4, 5, 0, 1]
        KSTBANK = [7, 2, 3, 6]
        WOBANK = [6, 7]

        ORDER2 = [0, 1, 4, 5, 2, 3, 6, 7]
        HALF = [ORDER2[0:4], ORDER2[4:8]]
        X2BANK = [7, 1]
        HB = [[2, 3], [6, 7]]

        def slot(k):
            return k // G, k % G

        @block.sync
        def _(sp):
            sp.dma_start(wA_sb[:], wA).then_inc(S["ld_wA"], 16)
            sp.dma_start(ctx_sb[:], ctxT).then_inc(S["ld_ctx"], 16)
            sp.dma_start(wv_sb[:], wv).then_inc(S["ld_wv"], 16)
            sp.dma_start(wks_sb[:], wks).then_inc(S["ld_wks"], 16)
            sp.dma_start(bqk_sb[:, 0, :], bqs).then_inc(S["ld_bias"], 16)
            sp.dma_start(bqk_sb[:, 1, :], bks).then_inc(S["ld_bias"], 16)
            for i, v in enumerate((boA, bv, boX)):
                sp.dma_start(bo_bc[:, i, :], v.partition_broadcast(P)).then_inc(S["ld_bias"], 16)
            sp.dma_start(x_sb[:], x.rearrange("b (k p) d -> p (b k) d", p=P)).then_inc(S["ld_x"], 16)
            sp.dma_start(wqs_sb[:], wqs).then_inc(S["ld_wqs"], 16)
            sp.dma_start(wo_sb[:], wo).then_inc(S["ld_wo"], 16)
            sp.dma_start(wop_sb[:], wop).then_inc(S["ld_wop"], 16)
            sp.dma_start(gate_sb[:, 0:E], gateT).then_inc(S["ld_gate"], 16)
            sp.dma_start(b1_sb[:, 0:U, :], b1).then_inc(S["ld_small"], 16)
            sp.dma_start(mult_sb[:], mult).then_inc(S["ld_small"], 16)
            sp.dma_start(b2_sb[:], b2).then_inc(S["ld_small"], 16)
            sp.dma_start(w1_sb[:, 0:U, :], w1T).then_inc(S["ld_w1"], 16)
            sp.dma_start(w2_sb[:], w2T).then_inc(S["ld_w2"], 16)

            for s in range(B):
                sp.wait_ge(S["cT_ready"], s + 1)
                sp.dma_start(comb_dram[:, s, :], combT[0:E, s, :]).then_inc(S["comb_stored"], 16)
            sp.wait_ge(S["comb_stored"], 16 * B)
            sp.wait_ge(S["pv_mm"], 8)
            for j in range(1, UPL):
                sp.dma_start(comb_bc[:, j, :, :], comb_dram[j - 1, :, :].partition_broadcast(P)).then_inc(slot_filled[j], 16)
            with sp.Fori(0, (U - 1) // UPL - 1) as i:
                for j in range(UPL):
                    sp.wait_ge(S["gc_ready"], 8 * i + 2 * (j + 2))
                    sp.dma_start(comb_bc[:, j, :, :], comb_dram[bass.ds(4 * i + (UPL + j - 1), 1), :, :].rearrange("a b n -> (a b) n").partition_broadcast(P)).then_inc(slot_filled[j], 16)

            for i in range(4):
                sp.wait_ge(S["res_ready"], 2 * (i + 1))
                t = ORDER2[2 * i]
                sp.dma_start(out.rearrange("b (k p) d -> p (b k) d", p=P)[:, t:t + 2, :],
                             res[:, 2 * i:2 * i + 2, :]).then_inc(S["stored"], 16)
            sp.wait_ge(S["stored"], 64)

        @block.tensor
        def _(pe):
            mm = nc.tensor.matmul

            pe.wait_ge(S["ld_wA"], 16)
            pe.wait_ge(S["ld_xT0"], 16)
            for t in range(NT):
                if t == TPB:
                    pe.wait_ge(S["ld_xT1"], 16)
                i = mm(bank[t // 2][:, (t % 2) * 256:(t % 2) * 256 + 256], xT_sb[:, t * P:(t + 1) * P],
                       wA_sb[:, D:3 * D], start=True, stop=True)
                if t % 2:
                    i.then_inc(S["kv_mm"], 1)
            for b in range(B):
                mm(bank[4 + b][:], wA_sb[:, 0:D], xT_sb[:, b * N:(b + 1) * N], start=True, stop=True).then_inc(S["q_mm"], 1)
            pe.wait_ge(S["ld_ctx"], 16)
            pe.wait_ge(S["ld_wv"], 16)
            for b in range(B):
                for c, (k0, n) in enumerate(((0, P), (P, C2))):
                    i = mm(bank[6][0:n, (2 * b + c) * D:(2 * b + c + 1) * D], ctx_sb[:, b * NS + k0:b * NS + k0 + n],
                           wv_sb[:], start=True, stop=True)
            i.then_inc(S["vx_mm"], 1)

            def kstack(g):
                mm(bank[KSTBANK[g]][:, 0:B * NS], wks_sb[:, g, :], ctx_sb[:], start=True, stop=True).then_inc(S["kst_mm"], 1)

            pe.wait_ge(S["ld_wks"], 16)
            kstack(0)
            for b in range(B):
                pe.wait_ge(S["k_ready"], 2 * b + 2)
                pe.wait_ge(S["v_ready"], 2 * b + 2)
                pe.wait_ge(S["c_misc"], 1)
                for k in range(TPB):
                    i = mm(bank[b][:, 0:P + 1], ksb[:, b * TPB + k, :], vsb[:, b * TPB + k, :],
                           start=(k == 0), stop=(k == TPB - 1))
                i.then_inc(S["kvs_mm"], 1)
            kstack(1)
            kstack(2)
            def num(i):
                b = PAIRS[i][0] // TPB
                pe.wait_ge(S["q_ready"], b + 1)
                pe.wait_ge(S["bdk_ready"], b + 1)
                if i == 2:
                    pe.wait_ge(S["bdk_ready"], B)
                if i < 2:
                    pe.wait_ge(S["q_ready"], i + 1)
                for j, t in enumerate(PAIRS[i]):
                    r = mm(bank[NUMBANK[i]][:, j * 256:j * 256 + P + H], qT[:, b, (t % TPB) * P:(t % TPB + 1) * P],
                           bd[:, b, :], start=True, stop=True)
                r.then_inc(S["num_mm"], 1)

            def o_transposes(i):
                pe.wait_ge(S["o_ready"], i + 1)
                if i == 0:
                    pe.wait_ge(S["c_ident"], 1)
                    pe.wait_ge(S["kst_full"], 2)
                if i == 2:
                    pe.wait_ge(S["kst_full"], 3)
                for j in range(2):
                    c = (i % 2) * 2 + j
                    r = nc.tensor.transpose(bank[2 + i // 2][:, c * P:(c + 1) * P], osb[:, i, j, :], ident[:])
                if i % 2:
                    r.then_inc(S["oT_mm"], 1)

            def wo_a(h):
                pe.wait_ge(S["oT_ready"], h + 1)
                if h == 0:
                    pe.wait_ge(S["kst_full"], 4)
                else:
                    pe.wait_ge(S["cb_ready"], 1)
                for c in range(4):
                    r = mm(bank[WOBANK[h]][:, c * P:(c + 1) * P], oT[:, h, c, :], wA_sb[:, 3 * D:4 * D], start=True, stop=True)
                r.then_inc(S["wo_mm"], 1)

            num(0)
            num(1)
            o_transposes(0)
            pe.wait_ge(S["vx_ready"], 2)
            kstack(3)
            pe.wait_ge(S["kst_full"], 1)
            for b in range(B):
                mm(bank[7][:, b:b + 1], vx[:, b, 0, :], mcol[:], start=True, stop=False)
                i = mm(bank[7][:, b:b + 1], vx[0:C2, b, 1, :], mcol[0:C2, :], start=False, stop=True)
            i.then_inc(S["mean_mm"], 1)
            o_transposes(1)
            num(2)
            num(3)
            wo_a(0)
            o_transposes(2)
            pe.wait_ge(S["mvbc_ready"], 2 * B)
            pe.wait_ge(S["ld_wo"], 16)
            for b in range(B):
                i = mm(bank[7][:, 128 + b * P:128 + (b + 1) * P], mv_bc[:, b, :], wo_sb[:], start=True, stop=True)
            i.then_inc(S["cb_mm"], 1)
            o_transposes(3)
            wo_a(1)
            for b in range(B):
                pe.wait_ge(S["x1_ready"], 2 * b + 2)
                for j in range(2):
                    r = nc.tensor.transpose(bank[4 + b][:, j * P:(j + 1) * P], x1[:, b * TPB + 2 + j, :], ident[:])
                r.then_inc(S["x1T_mm"], 1)
            pe.wait_ge(S["x1T_ready"], B)
            pe.wait_ge(S["ld_wqs"], 16)
            pe.wait_ge(S["o_ready"], 4)
            pe.wait_ge(S["oT_ready"], 2)
            for g in range(G):
                mm(bank[g][:, 0:B * NS], wqs_sb[:, g, :], x1T[:].rearrange("p b n -> p (b n)"), start=True, stop=True)\
                    .then_inc(S["qst_mm"], 1)

            pe.wait_ge(S["qs_ready"], G)
            pe.wait_ge(S["ks_ready"], G)
            pe.wait_ge(S["c_mask16"], 2)
            pe.wait_ge(S["c_ident16"], 1)

            def scores(n):
                b, c = divmod(n, 8)
                bk = bank[n % 2]
                if n >= 2:
                    pe.wait_ge(S["m_ready"], 2 * (n - 1))
                q0 = b * NS
                for j in range(2):
                    v, g = slot(2 * c + j)
                    rows = slice(32 * v, 32 * v + 32)
                    mm(bk[:, j * NS:(j + 1) * NS], qs[rows, g, q0 + QB:q0 + NS], ks[rows, g, q0:q0 + NS],
                       start=(j == 0), stop=False, skip_group_check=True, tile_position=(32 * v, 0))
                for j in range(2):
                    v, g = slot(2 * c + j)
                    rows = slice(32 * v, 32 * v + 32)
                    b0 = 2 * NS + j * C2
                    mm(bk[0:QB, b0:b0 + C2], qs[rows, g, q0:q0 + QB], ks[rows, g, q0:q0 + C2],
                       start=False, stop=False, skip_group_check=True, tile_position=(32 * v, 0))
                mm(bk[0:QB, 2 * NS:2 * NS + 2 * C2].rearrange("p (h n) -> p h n", h=2), ident16[0:QB, 0:QB],
                   maskS[0:QB, 0:C2].unsqueeze(1).broadcast_to([QB, 2, C2]), start=False, stop=False, skip_group_check=True)
                mm(bk[:, 0:2 * NS].rearrange("p (h n) -> p h n", h=2)[:, :, C2:NS], ident16[:],
                   maskS[:].unsqueeze(1).broadcast_to([P, 2, P]), start=False, stop=True, skip_group_check=True)\
                    .then_inc(S["s_mm"], 1)

            def max_transposes(b):
                pe.wait_ge(S["mlo_ready"], 2 * (b + 1))
                if b:
                    pe.wait_ge(S["cT_ready"], 1)
                for g in range(G):
                    o = bank[6 + g // 2][:, (g % 2) * NS:(g % 2 + 1) * NS]
                    nc.tensor.transpose(o[:, 0:QB], mmB[0:QB, g, :], ident[0:QB, 0:QB])
                    r = nc.tensor.transpose(o[:, QB:NS], mmA[:, g, :], ident[:])
                r.then_inc(S["mt_mm"], 1)

            def scores_T(n):
                b, c = divmod(n, 8)
                bk = bank[2 + n % 2]
                pe.wait_ge(S["qm_ready"], 2 * (b + 1))
                if n >= 2:
                    pe.wait_ge(S["p_ready"], 2 * (n - 1))
                q0 = b * NS
                for j in range(2):
                    v, g = slot(2 * c + j)
                    rows = slice(32 * v, 32 * v + 32)
                    mm(bk[:, j * NS:(j + 1) * NS], ks[rows, g, q0:q0 + P], qs[rows, g, q0:q0 + NS],
                       start=(j == 0), stop=False, skip_group_check=True, tile_position=(32 * v, 0))
                for j in range(2):
                    v, g = slot(2 * c + j)
                    rows = slice(32 * v, 32 * v + 32)
                    b0 = 2 * NS + j * C2
                    mm(bk[0:C2, b0:b0 + C2], ks[rows, g, q0 + P:q0 + NS], qs[rows, g, q0 + P:q0 + NS],
                       start=False, stop=False, skip_group_check=True, tile_position=(32 * v, 0))
                mm(bk[0:C2, 2 * NS:2 * NS + 2 * C2].rearrange("p (h n) -> p h n", h=2), ident16[0:C2, 0:C2],
                   maskT[0:C2, 0:C2].unsqueeze(1).broadcast_to([C2, 2, C2]), start=False, stop=False, skip_group_check=True)
                mm(bk[:, 0:2 * NS].rearrange("p (h n) -> p h n", h=2)[:, :, 0:P], ident16[:],
                   maskT[:].unsqueeze(1).broadcast_to([P, 2, P]), start=False, stop=True, skip_group_check=True)\
                    .then_inc(S["sT_mm"], 1)

            def pv(b, u):
                pe.wait_ge(S["p_ready"], 2 * (8 * b + 2 * u + 2))
                pe.wait_ge(S["va_ready"], 1 + 2 * B)
                if b == 1 and u == 0:
                    pe.wait_ge(S["oraw_ready"], 2)
                o = bank[4 + u // 2][:, (u % 2) * NS:(u % 2 + 1) * NS]
                for w in range(G):
                    k = G * u + w
                    mm(o[32 * w:32 * w + 32, :], va[:, b, 0, k, :], pT1[:, b, k, :], start=(u % 2 == 0), stop=False,
                       skip_group_check=True, tile_position=(0, 32 * w))
                for w in range(G):
                    k = G * u + w
                    r = mm(o[32 * w:32 * w + 32, P:NS], va[0:C2, b, 1, k, :], pT2[0:C2, b, k, :], start=False, stop=True,
                           skip_group_check=True, tile_position=(0, 32 * w))
                r.then_inc(S["pv_mm"], 1)

            def den_bc(b):
                pe.wait_ge(S["c_selD"], 1)
                for hf in range(2):
                    pe.wait_ge(S["oraw_ready"], 2 * b + hf + 1)
                    if b:
                        pe.wait_ge(S["rln_ready"], 2)
                    mm(bank[6 + hf][:, 0:2 * NS], selD[:], oraw[:, b, 2 * hf:2 * hf + 2, :].rearrange("p u n -> p (u n)"),
                       start=True, stop=True).then_inc(S["db_mm"], 1)

            def wo_x(b):
                pe.wait_ge(S["on_ready"], 2 * (b + 1))
                pe.wait_ge(S["ld_wop"], 16)
                pe.wait_ge(S["m_ready"], 32)
                if b:
                    pe.wait_ge(S["p_ready"], 32)
                for j in range(2):
                    o = bank[1 + 2 * b][:, j * P:(j + 1) * P]
                    if j == 0:
                        mm(o, mv_t2[:, b, :], wo_sb[:], start=True, stop=False)
                    for u in range(G):
                        r = mm(o, on[:, b, u, j * P:(j + 1) * P], wop_sb[:, u, :], start=(u == 0 and j == 1),
                               stop=(u == G - 1))
                r.then_inc(S["wox_mm"], 1)

            def x2_transposes(s, part):
                for c in (2 * part, 2 * part + 1):
                    pe.wait_ge(S["x2_ready"], 4 * s + c + 1)
                    r = nc.tensor.transpose(bank[X2BANK[s]][:, c * P:(c + 1) * P], x2[:, HALF[s][c], :], ident[:])
                if part:
                    r.then_inc(S["x2T_mm"], 1)

            def router(s):
                pe.wait_ge(S["x2hi_ready"], s + 1)
                pe.wait_ge(S["x2lo_ready"], s + 1)
                pe.wait_ge(S["g_lo"], 1)
                if s:
                    pe.wait_ge(S["rln_ready"], 4)
                for c in range(TPB):
                    o = bank[6][:, c * 16:(c + 1) * 16]
                    q = slice(c * P, (c + 1) * P)
                    mm(o, x2hi[:, s, q], ghi[:], start=True, stop=False)
                    mm(o, x2hi[:, s, q], glo[:], start=False, stop=False)
                    r = mm(o, x2lo[:, s, q], ghi[:], start=False, stop=True)
                r.then_inc(S["lg_mm"], 1)

            def comb_transposes(s):
                pe.wait_ge(S["comb_ready"], s + 1)
                for c in range(TPB):
                    r = nc.tensor.transpose(bank[7][0:16, c * P:(c + 1) * P], comb[:, s * TPB + c, :], ident[:])
                r.then_inc(S["cT_mm"], 1)

            for n in range(8):
                scores(n)
            max_transposes(0)
            for c in range(8):
                scores_T(c)
                scores(8 + c)
                if c >= 3 and c % 2:
                    pv(0, (c - 3) // 2)
                if c == 2:
                    pe.wait_ge(S["qm_ready"], 2)
                    x2_transposes(0, 0)
                    x2_transposes(0, 1)
                if c == 4:
                    router(0)
                if c == 6:
                    comb_transposes(0)
            max_transposes(1)
            for c in range(8):
                scores_T(8 + c)
                if c == 1:
                    pv(0, 3)
                if c == 3:
                    den_bc(0)
                if c == 6:
                    wo_x(0)
                if c >= 3 and c % 2:
                    pv(1, (c - 3) // 2)
            pv(1, 3)
            den_bc(1)
            def fc1(u, s, i=None):
                w = slice(u * 256 + P, u * 256 + 256), slice(u * 256, u * 256 + P)
                for part, (bk, signal) in enumerate(((bank[s], "g_mm"), (bank[HB[u][s]], "h_mm"))):
                    c = w[part]
                    if i is not None:
                        n = i(0, s)
                        pe.wait_ge(S["gelu_done" if part == 0 else "a_ready"], n - 1)
                    mm(bk[:], w1hi[:, c], x2hi[:, s, :], start=True, stop=False)
                    mm(bk[:], w1hi[:, c], x2lo[:, s, :], start=False, stop=False)
                    mm(bk[:], w1lo[:, c], x2hi[:, s, :], start=False, stop=True).then_inc(S[signal], 1)

            def fc2(u, s, n):
                pe.wait_ge(S["alo_ready"], n + 3)
                hi, lo = ahi[:, s * N:(s + 1) * N], alo[:, s * N:(s + 1) * N]
                c = slice(u * D, (u + 1) * D)
                mm(bank[4 + s][:], w2hi[:, c], hi, start=False, stop=False, skip_group_check=True)
                mm(bank[4 + s][:], w2hi[:, c], lo, start=False, stop=False, skip_group_check=True)
                mm(bank[4 + s][:], w2lo[:, c], hi, start=False, stop=False, skip_group_check=True).then_inc(S["fc2_mm"], 1)

            def residual(s):
                pe.wait_ge(S["c_ident16"], 2)
                pe.wait_ge(S["oraw_ready"], 4)
                mm(bank[4 + s][:], identr[:], x2hi[:, s, :], start=True, stop=False, skip_group_check=True)
                mm(bank[4 + s][:], identr[:], x2lo[:, s, :], start=False, stop=False, skip_group_check=True)\
                    .then_inc(S["fc2_mm"], 1)

            pe.wait_ge(S["w1hi_ready"], 1)
            pe.wait_ge(S["w1lo_ready"], 1)
            residual(0)
            pe.wait_ge(S["p_ready"], 32)
            fc1(0, 0)
            wo_x(1)
            pe.wait_ge(S["y2_ready"], 1)
            x2_transposes(1, 0)
            x2_transposes(1, 1)
            pe.wait_ge(S["x2hi_ready"], 2)
            pe.wait_ge(S["x2lo_ready"], 2)
            residual(1)
            router(1)
            pe.wait_ge(S["y2_ready"], 2)
            fc1(0, 1)
            comb_transposes(1)
            pe.wait_ge(S["lg_ready"], 2)
            pe.wait_ge(S["cT_ready"], 2)

            with pe.Fori(0, (U - 1) // UPL) as i:
                for j in range(UPL):
                    par = (1 + j) % 2
                    pe.wait_ge(S["w1hi_ready"], UPL * i + (j + 2))
                    pe.wait_ge(S["w1lo_ready"], UPL * i + (j + 2))
                    for s in range(B):
                        fc1(par, s, lambda _, s: 2 * UPL * i + (2 * (1 + j) + s))
                    pe.wait_ge(S["w2hi_ready"], UPL * i + (j + 1))
                    pe.wait_ge(S["w2lo_ready"], UPL * i + (j + 1))
                    for s in range(B):
                        fc2(1 - par, s, 2 * UPL * i + (2 * j + s))
            for s in range(B):
                fc2((U - 1) % 2, s, 2 * (U - 1) + s)
                if s == 0:
                    pe.wait_ge(S["cT_ready"], B)
                    pe.wait_ge(S["ld_small"], 48)
                mm(bank[4 + s][:], b2_sb[:], combT[:, s, :], start=False, stop=True, skip_group_check=True)\
                    .then_inc(S["ybias_mm"], 1)
            for s in range(B):
                pe.wait_ge(S[f"yT{s}_ready"], 1)
                for k in range(TPB):
                    r = nc.tensor.transpose(bank[s][:, k * P:(k + 1) * P], yT[:, s, k * P:(k + 1) * P], ident[:])
                r.then_inc(S["yt_mm"], 1)

        @block.gpsimd
        def _(pool):
            pool.memset(vsb[:, :, P:P + 1], 1.0).then_inc(S["c_misc"], 1)
            pool.memset(mcol[:], 1.0 / NS).then_inc(S["c_misc"], 1)
            pool.memset(epsc[:], LNEPS).then_inc(S["c_misc"], 1)
            pool.memset(headmask[:], 1.0).then_inc(S["c_headmask"], 1)
            pool.memset(ident[:], 0.0).then_inc(S["c_zero"], 1)
            pool.wait_ge(S["c_headmask"], 1)
            hm = headmask[:].rearrange("p (h d) -> p h d", d=DH)
            pool.affine_select(out=hm, in_=hm, compare_op=ALU.is_ge, fill=0.0, base=0,
                               pattern=[[-DH, H], [0, DH]], channel_multiplier=1).then_inc(S["c_headmask"], 1)
            pool.wait_ge(S["c_headmask"], 2)
            pool.affine_select(out=hm, in_=hm, compare_op=ALU.is_ge, fill=0.0, base=DH - 1,
                               pattern=[[DH, H], [0, DH]], channel_multiplier=-1).then_inc(S["c_headmask"], 1)
            pool.wait_ge(S["c_zero"], 1)
            pool.affine_select(out=ident[:], in_=ident[:], compare_op=ALU.not_equal, fill=1.0, base=0,
                               pattern=[[-1, P]], channel_multiplier=1).then_inc(S["c_ident"], 1)
            pool.memset(mv_t2[:], 0.0).then_inc(S["c_mvt0"], 1)
            pool.wait_ge(S["ld_x"], 16)
            pool.wait_ge(S["ld_bias"], 80)
            for t0, t1 in PAIRS:
                pool.tensor_tensor(xb[:, t0:t1 + 1, :], x_sb[:, t0:t1 + 1, :],
                                   bo_bc[:, 0:1, :].broadcast_to([P, 2, D]), ALU.add).then_inc(S["xb_ready"], 1)
            pool.memset(maskf[:], 0.0).then_inc(S["c_maskf"], 1)
            pool.memset(selD[:], 0.0).then_inc(S["c_selD0"], 1)
            pool.wait_ge(S["c_maskf"], 1)
            pool.affine_select(out=maskf[:, 0, :], in_=maskf[:, 0, :], compare_op=ALU.is_ge, fill=NEG, base=0,
                               pattern=[[-1, P]], channel_multiplier=1).then_inc(S["c_maskf"], 1)
            pool.affine_select(out=maskf[:, 1, :], in_=maskf[:, 1, :], compare_op=ALU.is_ge, fill=NEG, base=0,
                               pattern=[[1, P]], channel_multiplier=-1).then_inc(S["c_maskf"], 1)
            pool.wait_ge(S["c_selD0"], 1)
            sd = selD[:].rearrange("p (w c) -> p w c", c=32)
            pool.affine_select(out=sd, in_=sd, compare_op=ALU.not_equal, fill=1.0, base=-DH,
                               pattern=[[-32, G], [0, 32]], channel_multiplier=1).then_inc(S["c_selD"], 1)
            pool.memset(mmA[:], 0.0).then_inc(S["c_mm0"], 1)
            pool.memset(mmB[:], 0.0).then_inc(S["c_mm0"], 1)
            pool.memset(va[:], 0.0).then_inc(S["c_va0"], 1)
            pool.wait_ge(S["c_va0"], 1)
            pool.memset(va[:, :, :, :, DH:DH + 1], 1.0).then_inc(S["va_ready"], 1)
            pool.wait_ge(S["vx_ready"], 2)
            for b in range(B):
                for c, n in enumerate((P, C2)):
                    pool.tensor_copy(va[0:n, b, c, :, 0:DH].rearrange("p (v g) d -> p v g d", v=G),
                                     vx[0:n, b, c, :].rearrange("p (g v d) -> p v g d", g=G, v=G))                        .then_inc(S["va_ready"], 1)
            for g in range(G):
                pool.wait_ge(S["kst_full"], g + 1)
                pool.wait_ge(S["lomask_ready"], 2)
                pool.tensor_scalar(hisk[:, g, :], fullk[:, g, :], lomask[:, 1:2], None, ALU.mult).then_inc(S["kst_his"], 1)
                pool.wait_ge(S["kst_his"], g + 1)
                pool.tensor_tensor(ks[:, g, :], fullk[:, g, :], hisk[:, g, :].bitcast(F32), ALU.subtract)                    .then_inc(S["ks_ready"], 1)
            pool.memset(on[:], 0.0).then_inc(S["c_on0"], 1)
            pool.memset(gate_sb[:, E:16], 0.0).then_inc(S["c_gate0"], 1)
            pool.memset(lg[:], PAD).then_inc(S["c_lg0"], 1)
            pool.memset(vals[:], PAD).then_inc(S["c_lg0"], 1)
            pool.memset(comb[:, :, E:16], 1.0).then_inc(S["c_comb0"], 1)
            pool.memset(w1_sb[:, U, :], 0.0).then_inc(S["c_w1pad"], 1)
            pool.memset(b1_sb[:, U, :], 0.0).then_inc(S["c_w1pad"], 1)

            for t in (0, 1, 4, 5):
                pool.wait_ge(S["cb_ready"], 1)
                pool.wait_ge(S["x1_ready"], POS[t] + 1)
                pool.tensor_tensor(y2[:, t, :], x1[:, t, :], cb[:, t // TPB, :], ALU.add).then_inc(S["y2a_ready"], 1)
            for n, t in enumerate((2, 3, 6, 7)):
                pool.wait_ge(S["x1_ready"], POS[t] + 1)
                pool.tensor_tensor(x1b[:, t, :], x1[:, t, :], bo_bc[:, 2, :], ALU.add).then_inc(S["x1b_ready"], 1)

            pool.wait_ge(S["pv_mm"], 8)
            pool.memset(comb_bc[:, 0, :, :], 1.0).then_inc(slot_filled[0], 16)

            def w1lo_stage(u, par):
                pool.wait_ge(S["w1hi_ready"], u + 1)
                pool.wait_ge(S["ld_w1"], 16)
                pool.tensor_tensor(w1lo[:, par * 256:par * 256 + 256], w1_sb[:, bass.ds(u, 1), :].rearrange("p a n -> p (a n)"),
                                   w1hi[:, par * 256:par * 256 + 256].bitcast(F32), ALU.subtract).then_inc(S["w1lo_ready"], 1)

            def gate_product(n, s, slot_):
                pool.wait_ge(S["gelu_done"], n + 1)
                pool.tensor_tensor(gl[:, s, :], gl[:, s, :], comb_bc[:, slot_, s, :], ALU.mult).then_inc(S["gc_ready"], 1)

            pool.wait_ge(S["c_w1pad"], 1)
            w1lo_stage(0, 0)
            w1lo_stage(1, 1)
            pool.wait_ge(slot_filled[0], 16)
            for s in range(B):
                gate_product(s, s, 0)
            with pool.Fori(0, (U - 1) // UPL) as i:
                for j in range(UPL):
                    u = UPL * i + (1 + j)
                    w1lo_stage(UPL * i + (2 + j), (2 + j) % 2)
                    pool.wait_ge(slot_filled[j], 16 * i + 16)
                    for s in range(B):
                        gate_product(2 * UPL * i + (2 * (1 + j) + s), s, j)

        @block.vector
        def _(dve):
            sub_, add_, mul_ = ALU.subtract, ALU.add, ALU.mult
            dve.memset(start[:, 0:1], 0.0).then_inc(S["a_ready"], 2)
            dve.memset(start[:, 1:2], 0.0).then_inc(S["alo_ready"], 2)
            for i in range(4):
                dve.wait_ge(S["ek_done"], i + 1)
                dve.tensor_scalar(ek[:, i, :, :], ek[:, i, :, :], 1.0, None, ALU.min).then_inc(S["ekmin_done"], 1)
                dve.wait_ge(S["ekmin_done"], i + 1)
                dve.wait_ge(S["v_ready"], i + 1)
                dve.scalar_tensor_tensor(out=ksb[:, 2 * i:2 * i + 2, :],
                                         in0=bank[i][:].rearrange("p (t n) -> p t n", t=2)[:, :, 0:P], scalar=0.0,
                                         in1=ek[:, i, :, :], op0=ALU.max, op1=add_).then_inc(S["k_ready"], 1)
            for b in range(B):
                dve.wait_ge(S["eq_done"], b + 1)
                dve.tensor_scalar(eq[:, b, :], eq[:, b, :], 1.0, None, ALU.min).then_inc(S["eqmin_done"], 1)
                dve.wait_ge(S["eqmin_done"], b + 1)
                dve.scalar_tensor_tensor(out=qT[:, b, :], in0=bank[4 + b][:], scalar=0.0, in1=eq[:, b, :],
                                         op0=ALU.max, op1=add_).then_inc(S["q_ready"], 1)
            dve.wait_ge(S["c_headmask"], 3)
            for b in range(B):
                dve.wait_ge(S["kvs_mm"], b + 1)
                dve.tensor_tensor(bd[:, b, 0:P], bank[b][:, 0:P], headmask[:], mul_).then_inc(S["bd_ready"], 1)
                dve.tensor_scalar(bd[:, b, P:P + H], headmask[:, 0:P:DH], bank[b][:, P:P + 1], None, mul_)                    .then_inc(S["bdk_ready"], 1)
            dve.wait_ge(S["vx_mm"], 1)
            dve.wait_ge(S["ld_bias"], 80)
            v6 = bank[6][:].rearrange("p (b c d) -> p b c d", b=B, c=2)
            for c, n in enumerate((P, C2)):
                dve.tensor_tensor(vx[0:n, :, c, :], v6[0:n, :, c, :], bo_bc[0:n, 1:2, :].broadcast_to([n, B, D]), add_)                    .then_inc(S["vx_ready"], 1)
            hw = headmask[:].rearrange("p (w c d) -> p w c d", w=G, c=4)
            dve.tensor_reduce(lomask[:, 0:1], hw[:, :, 2:4, 0], AX.XY, add_).then_inc(S["lomask_ready"], 1)
            dve.tensor_reduce(lomask[:, 1:2], hw[:, :, 1, 0], AX.X, add_).then_inc(S["lomask_ready"], 1)

            def kfull(g):
                dve.wait_ge(S["kst_mm"], g + 1)
                dve.tensor_scalar(fullk[:, g, :], bank[KSTBANK[g]][:, 0:B * NS], bqk_sb[:, 1, g:g + 1], None, add_)                    .then_inc(S["kst_full"], 1)

            def normalise(i):
                dve.wait_ge(S["num_mm"], i + 1)
                o = bank[NUMBANK[i]][:].rearrange("p (t n) -> p t n", t=2)
                dve.tensor_scalar(rden[:, i, :, :], o[:, :, P:P + H], EPS, None, add_).then_inc(S["den_ready"], 1)
                dve.wait_ge(S["den_ready"], i + 1)
                dve.reciprocal(rden[:, i, :, :], rden[:, i, :, :]).then_inc(S["rden_ready"], 1)
                dve.wait_ge(S["rden_ready"], i + 1)
                dve.tensor_tensor(osb[:, i, :, :].rearrange("p t (h d) -> p t h d", h=H),
                                  o[:, :, 0:P].rearrange("p t (h d) -> p t h d", h=H),
                                  rden[:, i, :, :].unsqueeze(3).broadcast_to([P, 2, H, DH]), mul_).then_inc(S["o_ready"], 1)

            kfull(0)
            kfull(1)
            normalise(0)
            kfull(2)
            normalise(1)
            kfull(3)
            dve.wait_ge(S["mean_mm"], 1)
            dve.wait_ge(S["c_mvt0"], 1)
            for b in range(B):
                dve.tensor_copy(mv_bc[:, b, :], bank[7][:, b:b + 1].broadcast_to([P, P])).then_inc(S["mvbc_ready"], 1)
                dve.tensor_copy(mv_t2[:, b, 0:QB0], bank[7][:, b:b + 1].broadcast_to([P, QB0])).then_inc(S["mvbc_ready"], 1)
            normalise(2)
            normalise(3)
            dve.wait_ge(S["cb_mm"], 1)
            dve.tensor_tensor(cb[:], bank[7][:, P:P + B * D].rearrange("p (b d) -> p b d", b=B),
                              bo_bc[:, 2:3, :].broadcast_to([P, B, D]), add_).then_inc(S["cb_ready"], 1)

            def stats(src, st_, mv_, tiles, n0, s_st, s_mv):
                for t in tiles:
                    dve.bn_stats(st_[:, t, :], src(t)).then_inc(S[s_st], 1)
                for n, t in enumerate(tiles):
                    dve.wait_ge(S[s_st], n0 + n + 1)
                    dve.bn_aggr(mv_[:, t, :], st_[:, t, :]).then_inc(S[s_mv], 1)

            def apply(dst, src, mv_, rs, tiles, signal):
                for t in tiles:
                    dve.tensor_scalar(dst[:, t, :], src(t), mv_[:, t, 0:1], rs[:, t:t + 1], sub_, mul_).then_inc(S[signal], 1)

            def first_norm(h):
                dve.wait_ge(S["wo_mm"], h + 1)
                for q in range(2):
                    i = 2 * h + q
                    t = PAIRS[i][0]
                    dve.wait_ge(S["xb_ready"], i + 1)
                    dve.tensor_tensor(y[:, t:t + 2, :], bank[WOBANK[h]][:, q * 256:(q + 1) * 256].rearrange("p (t d) -> p t d", t=2),
                                      xb[:, t:t + 2, :], add_).then_inc(S["y_ready"], 1)
                dve.wait_ge(S["y_ready"], 2 * h + 2)
                stats(lambda t: y[:, t, :], st, mv, PAIRS[2 * h] + PAIRS[2 * h + 1], 4 * h, "st_done", "mv_ready")

            def first_apply(h):
                dve.wait_ge(S["rstd_ready"], h + 1)
                apply(x1, lambda t: y[:, t, :], mv, rstd, PAIRS[2 * h] + PAIRS[2 * h + 1], "x1_ready")

            first_norm(0)
            first_apply(0)
            first_norm(1)
            dve.wait_ge(S["ks_ready"], G)
            for g in range(G):
                dve.wait_ge(S["qst_mm"], g + 1)
                dve.tensor_scalar(fullq[:, g, :], bank[g][:, 0:B * NS], bqk_sb[:, 0, g:g + 1], SCALE, add_, mul_)                    .then_inc(S["qst_full"], 1)
            for g in range(G):
                dve.wait_ge(S["qst_his"], g + 1)
                dve.tensor_tensor(qs[:, g, :], fullq[:, g, :], hisq[:, g, :].bitcast(F32), sub_).then_inc(S["qs_ready"], 1)
                if g == 0:
                    dve.wait_ge(S["c_ident"], 1)
                    dve.wait_ge(S["c_maskf"], 3)
                    dve.tensor_copy(ident16[:], ident[:]).then_inc(S["c_ident16"], 1)
                    dve.tensor_copy(maskS[:], maskf[:, 0, :]).then_inc(S["c_mask16"], 1)
                    dve.tensor_copy(maskT[:], maskf[:, 1, :]).then_inc(S["c_mask16"], 1)
            first_apply(1)

            def maxima(n):
                b, c = divmod(n, 8)
                bk = bank[n % 2]
                dve.wait_ge(S["s_mm"], n + 1)
                dve.tensor_reduce(mA[:, b, 2 * c:2 * c + 2], bk[:, 0:2 * NS].rearrange("p (h n) -> p h n", h=2), AX.X, ALU.max)                    .then_inc(S["m_ready"], 1)
                dve.tensor_reduce(mB[0:QB, b, 2 * c:2 * c + 2], bk[0:QB, 2 * NS:2 * NS + 2 * C2].rearrange("p (h n) -> p h n", h=2),
                                  AX.X, ALU.max).then_inc(S["m_ready"], 1)

            def maxima_split(b):
                dve.wait_ge(S["m_ready"], 16 * (b + 1))
                dve.wait_ge(S["c_mm0"], 2)
                if b:
                    dve.wait_ge(S["mt_mm"], 1)
                views = [(t[0:r].rearrange("p g (v c) -> p g v c", v=G), m[0:r, b, :].rearrange("p (v g) -> p g v", v=G))
                         for t, m, r in ((mmA, mA, P), (mmB, mB, QB))]
                for to, m in views:
                    dve.tensor_scalar(to[:, :, :, 3 * DH].bitcast(F32R), m, -1.0, None, mul_).then_inc(S["mhi_ready"], 1)
                for n, (to, m) in enumerate(views):
                    dve.wait_ge(S["mhi_ready"], 2 * b + n + 1)
                    dve.scalar_tensor_tensor(out=to[:, :, :, 3 * DH + 1], in0=m, scalar=-1.0, in1=to[:, :, :, 3 * DH],
                                             op0=mul_, op1=sub_).then_inc(S["mlo_ready"], 1)
                dve.wait_ge(S["mt_mm"], b + 1)
                for hf in range(2):
                    q = qs[:, 2 * hf:2 * hf + 2, b * NS:(b + 1) * NS]
                    dve.tensor_tensor(q, bank[6 + hf][:, 0:2 * NS].rearrange("p (g n) -> p g n", g=2), q.bitcast(F32), add_)\
                        .then_inc(S["qm_ready"], 1)

            def second_norm(tiles, n0):
                stats(lambda t: y2[:, t, :], st2, mv2, tiles, n0, "st2_done", "mv2_ready")

            def second_apply(tiles, n):
                dve.wait_ge(S["rstd2_ready"], n)
                apply(x2, lambda t: y2[:, t, :], mv2, rstd2, tiles, "x2_ready")

            def b1g_stage(u, par):
                dve.wait_ge(S["ld_small"], 48)
                dve.tensor_copy(b1g[:, par:par + 1], b1_sb[:, bass.ds(u, 1), 1:2].rearrange("p a b -> p (a b)"))\
                    .then_inc(S["b1g_ready"], 1)

            def w1hi_stage(u, par):
                dve.wait_ge(S["ld_w1"], 16)
                dve.tensor_copy(w1hi[:, par * 256:par * 256 + 256], w1_sb[:, bass.ds(u, 1), :].rearrange("p a n -> p (a n)"))                    .then_inc(S["w1hi_ready"], 1)

            def o_normalise(b):
                dve.wait_ge(S["c_on0"], 1)
                for hf in range(2):
                    dve.wait_ge(S["rdx_ready"], 2 * b + hf + 1)
                    dve.tensor_tensor(on[:, b, 2 * hf:2 * hf + 2, QB0:2 * P], oraw[:, b, 2 * hf:2 * hf + 2, :],
                                      rdx[:, b, 2 * hf:2 * hf + 2, :], mul_).then_inc(S["on_ready"], 1)

            def attended(b):
                dve.wait_ge(S["wox_mm"], b + 1)
                dve.wait_ge(S["x1b_ready"], 2 * b + 2)
                t = b * TPB + 2
                dve.tensor_tensor(y2[:, t:t + 2, :], bank[1 + 2 * b][:, 0:2 * P].rearrange("p (t d) -> p t d", t=2), x1b[:, t:t + 2, :], add_)                    .then_inc(S["y2_ready"], 1)
                dve.wait_ge(S["y2_ready"], b + 1)
                second_norm((t, t + 1), 4 + 2 * b)
                second_apply((t, t + 1), 2 + b)

            def x2_split(b):
                dve.wait_ge(S["x2hi_ready"], b + 1)
                dve.tensor_tensor(x2lo[:, b, :], bank[X2BANK[b]][:], x2hi[:, b, :].bitcast(F32), sub_).then_inc(S["x2lo_ready"], 1)

            def gates(b):
                T = slice(b * TPB, (b + 1) * TPB)
                dve.wait_ge(S["lg_mm"], b + 1)
                dve.wait_ge(S["c_lg0"], 2)
                dve.tensor_copy(lg[:, T, 0:E], bank[6][:, 0:TPB * 16].rearrange("p (t e) -> p t e", e=16)[:, :, 0:E])                    .then_inc(S["lg_ready"], 1)
                dve.wait_ge(S["lg_ready"], b + 1)
                for t in range(b * TPB, (b + 1) * TPB):
                    dve.max(top[:, t, :], lg[:, t, 0:E]).then_inc(S["top_ready"], 1)
                dve.wait_ge(S["top_ready"], TPB * (b + 1))
                dve.tensor_copy(vals[:, T, 0:3], top[:, T, 0:3]).then_inc(S["vals_ready"], 1)
                dve.tensor_tensor(dl[:, T, :], lg[:, T, 0:E], top[:, T, 0:1].broadcast_to([P, TPB, E]), sub_).then_inc(S["dl_ready"], 1)
                dve.wait_ge(S["vals_ready"], b + 1)
                for t in range(b * TPB, (b + 1) * TPB):
                    dve.match_replace(rep[:, t, :], vals[:, t, :], lg[:, t, :], PAD).then_inc(S["rep_ready"], 1)
                dve.wait_ge(S["rep_ready"], TPB * (b + 1))
                dve.tensor_tensor(sel[:, T, :], rep[:, T, 0:E], lg[:, T, 0:E], ALU.not_equal).then_inc(S["sel_ready"], 1)
                dve.wait_ge(S["el_ready"], b + 1)
                dve.wait_ge(S["sel_ready"], b + 1)
                dve.tensor_tensor(em[:, T, :], el[:, T, :], sel[:, T, :], mul_).then_inc(S["em_ready"], 1)
                dve.tensor_reduce(zs[:, T], el[:, T, :], AX.X, add_).then_inc(S["zs_ready"], 1)
                dve.wait_ge(S["em_ready"], b + 1)
                dve.tensor_reduce(s3[:, T], em[:, T, :], AX.X, add_).then_inc(S["s3_ready"], 1)
                dve.wait_ge(S["s3_ready"], b + 1)
                dve.wait_ge(S["zs_ready"], b + 1)
                dve.scalar_tensor_tensor(out=dn[:, T], in0=zs[:, T], scalar=1e-20, in1=s3[:, T], op0=mul_, op1=add_)                    .then_inc(S["dn_ready"], 1)
                dve.wait_ge(S["dn_ready"], b + 1)
                dve.reciprocal(rd[:, T], dn[:, T]).then_inc(S["rd_ready"], 1)
                dve.wait_ge(S["rd_ready"], b + 1)
                dve.wait_ge(S["c_comb0"], 1)
                dve.tensor_tensor(comb[:, T, 0:E], em[:, T, :], rd[:, T].unsqueeze(2).broadcast_to([P, TPB, E]), mul_)                    .then_inc(S["comb_ready"], 1)

            for n in range(8):
                maxima(n)
                if n == 4:
                    dve.wait_ge(S["ld_gate"], 16)
                    dve.wait_ge(S["c_gate0"], 1)
                    dve.tensor_copy(ghi[:], gate_sb[:]).then_inc(S["g_hi"], 1)
                    dve.wait_ge(S["g_hi"], 1)
                    dve.tensor_tensor(glo[:], gate_sb[:], ghi[:].bitcast(F32), sub_).then_inc(S["g_lo"], 1)
                    dve.tensor_copy(identr[:], ident[:]).then_inc(S["c_ident16"], 1)
            maxima_split(0)
            for n in range(8, 16):
                maxima(n)
                if n == 8:
                    dve.wait_ge(S["y2a_ready"], 4)
                    second_norm((0, 1, 4, 5), 0)
                if n == 9:
                    second_apply((0, 1, 4, 5), 1)
                if n == 10:
                    x2_split(0)
                if n == 12:
                    gates(0)
            maxima_split(1)
            w1hi_stage(0, 0)
            w1hi_stage(1, 1)
            dve.wait_ge(S["c_w1pad"], 2)
            b1g_stage(0, 0)
            b1g_stage(1, 1)

            o_normalise(0)
            attended(0)
            o_normalise(1)
            attended(1)
            x2_split(1)
            gates(1)

            def w2_stage(u, par):
                c = slice(par * D, (par + 1) * D)
                w = w2_sb[:, bass.ds(u, 1), :].rearrange("p a n -> p (a n)")
                m = mult_sb[:, bass.ds(u, 1)]
                dve.tensor_scalar(w2hi[:, c], w, m, None, mul_).then_inc(S["w2hi_ready"], 1)
                dve.wait_ge(S["w2hi_ready"], u + 1)
                dve.scalar_tensor_tensor(out=w2lo[:, c], in0=w, scalar=m, in1=w2hi[:, c].bitcast(F32), op0=mul_, op1=sub_)                    .then_inc(S["w2lo_ready"], 1)

            def act_product(n, s, u, par, first=False):
                dve.wait_ge(S["gc_ready"], n + 1)
                dve.wait_ge(S["h_mm"], n + 1)
                if not first:
                    dve.wait_ge(S["alo_ready"], n + 1)
                dve.scalar_tensor_tensor(out=a[:, s, :], in0=bank[HB[par][s]][:], scalar=b1_sb[:, bass.ds(u, 1), 0:1].rearrange("p a b -> p (a b)"),
                                         in1=gl[:, s, :], op0=add_, op1=mul_).then_inc(S["a_ready"], 1)

            def act_lo(n, s):
                dve.wait_ge(S["ahi_ready"], n + 1)
                dve.tensor_tensor(alo[:, s * N:(s + 1) * N], a[:, s, :], ahi[:, s * N:(s + 1) * N].bitcast(F32), sub_)                    .then_inc(S["alo_ready"], 1)

            dve.wait_ge(S["ld_w2"], 16)
            dve.wait_ge(S["ld_small"], 48)
            w2_stage(0, 0)
            act_product(0, 0, 0, 0, first=True)
            with dve.Fori(0, (U - 1) // UPL) as i:
                for j in range(UPL):
                    u = UPL * i + (1 + j)
                    par = (1 + j) % 2
                    dve.wait_ge(S["h_mm"], 2 * UPL * i + 2 * (1 + j))
                    w1hi_stage(UPL * i + (2 + j), 1 - par)
                    act_product(2 * UPL * i + (2 * j + 1), 1, UPL * i + j, 1 - par)
                    act_lo(2 * UPL * i + 2 * j, 0)
                    b1g_stage(UPL * i + (2 + j), 1 - par)
                    dve.wait_ge(S["fc2_mm"], 2 * UPL * i + (2 * j + 2))
                    w2_stage(u, par)
                    act_lo(2 * UPL * i + (2 * j + 1), 1)
                    act_product(2 * UPL * i + (2 * j + 2), 0, u, par)
            act_product(2 * U - 1, 1, U - 1, (U - 1) % 2)
            act_lo(2 * U - 2, 0)
            act_lo(2 * U - 1, 1)

            dve.wait_ge(S["ybias_mm"], 2)
            dve.tensor_copy(yT[:, 1, :], bank[5][:]).then_inc(S["yT1_ready"], 1)
            for b in range(B):
                dve.wait_ge(S["yt_mm"], b + 1)
                T = range(b * TPB, (b + 1) * TPB)
                src = lambda t: bank[t // TPB][:, (t % TPB) * P:(t % TPB + 1) * P]
                stats(src, st3, mv3, T, 4 * b, "st3_done", "mv3_ready")
                dve.wait_ge(S["rstd3_ready"], b + 1)
                apply(res, src, mv3, rstd3, T, "res_ready")

        @block.scalar
        def _(act):
            def A(out, in_, f, **kw):
                return nc.scalar.activation(out, in_, f, **kw)

            act.preload_act_table_set("natural_log_exp_and_others")
            for b in range(B):
                act.dma_start(xT_sb[:, b * N:(b + 1) * N], xT[:, b * N:(b + 1) * N]).then_inc(S[f"ld_xT{b}"], 16)
            for i in range(4):
                o = bank[i][:].rearrange("p (t n) -> p t n", t=2)
                act.wait_ge(S["kv_mm"], i + 1)
                A(ek[:, i, :, :], o[:, :, 0:P], ACT.Exp).then_inc(S["ek_done"], 1)
                A(vsb[:, 2 * i:2 * i + 2, 0:P], o[:, :, P:2 * P], ACT.Copy).then_inc(S["v_ready"], 1)
            for b in range(B):
                act.wait_ge(S["q_mm"], b + 1)
                A(eq[:, b, :], bank[4 + b][:], ACT.Exp).then_inc(S["eq_done"], 1)

            def rsqrt(mv_view, ln_view, rs_view, n, names):
                act.wait_ge(S["c_misc"], 3)
                A(ln_view, mv_view, ACT.Ln, bias=epsc[:, 0:1]).then_inc(S[names[0]], 1)
                act.wait_ge(S[names[0]], n)
                A(rs_view, ln_view, ACT.Exp, scale=-0.5).then_inc(S[names[1]], 1)

            def tiles_of(tensor, k0):
                return tensor[:].rearrange("p (b k) -> p b k", b=B)[:, :, k0:k0 + 2]

            def var_of(tensor, k0):
                return tensor[:].rearrange("p (b k) s -> p b k s", b=B)[:, :, k0:k0 + 2, 1]

            for h in range(2):
                act.wait_ge(S["oT_mm"], h + 1)
                A(oT[:, h, :, :].rearrange("p c n -> p (c n)"), bank[2 + h][:], ACT.Copy).then_inc(S["oT_ready"], 1)
            act.wait_ge(S["mv_ready"], 4)
            rsqrt(var_of(mv, 2), tiles_of(lnv, 2), tiles_of(rstd, 2), 1, ("lnv_done", "rstd_ready"))
            for b in range(B):
                act.wait_ge(S["x1T_mm"], b + 1)
                A(x1T[:, b, :], bank[4 + b][:, QB0:2 * P], ACT.Copy).then_inc(S["x1T_ready"], 1)
            act.wait_ge(S["mv_ready"], 8)
            rsqrt(var_of(mv, 0), tiles_of(lnv, 0), tiles_of(rstd, 0), 2, ("lnv_done", "rstd_ready"))
            act.wait_ge(S["lomask_ready"], 2)
            for g in range(G):
                act.wait_ge(S["qst_full"], g + 1)
                A(hisq[:, g, :], fullq[:, g, :], ACT.Copy, scale=lomask[:, 0:1]).then_inc(S["qst_his"], 1)

            def probabilities(n):
                b, c = divmod(n, 8)
                bk = bank[2 + n % 2]
                act.wait_ge(S["sT_mm"], n + 1)
                A(pT1[:, b, 2 * c:2 * c + 2, :], bk[:, 0:2 * NS].rearrange("p (h n) -> p h n", h=2), ACT.Exp).then_inc(S["p_ready"], 1)
                A(pT2[0:C2, b, 2 * c:2 * c + 2, :], bk[0:C2, 2 * NS:2 * NS + 2 * C2].rearrange("p (h n) -> p h n", h=2), ACT.Exp)                    .then_inc(S["p_ready"], 1)

            def o_copy(b, hf):
                act.wait_ge(S["pv_mm"], 4 * b + 2 * hf + 2)
                A(oraw[:, b, 2 * hf:2 * hf + 2, :], bank[4 + hf][:, 0:2 * NS].rearrange("p (u n) -> p u n", u=2), ACT.Copy)                    .then_inc(S["oraw_ready"], 1)

            def attended_rsqrt(b):
                t = slice(b * TPB + 2, b * TPB + 4)
                act.wait_ge(S["mv2_ready"], 6 + 2 * b)
                rsqrt(mv2[:, t, 1], lnv2[:, t], rstd2[:, t], 2 + b, ("lnv2_done", "rstd2_ready"))

            def x2_hi(b):
                act.wait_ge(S["x2T_mm"], b + 1)
                A(x2hi[:, b, :], bank[X2BANK[b]][:], ACT.Copy).then_inc(S["x2hi_ready"], 1)

            def gate_exp(b):
                T = slice(b * TPB, (b + 1) * TPB)
                act.wait_ge(S["dl_ready"], b + 1)
                A(el[:, T, :], dl[:, T, :], ACT.Exp).then_inc(S["el_ready"], 1)

            def comb_copy(s):
                act.wait_ge(S["cT_mm"], s + 1)
                A(combT[:, s, :], bank[7][0:16, :], ACT.Copy).then_inc(S["cT_ready"], 1)

            def den_inverse(b):
                for hf in range(2):
                    act.wait_ge(S["db_mm"], 2 * b + hf + 1)
                    if b == 0:
                        act.wait_ge(S["qs_ready"], G)
                    A(rdx[:, b, 2 * hf:2 * hf + 2, :], bank[6 + hf][:, 0:2 * NS].rearrange("p (u n) -> p u n", u=2), ACT.Ln)\
                        .then_inc(S["rln_ready"], 1)
                for hf in range(2):
                    act.wait_ge(S["rln_ready"], 2 * b + hf + 1)
                    A(rdx[:, b, 2 * hf:2 * hf + 2, :], rdx[:, b, 2 * hf:2 * hf + 2, :], ACT.Exp, scale=-1.0)\
                        .then_inc(S["rdx_ready"], 1)

            for n in range(16):
                probabilities(n)
                if n == 1:
                    act.wait_ge(S["mv2_ready"], 4)
                    rsqrt(var_of(mv2, 0), tiles_of(lnv2, 0), tiles_of(rstd2, 0), 1, ("lnv2_done", "rstd2_ready"))
                if n == 2:
                    x2_hi(0)
                if n == 4:
                    gate_exp(0)
                if n == 6:
                    comb_copy(0)
                if n == 7:
                    o_copy(0, 0)
                if n == 9:
                    o_copy(0, 1)
                if n == 11:
                    den_inverse(0)
                if n == 14:
                    attended_rsqrt(0)
            o_copy(1, 0)
            o_copy(1, 1)
            den_inverse(1)
            attended_rsqrt(1)
            x2_hi(1)
            gate_exp(1)
            comb_copy(1)

            def gelu(n, s, u, par, first=False):
                act.wait_ge(S["g_mm"], n + 1)
                if not first:
                    act.wait_ge(S["a_ready"], n + 1)
                act.wait_ge(S["b1g_ready"], u + 1)
                A(gl[:, s, :], bank[s][:], ACT.Gelu, bias=b1g[:, par:par + 1])                    .then_inc(S["gelu_done"], 1)

            def act_hi(n, s, first=False):
                act.wait_ge(S["a_ready"], n + 3)
                if not first:
                    act.wait_ge(S["fc2_mm"], n + 1)
                A(ahi[:, s * N:(s + 1) * N], a[:, s, :], ACT.Copy).then_inc(S["ahi_ready"], 1)

            gelu(0, 0, 0, 0, first=True)
            gelu(1, 1, 0, 0, first=True)
            act_hi(0, 0, first=True)
            with act.Fori(0, (U - 1) // UPL) as i:
                for j in range(UPL):
                    u = UPL * i + (1 + j)
                    gelu(2 * UPL * i + (2 * j + 2), 0, u, (1 + j) % 2)
                    act_hi(2 * UPL * i + (2 * j + 1), 1)
                    gelu(2 * UPL * i + (2 * j + 3), 1, u, (1 + j) % 2)
                    act_hi(2 * UPL * i + (2 * j + 2), 0)
            act_hi(2 * U - 1, 1)

            act.preload_act_table_set("natural_log_exp_and_others")
            act.wait_ge(S["ybias_mm"], 1)
            A(yT[:, 0, :], bank[4][:], ACT.Copy).then_inc(S["yT0_ready"], 1)
            for b in range(B):
                t = slice(b * TPB, (b + 1) * TPB)
                act.wait_ge(S["mv3_ready"], 4 * b + 4)
                rsqrt(mv3[:, t, 1], lnv3[:, t], rstd3[:, t], b + 1, ("lnv3_done", "rstd3_ready"))


def kernel(**inputs):
    import numpy as np
    import concourse.bacc as bacc
    from concourse.bass_utils import run_bass_kernel_spmd as run

    I = {k: np.asarray(v) for k, v in inputs.items()}
    c = np.ascontiguousarray

    def stacked(w, last):
        w = w.reshape(w.shape[:-1] + (G, G, 1, DH))
        w = np.concatenate([w, w, w, np.broadcast_to(np.asarray(last, w.dtype), w.shape)], axis=-2)
        return w.reshape(w.shape[:-4] + (G, P))

    none, ones = np.zeros(DH), np.arange(DH) < 2
    wq, wk = I["L0_xattn_Wq"], I["L0_xattn_Wk"]
    wo = I["L0_xattn_Wo"]
    wop = np.zeros((G, 32, G, D), wo.dtype)
    wop[:, 0:DH, :, :] = wo.reshape(G, G, DH, D).transpose(0, 2, 1, 3)
    f1, s1 = I["L0_ffn_fc1_w"], I["L0_ffn_s_fc1_w"]
    s1 = s1.reshape(2, 2, P, D).transpose(1, 0, 2, 3).reshape(2, 2 * P, D)
    sb1 = I["L0_ffn_s_fc1_b"].reshape(2, 2, P).transpose(1, 0, 2)
    f2, s2 = I["L0_ffn_fc2_w"], I["L0_ffn_s_fc2_w"]
    s2 = s2.reshape(D, 2, P).transpose(1, 0, 2)
    arrays = {
        "x": c(I["x"]),
        "xT": c(I["x"].transpose(2, 0, 1).reshape(D, B * N)),
        "ctxT": c(I["ctx_1024"].transpose(2, 0, 1).reshape(D, B * NS)),
        "wA": c(np.concatenate([I["L0_attn_W" + n].T for n in "qkvo"], axis=1)),
        "boA": c(I["L0_attn_bo"]),
        "wqs": c(stacked(wq, none)),
        "wks": c(stacked(wk, none)),
        "bqs": c(stacked(I["L0_xattn_bq"], none).T),
        "bks": c(stacked(I["L0_xattn_bk"], ones).T),
        "wv": c(I["L0_xattn_Wv"]),
        "bv": c(I["L0_xattn_bv"]),
        "wo": c(wo),
        "wop": c(wop.reshape(P, G, D)),
        "boX": c(I["L0_xattn_bo"]),
        "gateT": c(I["L0_ffn_gate_w"].T),
        "w1T": c(np.concatenate([s1, f1]).transpose(2, 0, 1)),
        "b1": c(np.concatenate([sb1, I["L0_ffn_fc1_b"].reshape(E, 2, P)]).transpose(2, 0, 1)),
        "mult": c(np.concatenate([I["L0_ffn_s_geglu_mult"].reshape(2, P), I["L0_ffn_geglu_mult"]]).T),
        "w2T": c(np.concatenate([s2, f2]).transpose(2, 0, 1)),
        "b2": c(np.concatenate([I["L0_ffn_fc2_b"], I["L0_ffn_s_fc2_b"][None]])),
    }
    nc = bacc.Bacc("TRN2", target_bir_lowering=False, num_devices=1)
    args = {n: nc.dram_tensor(n + "_d", v.shape, mybir.dt.from_np(v.dtype), kind="ExternalInput").ap() for n, v in arrays.items()}
    comb_dram = nc.dram_tensor("comb_d", (E, B, N), F32, kind="Internal").ap()
    out = nc.dram_tensor("out_d", (B, N, D), F32, kind="ExternalOutput").ap()
    build(nc, comb_dram=comb_dram, out=out, **args)
    r = run(nc, [{n + "_d": v for n, v in arrays.items()}], core_ids=[0])
    return r.results[0]["out_d"]
```

```python
from contextlib import ExitStack

import concourse.bass as bass
from concourse import mybir

F32 = mybir.dt.float32
F32R = mybir.dt.float32r
BF16 = mybir.dt.bfloat16
ALU = mybir.AluOpType
ACT = mybir.ActivationFunctionType
AX = mybir.AxisListType

P = 128
D = 128
B, N = 2, 512
NT = B * N // P
TPB = N // P
H, DH = 16, 8
NS = 154
C2 = NS - P
QA = N - NS
QB0 = QA - 2 * P
QB = P - QB0
G = 4
E = 15
U = 17
LNEPS = 1e-5
EPS = 1e-6
NEG = -1e10
PAD = -3e38
SCALE = DH ** -0.5
UPL = 4
R = 4
WSPLIT = P
LAG = 3
assert QB == C2 and QB0 + QB == P and U == 1 + UPL * 4


def build(nc, x, xT, ctxT, wA, boA, wqs, wks, bqs, bks, wv, bv, wo, wop, boX, gateT, w1T, b1, mult,
          w2T, b2, comb_dram, out):
    with ExitStack() as ctx:
        def sb(name, shape, dt=F32):
            return ctx.enter_context(nc.sbuf_tensor(name, shape, dt))

        def sem(name):
            return ctx.enter_context(nc.semaphore(name))

        bank = [ctx.enter_context(nc.psum_tensor(f"bank{i}", [P, 512], F32)) for i in range(8)]

        ident = sb("ident", [P, P])
        ident16 = sb("ident16", [P, P], BF16)
        identr = sb("identr", [P, P], F32R)
        headmask = sb("headmask", [P, P])
        selD = sb("selD", [P, P])
        maskf = sb("maskf", [P, 2, P])
        maskS = sb("maskS", [P, P], BF16)
        maskT = sb("maskT", [P, P], BF16)
        lomask = sb("lomask", [P, 2])
        mcol = sb("mcol", [P, 1])

        x_sb = sb("x_sb", [P, NT, D])
        xT_sb = sb("xT_sb", [P, NT * P])
        wA_sb = sb("wA_sb", [P, 4 * D])
        ctx_sb = sb("ctx_sb", [P, B * NS])
        bo_bc = sb("bo_bc", [P, 3, D])
        wqs_sb = sb("wqs_sb", [P, G, P])
        wks_sb = sb("wks_sb", [P, G, P])
        bqk_sb = sb("bqk_sb", [P, 2, G])
        wv_sb = sb("wv_sb", [P, D])
        wo_sb = sb("wo_sb", [P, D])
        wop_sb = sb("wop_sb", [P, G, D])
        gate_sb = sb("gate_sb", [P, 16])
        w1_sb = sb("w1_sb", [P, U, 2 * P])
        b1_sb = sb("b1_sb", [P, U, 2])
        mult_sb = sb("mult_sb", [P, U])
        w2_sb = sb("w2_sb", [P, U, D])
        b2_sb = sb("b2_sb", [16, D])

        ek = sb("ek", [P, 4, 2, P])
        ksb = sb("ksb", [P, NT, P])
        vsb = sb("vsb", [P, NT, P + 1])
        eq = sb("eq", [P, B, N])
        qT = sb("qT", [P, B, N])
        bd = sb("bd", [P, B, P + H])
        rden = sb("rden", [P, 4, 2, H])
        osb = sb("osb", [P, 4, 2, P])
        oT = sb("oT", [P, 2, 4, P])
        xb = sb("xb", [P, NT, D])
        y = sb("y", [P, NT, D])
        st = sb("st", [P, NT, 6])
        mv = sb("mv", [P, NT, 2])
        lnv = sb("lnv", [P, NT])
        rstd = sb("rstd", [P, NT])
        x1 = sb("x1", [P, NT, D])
        x1b = osb[:].rearrange("p i t d -> p (i t) d")
        epsc = sb("epsc", [P, 1])

        vx = sb("vx", [P, B, 2, D])
        va = sb("va", [P, B, 2, H, 32])
        mv_bc = sb("mv_bc", [P, B, P])
        mv_t2 = sb("mv_t2", [P, B, P])
        cb = sb("cb", [P, B, D])
        fullk = sb("fullk", [P, G, B * NS])
        fullq = fullk
        stacks = sb("stacks", [P, 2, G, B * NS], F32R)
        hisk = sb("hisk", [P, G, B * NS], F32R)
        hisq = hisk
        ks = stacks[:, 0, :, :]
        qs = stacks[:, 1, :, :]
        x1T = sb("x1T", [P, B, NS])
        mA = sb("mA", [P, B, H])
        mB = sb("mB", [P, B, H])
        mmA = sb("mmA", [P, G, P])
        mmB = sb("mmB", [P, G, P])
        pT1 = sb("pT1", [P, B, H, NS])
        pT2 = sb("pT2", [P, B, H, C2])
        oraw = sb("oraw", [P, B, G, NS])
        rdx = fullk[:].rearrange("p g (b n) -> p (g b n)", b=B).rearrange("p (b g n) -> p b g n", b=B, g=G)
        on = sb("on", [P, B, G, 2 * P])
        st2 = sb("st2", [P, NT, 6])
        mv2 = sb("mv2", [P, NT, 2])
        lnv2 = sb("lnv2", [P, NT])
        rstd2 = sb("rstd2", [P, NT])
        y2 = x_sb
        x2 = xb

        x2hi = sb("x2hi", [P, B, N], F32R)
        x2lo = sb("x2lo", [P, B, N], F32R)
        ghi = sb("ghi", [P, 16], F32R)
        glo = sb("glo", [P, 16], F32R)
        LG = E + 5
        lg = sb("lg", [P, NT, LG])
        top = sb("top", [P, NT, 8])
        vals = sb("vals", [P, NT, 8])
        rep = sb("rep", [P, NT, LG])
        sel = sb("sel", [P, NT, E])
        dl = sb("dl", [P, NT, E])
        el = sb("el", [P, NT, E])
        em = sb("em", [P, NT, E])
        zs = sb("zs", [P, NT])
        s3 = sb("s3", [P, NT])
        dn = sb("dn", [P, NT])
        rd = sb("rd", [P, NT])
        comb = sb("comb", [P, NT, 16])
        combT = sb("combT", [16, B, N])
        comb_bc = pT1[:].rearrange("p b h n -> p (b h n)")[:, 0:B * UPL * N].rearrange("p (s j n) -> p s j n", s=B, j=UPL)
        w1hi = sb("w1hi", [P, R, 2 * P], F32R)
        w1lo = hisk[:].rearrange("p g n -> p (g n)")[:, 0:R * 2 * P].rearrange("p (r n) -> p r n", r=R)
        w2hi = sb("w2hi", [P, R, D], F32R)
        w2lo = sb("w2lo", [P, R, D], F32R)
        b1g = sb("b1g", [P, R])
        ahi = stacks[:].rearrange("p a g n -> p (a g n)")[:, 0:R * N].rearrange("p (r n) -> p r n", r=R)
        alo = sb("alo", [P, R, N], F32R)
        gl = ek[:].rearrange("p i t n -> p (i t n)").rearrange("p (s n) -> p s n", s=2)
        a = eq
        yT = qT
        st3 = sb("st3", [P, NT, 6])
        mv3 = sb("mv3", [P, NT, 2])
        lnv3 = sb("lnv3", [P, NT])
        rstd3 = sb("rstd3", [P, NT])
        res = ksb

        names = (
            "ld_xT0 ld_xT1 ld_wA ld_x ld_ctx ld_wks ld_wqs ld_bias ld_wv ld_wo ld_wop ld_gate ld_w1 "
            "ld_w2 ld_small b1g_ready c_mm0 c_mvt0 c_on0 c_gate0 c_lg0 c_comb0 c_selD0 lomask_ready "
            "y2a_ready yT0_ready yT1_ready c_ident c_ident16 c_headmask qm_ready rln_ready c_selD "
            "c_maskf c_mask16 c_misc c_va0 c_zero kv_mm q_mm ek_done ekmin_done k_ready v_ready "
            "eq_done eqmin_done q_ready kvs_mm bd_ready bdk_ready num_mm den_ready rden_ready o_ready "
            "oT_mm oT_ready wo_mm xb_ready y_ready st_done mv_ready lnv_done rstd_ready x1_ready "
            "x1b_ready vx_mm vx_ready va_ready mean_mm mvbc_ready cb_mm cb_ready kst_mm kst_full "
            "kst_his ks_ready qst_mm qst_full qst_his qs_ready x1T_mm x1T_ready s_mm m_ready "
            "mhi_ready mlo_ready mt_mm sT_mm p_ready pv_mm oraw_ready db_mm rdx_ready on_ready wox_mm "
            "y2_ready st2_done mv2_ready lnv2_done rstd2_ready x2_ready x2T_mm x2hi_ready x2lo_ready "
            "g_hi g_lo lg_mm lg_ready top_ready vals_ready rep_ready sel_ready dl_ready el_ready "
            "em_ready zs_ready s3_ready dn_ready rd_ready comb_ready cT_mm cT_ready comb_stored0 "
            "comb_stored1 w1hi_ready w1lo_ready w1glo_ready w2hi_ready w2lo_ready g_mm h_mm gelu_done "
            "gc_ready a_ready ahi_ready alo_ready fc2_mm yt_mm st3_done mv3_ready lnv3_done "
            "rstd3_ready res_ready stored ").split()
        S = {n: sem(n) for n in names}
        slot_filled = [[sem(f"slot_filled{s}{j}") for j in range(UPL)] for s in range(B)]

        block = ctx.enter_context(nc.Block())

        PAIRS = [(2, 3), (6, 7), (0, 1), (4, 5)]
        POS = {t: 2 * i + j for i, pr in enumerate(PAIRS) for j, t in enumerate(pr)}
        NUMBANK = [4, 5, 0, 1]
        KSTBANK = [7, 2, 3, 6]
        WOBANK = [6, 7]

        ORDER2 = [0, 1, 4, 5, 2, 3, 6, 7]
        HALF = [ORDER2[0:4], ORDER2[4:8]]
        X2BANK = [1, 7]
        LGBANK = [0, 6]
        CBANK = [0, 7]
        WOXBANK = [1, 5]
        OUTBANK = [4, 5]

        WALK = [(0, 7, False), (7, 15, True), (15, 22, False), (22, 30, True), (30, 2 * U, False)]

        def walk(engine, item, after):
            for n0, n1, loop in WALK:
                if not loop:
                    for n in range(n0, n1):
                        item(n, n // U, n % U, n)
                        after(n)
                else:
                    with engine.Fori(0, (n1 - n0) // UPL) as i:
                        for j in range(UPL):
                            item(UPL * i + (n0 + j), n0 // U, UPL * i + (n0 + j - U * (n0 // U)), n0 + j)

        def back(n, s, u, k):
            if isinstance(n, int):
                return n - k, (n - k) // U, (n - k) % U
            return n - k, s, u - k

        CHUNKS = [0, 2, 4, 6, 1, 3, 5, 7]

        def sbank(n):
            return n % 4 if n < 8 else n % 2

        def slot(k):
            return k // G, k % G

        @block.sync
        def _(sp):
            sp.dma_start(wA_sb[:], wA).then_inc(S["ld_wA"], 16)
            sp.dma_start(ctx_sb[:], ctxT).then_inc(S["ld_ctx"], 16)
            sp.dma_start(wv_sb[:], wv).then_inc(S["ld_wv"], 16)
            sp.dma_start(wks_sb[:], wks).then_inc(S["ld_wks"], 16)
            sp.dma_start(bqk_sb[:, 0, :], bqs).then_inc(S["ld_bias"], 16)
            sp.dma_start(bqk_sb[:, 1, :], bks).then_inc(S["ld_bias"], 16)
            for i, v in enumerate((boA, bv, boX)):
                sp.dma_start(bo_bc[:, i, :], v.partition_broadcast(P)).then_inc(S["ld_bias"], 16)
            sp.dma_start(x_sb[:], x.rearrange("b (k p) d -> p (b k) d", p=P)).then_inc(S["ld_x"], 16)
            sp.dma_start(wqs_sb[:], wqs).then_inc(S["ld_wqs"], 16)
            sp.dma_start(wo_sb[:], wo).then_inc(S["ld_wo"], 16)
            sp.dma_start(wop_sb[:], wop).then_inc(S["ld_wop"], 16)
            sp.dma_start(gate_sb[:, 0:E], gateT).then_inc(S["ld_gate"], 16)
            sp.dma_start(b1_sb[:], b1).then_inc(S["ld_small"], 16)
            sp.dma_start(mult_sb[:], mult).then_inc(S["ld_small"], 16)
            sp.dma_start(b2_sb[:], b2).then_inc(S["ld_small"], 16)
            sp.dma_start(w1_sb[:], w1T).then_inc(S["ld_w1"], 16)
            sp.dma_start(w2_sb[:], w2T).then_inc(S["ld_w2"], 16)

            sp.wait_ge(S["cT_ready"], 1)
            sp.dma_start(comb_dram[:, 0, :], combT[0:E, 0, :]).then_inc(S["comb_stored0"], 16)
            sp.wait_ge(S["pv_mm"], 8)
            for s in range(B):
                if s:
                    sp.wait_ge(S["cT_ready"], 2)
                    sp.dma_start(comb_dram[:, 1, :], combT[0:E, 1, :]).then_inc(S["comb_stored1"], 16)
                sp.wait_ge(S[f"comb_stored{s}"], 16)
                for j in range(1, UPL):
                    sp.dma_start(comb_bc[:, s, j, :], comb_dram[j - 1, s, :].partition_broadcast(P))\
                        .then_inc(slot_filled[s][j], 16)
                with sp.Fori(0, (U - 1) // UPL - 1) as i:
                    for j in range(UPL):
                        sp.wait_ge(S["gc_ready"], UPL * i + (j + 2 + U * s))
                        sp.dma_start(comb_bc[:, s, j, :], comb_dram[bass.ds(UPL * i + (UPL + j - 1), 1), s, :].partition_broadcast(P))\
                            .then_inc(slot_filled[s][j], 16)

            for i in range(4):
                sp.wait_ge(S["res_ready"], 2 * (i + 1))
                t = ORDER2[2 * i]
                sp.dma_start(out.rearrange("b (k p) d -> p (b k) d", p=P)[:, t:t + 2, :],
                             res[:, 2 * i:2 * i + 2, :]).then_inc(S["stored"], 16)
            sp.wait_ge(S["stored"], 64)

        @block.tensor
        def _(pe):
            mm = nc.tensor.matmul

            pe.wait_ge(S["ld_wA"], 16)
            pe.wait_ge(S["ld_xT0"], 16)
            for t in range(NT):
                if t == TPB:
                    pe.wait_ge(S["ld_xT1"], 16)
                i = mm(bank[t // 2][:, (t % 2) * 256:(t % 2) * 256 + 256], xT_sb[:, t * P:(t + 1) * P],
                       wA_sb[:, D:3 * D], start=True, stop=True)
                if t % 2:
                    i.then_inc(S["kv_mm"], 1)
            for b in range(B):
                mm(bank[4 + b][:], wA_sb[:, 0:D], xT_sb[:, b * N:(b + 1) * N], start=True, stop=True).then_inc(S["q_mm"], 1)
            pe.wait_ge(S["ld_ctx"], 16)
            pe.wait_ge(S["ld_wv"], 16)
            for b in range(B):
                for c, (k0, n) in enumerate(((0, P), (P, C2))):
                    i = mm(bank[6][0:n, (2 * b + c) * D:(2 * b + c + 1) * D], ctx_sb[:, b * NS + k0:b * NS + k0 + n],
                           wv_sb[:], start=True, stop=True)
            i.then_inc(S["vx_mm"], 1)

            def kstack(g):
                mm(bank[KSTBANK[g]][:, 0:B * NS], wks_sb[:, g, :], ctx_sb[:], start=True, stop=True).then_inc(S["kst_mm"], 1)

            pe.wait_ge(S["ld_wks"], 16)
            kstack(0)
            for b in range(B):
                pe.wait_ge(S["k_ready"], 2 * b + 2)
                pe.wait_ge(S["v_ready"], 2 * b + 2)
                pe.wait_ge(S["c_misc"], 1)
                for k in range(TPB):
                    i = mm(bank[b][:, 0:P + 1], ksb[:, b * TPB + k, :], vsb[:, b * TPB + k, :],
                           start=(k == 0), stop=(k == TPB - 1))
                i.then_inc(S["kvs_mm"], 1)
            kstack(1)
            kstack(2)
            def num(i):
                b = PAIRS[i][0] // TPB
                pe.wait_ge(S["q_ready"], b + 1)
                pe.wait_ge(S["bdk_ready"], b + 1)
                if i == 2:
                    pe.wait_ge(S["bdk_ready"], B)
                if i < 2:
                    pe.wait_ge(S["q_ready"], i + 1)
                for j, t in enumerate(PAIRS[i]):
                    r = mm(bank[NUMBANK[i]][:, j * 256:j * 256 + P + H], qT[:, b, (t % TPB) * P:(t % TPB + 1) * P],
                           bd[:, b, :], start=True, stop=True)
                r.then_inc(S["num_mm"], 1)

            def o_transposes(i):
                pe.wait_ge(S["o_ready"], i + 1)
                if i == 0:
                    pe.wait_ge(S["c_ident"], 1)
                    pe.wait_ge(S["kst_full"], 2)
                if i == 2:
                    pe.wait_ge(S["kst_full"], 3)
                for j in range(2):
                    c = (i % 2) * 2 + j
                    r = nc.tensor.transpose(bank[2 + i // 2][:, c * P:(c + 1) * P], osb[:, i, j, :], ident[:])
                if i % 2:
                    r.then_inc(S["oT_mm"], 1)

            def wo_a(h):
                pe.wait_ge(S["oT_ready"], h + 1)
                if h == 0:
                    pe.wait_ge(S["kst_full"], 4)
                else:
                    pe.wait_ge(S["cb_ready"], 1)
                for c in range(4):
                    r = mm(bank[WOBANK[h]][:, c * P:(c + 1) * P], oT[:, h, c, :], wA_sb[:, 3 * D:4 * D], start=True, stop=True)
                r.then_inc(S["wo_mm"], 1)

            num(0)
            num(1)
            o_transposes(0)
            pe.wait_ge(S["vx_ready"], 2)
            kstack(3)
            pe.wait_ge(S["kst_full"], 1)
            for b in range(B):
                mm(bank[7][:, b:b + 1], vx[:, b, 0, :], mcol[:], start=True, stop=False)
                i = mm(bank[7][:, b:b + 1], vx[0:C2, b, 1, :], mcol[0:C2, :], start=False, stop=True)
            i.then_inc(S["mean_mm"], 1)
            o_transposes(1)
            num(2)
            num(3)
            wo_a(0)
            o_transposes(2)
            pe.wait_ge(S["mvbc_ready"], 2 * B)
            pe.wait_ge(S["ld_wo"], 16)
            for b in range(B):
                i = mm(bank[7][:, 128 + b * P:128 + (b + 1) * P], mv_bc[:, b, :], wo_sb[:], start=True, stop=True)
            i.then_inc(S["cb_mm"], 1)
            o_transposes(3)
            wo_a(1)
            for b in range(B):
                pe.wait_ge(S["x1_ready"], 2 * b + 2)
                for j in range(2):
                    r = nc.tensor.transpose(bank[4 + b][:, j * P:(j + 1) * P], x1[:, b * TPB + 2 + j, :], ident[:])
                r.then_inc(S["x1T_mm"], 1)
            pe.wait_ge(S["x1T_ready"], B)
            pe.wait_ge(S["ld_wqs"], 16)
            pe.wait_ge(S["o_ready"], 4)
            pe.wait_ge(S["oT_ready"], 2)
            for g in range(G):
                mm(bank[g][:, 0:B * NS], wqs_sb[:, g, :], x1T[:].rearrange("p b n -> p (b n)"), start=True, stop=True)\
                    .then_inc(S["qst_mm"], 1)

            pe.wait_ge(S["qs_ready"], 2)
            pe.wait_ge(S["ks_ready"], G)
            pe.wait_ge(S["c_mask16"], 2)
            pe.wait_ge(S["c_ident16"], 1)

            def scores(n):
                b, c = n // 8, CHUNKS[n % 8]
                bk = bank[sbank(n)]
                if n in (2, 3):
                    pe.wait_ge(S["qst_full"], n + 1)
                if n == 4:
                    pe.wait_ge(S["qs_ready"], G)
                if n >= 4:
                    pe.wait_ge(S["m_ready"], 2 * (max(m for m in range(n) if sbank(m) == sbank(n)) + 1))
                q0 = b * NS
                for j in range(2):
                    v, g = slot(2 * c + j)
                    rows = slice(32 * v, 32 * v + 32)
                    mm(bk[:, j * NS:(j + 1) * NS], qs[rows, g, q0 + QB:q0 + NS], ks[rows, g, q0:q0 + NS],
                       start=(j == 0), stop=False, skip_group_check=True, tile_position=(32 * v, 0))
                for j in range(2):
                    v, g = slot(2 * c + j)
                    rows = slice(32 * v, 32 * v + 32)
                    b0 = 2 * NS + j * C2
                    mm(bk[0:QB, b0:b0 + C2], qs[rows, g, q0:q0 + QB], ks[rows, g, q0:q0 + C2],
                       start=False, stop=False, skip_group_check=True, tile_position=(32 * v, 0))
                mm(bk[0:QB, 2 * NS:2 * NS + 2 * C2].rearrange("p (h n) -> p h n", h=2), ident16[0:QB, 0:QB],
                   maskS[0:QB, 0:C2].unsqueeze(1).broadcast_to([QB, 2, C2]), start=False, stop=False, skip_group_check=True)
                mm(bk[:, 0:2 * NS].rearrange("p (h n) -> p h n", h=2)[:, :, C2:NS], ident16[:],
                   maskS[:].unsqueeze(1).broadcast_to([P, 2, P]), start=False, stop=True, skip_group_check=True)\
                    .then_inc(S["s_mm"], 1)

            def max_transposes(b):
                pe.wait_ge(S["mlo_ready"], 2 * (b + 1))
                for g in range(G):
                    o = bank[6 + g // 2][:, (g % 2) * NS:(g % 2 + 1) * NS]
                    nc.tensor.transpose(o[:, 0:QB], mmB[0:QB, g, :], ident[0:QB, 0:QB])
                    r = nc.tensor.transpose(o[:, QB:NS], mmA[:, g, :], ident[:])
                r.then_inc(S["mt_mm"], 1)

            def scores_T(n):
                b, c = divmod(n, 8)
                bk = bank[2 + n % 2]
                pe.wait_ge(S["qm_ready"], 2 * (b + 1))
                if n >= 2:
                    pe.wait_ge(S["p_ready"], 2 * (n - 1))
                q0 = b * NS
                for j in range(2):
                    v, g = slot(2 * c + j)
                    rows = slice(32 * v, 32 * v + 32)
                    mm(bk[:, j * NS:(j + 1) * NS], ks[rows, g, q0:q0 + P], qs[rows, g, q0:q0 + NS],
                       start=(j == 0), stop=False, skip_group_check=True, tile_position=(32 * v, 0))
                for j in range(2):
                    v, g = slot(2 * c + j)
                    rows = slice(32 * v, 32 * v + 32)
                    b0 = 2 * NS + j * C2
                    mm(bk[0:C2, b0:b0 + C2], ks[rows, g, q0 + P:q0 + NS], qs[rows, g, q0 + P:q0 + NS],
                       start=False, stop=False, skip_group_check=True, tile_position=(32 * v, 0))
                mm(bk[0:C2, 2 * NS:2 * NS + 2 * C2].rearrange("p (h n) -> p h n", h=2), ident16[0:C2, 0:C2],
                   maskT[0:C2, 0:C2].unsqueeze(1).broadcast_to([C2, 2, C2]), start=False, stop=False, skip_group_check=True)
                mm(bk[:, 0:2 * NS].rearrange("p (h n) -> p h n", h=2)[:, :, 0:P], ident16[:],
                   maskT[:].unsqueeze(1).broadcast_to([P, 2, P]), start=False, stop=True, skip_group_check=True)\
                    .then_inc(S["sT_mm"], 1)

            def pv(b, u):
                pe.wait_ge(S["p_ready"], 2 * (8 * b + 2 * u + 2))
                pe.wait_ge(S["va_ready"], 1 + 2 * B)
                if b == 1 and u == 0:
                    pe.wait_ge(S["oraw_ready"], 2)
                o = bank[4 + u // 2][:, (u % 2) * NS:(u % 2 + 1) * NS]
                for w in range(G):
                    k = G * u + w
                    mm(o[32 * w:32 * w + 32, :], va[:, b, 0, k, :], pT1[:, b, k, :], start=(u % 2 == 0), stop=False,
                       skip_group_check=True, tile_position=(0, 32 * w))
                for w in range(G):
                    k = G * u + w
                    r = mm(o[32 * w:32 * w + 32, P:NS], va[0:C2, b, 1, k, :], pT2[0:C2, b, k, :], start=False, stop=True,
                           skip_group_check=True, tile_position=(0, 32 * w))
                r.then_inc(S["pv_mm"], 1)

            def den_bc(b):
                pe.wait_ge(S["c_selD"], 1)
                for hf in range(2):
                    pe.wait_ge(S["oraw_ready"], 2 * b + hf + 1)
                    if b:
                        pe.wait_ge(S["rln_ready"], 2)
                    mm(bank[6 + hf][:, 0:2 * NS], selD[:], oraw[:, b, 2 * hf:2 * hf + 2, :].rearrange("p u n -> p (u n)"),
                       start=True, stop=True).then_inc(S["db_mm"], 1)

            def wo_x(b):
                pe.wait_ge(S["on_ready"], 2 * (b + 1))
                pe.wait_ge(S["ld_wop"], 16)
                pe.wait_ge(S["x2lo_ready"], 1)
                if b:
                    pe.wait_ge(S["oraw_ready"], 4)
                for j in range(2):
                    o = bank[WOXBANK[b]][:, j * P:(j + 1) * P]
                    if j == 0:
                        mm(o, mv_t2[:, b, :], wo_sb[:], start=True, stop=False)
                    for u in range(G):
                        r = mm(o, on[:, b, u, j * P:(j + 1) * P], wop_sb[:, u, :], start=(u == 0 and j == 1),
                               stop=(u == G - 1))
                r.then_inc(S["wox_mm"], 1)

            def x2_transposes(s, part):
                if s:
                    pe.wait_ge(S["rln_ready"], 4)
                for c in (2 * part, 2 * part + 1):
                    pe.wait_ge(S["x2_ready"], 4 * s + c + 1)
                    r = nc.tensor.transpose(bank[X2BANK[s]][:, c * P:(c + 1) * P], x2[:, HALF[s][c], :], ident[:])
                if part:
                    r.then_inc(S["x2T_mm"], 1)

            def router(s):
                pe.wait_ge(S["x2hi_ready"], s + 1)
                pe.wait_ge(S["x2lo_ready"], s + 1)
                pe.wait_ge(S["g_lo"], 1)
                if s:
                    pe.wait_ge(S["rln_ready"], 4)
                for c in range(TPB):
                    o = bank[LGBANK[s]][:, c * 16:(c + 1) * 16]
                    q = slice(c * P, (c + 1) * P)
                    mm(o, x2hi[:, s, q], ghi[:], start=True, stop=False)
                    mm(o, x2hi[:, s, q], glo[:], start=False, stop=False)
                    r = mm(o, x2lo[:, s, q], ghi[:], start=False, stop=True)
                r.then_inc(S["lg_mm"], 1)

            def comb_transposes(s):
                pe.wait_ge(S["comb_ready"], s + 1)
                pe.wait_ge(S["lg_ready"], s + 1)
                for c in range(TPB):
                    r = nc.tensor.transpose(bank[CBANK[s]][0:16, c * P:(c + 1) * P], comb[:, s * TPB + c, :], ident[:])
                r.then_inc(S["cT_mm"], 1)

            for n in range(9):
                scores(n)
            max_transposes(0)
            scores(9)
            for c in range(8):
                scores_T(c)
                if c < 6:
                    scores(10 + c)
                if c >= 3 and c % 2:
                    pv(0, (c - 3) // 2)
                if c == 6:
                    max_transposes(1)
                    pe.wait_ge(S["m_ready"], 32)
                    x2_transposes(0, 0)
                    x2_transposes(0, 1)
            for c in range(8):
                scores_T(8 + c)
                if c == 1:
                    pv(0, 3)
                if c == 2:
                    router(0)
                if c == 3:
                    den_bc(0)
                if c == 6:
                    comb_transposes(0)
                if c == 7:
                    wo_x(0)
                if c >= 3 and c % 2:
                    pv(1, (c - 3) // 2)
            pv(1, 3)
            den_bc(1)

            def fc1(n, s, r):
                pe.wait_ge(S["w1hi_ready"], n + 1)
                pe.wait_ge(S["w1lo_ready"], n + 1)
                pe.wait_ge(S["w1glo_ready"], n + 1)
                for part, (c, signal) in enumerate(((slice(P, 2 * P), "g_mm"), (slice(0, P), "h_mm"))):
                    bk = bank[2 * part + r % 2]
                    if r >= 2:
                        pe.wait_ge(S["gelu_done" if part == 0 else "a_ready"], n - 1)
                    mm(bk[:], w1hi[:, r % R, c], x2hi[:, s, :], start=True, stop=False)
                    mm(bk[:], w1hi[:, r % R, c], x2lo[:, s, :], start=False, stop=False)
                    mm(bk[:], w1lo[:, r % R, c], x2hi[:, s, :], start=False, stop=True).then_inc(S[signal], 1)

            def fc2(n, s, r, last=False):
                pe.wait_ge(S["w2lo_ready"], n + 1)
                pe.wait_ge(S["alo_ready"], n + 1)
                o = bank[OUTBANK[s]][:]
                mm(o, w2hi[:, r % R, :], ahi[:, r % R, :], start=False, stop=False, skip_group_check=True)
                mm(o, w2hi[:, r % R, :], alo[:, r % R, :], start=False, stop=False, skip_group_check=True)
                i = mm(o, w2lo[:, r % R, :], ahi[:, r % R, :], start=False, stop=last, skip_group_check=True)
                i.then_inc(S["fc2_mm"], 1)

            def residual(s):
                mm(bank[OUTBANK[s]][:], identr[:], x2hi[:, s, :], start=True, stop=False, skip_group_check=True)
                mm(bank[OUTBANK[s]][:], identr[:], x2lo[:, s, :], start=False, stop=False, skip_group_check=True)

            def gated_bias(s):
                pe.wait_ge(S["cT_ready"], s + 1)
                pe.wait_ge(S["ld_small"], 48)
                mm(bank[OUTBANK[s]][:], b2_sb[:], combT[:, s, :], start=False, stop=False, skip_group_check=True)

            def y_transposes(s):
                for k in range(TPB):
                    if k % 2 == 0:
                        pe.wait_ge(S[f"yT{s}_ready"], 1 + (s * k) // 2)
                    r = nc.tensor.transpose(bank[6 + s][:, k * P:(k + 1) * P], yT[:, s, k * P:(k + 1) * P], ident[:])
                r.then_inc(S["yt_mm"], 1)

            def ffn_item(n, s, u, r):
                if isinstance(n, int) and n % U == 0 and n:
                    pe.wait_ge(S["y2_ready"], 2)
                    residual(1)
                    gated_bias(1)
                fc1(n, s, r)
                if r >= LAG:
                    m, ms, _ = back(n, s, u, LAG)
                    fc2(m, ms, r - LAG, last=isinstance(m, int) and m == U - 1)

            def after_item(n):
                if n == 0:
                    wo_x(1)
                if n == 3:
                    x2_transposes(1, 0)
                    x2_transposes(1, 1)
                if n == 6:
                    router(1)
                if n == 15:
                    comb_transposes(1)
                if n == 20:
                    y_transposes(0)

            pe.wait_ge(S["c_ident16"], 2)
            residual(0)
            gated_bias(0)
            pe.wait_ge(S["cT_ready"], 1)
            pe.wait_ge(S["p_ready"], 32)
            pe.wait_ge(S["y2_ready"], 1)
            walk(pe, ffn_item, after_item)
            for m in range(2 * U - LAG, 2 * U):
                fc2(m, 1, m, last=(m == 2 * U - 1))
            y_transposes(1)

        @block.gpsimd
        def _(pool):
            pool.memset(vsb[:, :, P:P + 1], 1.0).then_inc(S["c_misc"], 1)
            pool.memset(mcol[:], 1.0 / NS).then_inc(S["c_misc"], 1)
            pool.memset(epsc[:], LNEPS).then_inc(S["c_misc"], 1)
            pool.memset(headmask[:], 1.0).then_inc(S["c_headmask"], 1)
            pool.memset(ident[:], 0.0).then_inc(S["c_zero"], 1)
            pool.wait_ge(S["c_headmask"], 1)
            hm = headmask[:].rearrange("p (h d) -> p h d", d=DH)
            pool.affine_select(out=hm, in_=hm, compare_op=ALU.is_ge, fill=0.0, base=0,
                               pattern=[[-DH, H], [0, DH]], channel_multiplier=1).then_inc(S["c_headmask"], 1)
            pool.wait_ge(S["c_headmask"], 2)
            pool.affine_select(out=hm, in_=hm, compare_op=ALU.is_ge, fill=0.0, base=DH - 1,
                               pattern=[[DH, H], [0, DH]], channel_multiplier=-1).then_inc(S["c_headmask"], 1)
            pool.wait_ge(S["c_zero"], 1)
            pool.affine_select(out=ident[:], in_=ident[:], compare_op=ALU.not_equal, fill=1.0, base=0,
                               pattern=[[-1, P]], channel_multiplier=1).then_inc(S["c_ident"], 1)
            pool.memset(mv_t2[:], 0.0).then_inc(S["c_mvt0"], 1)
            pool.wait_ge(S["ld_x"], 16)
            pool.wait_ge(S["ld_bias"], 80)
            for t0, t1 in PAIRS:
                pool.tensor_tensor(xb[:, t0:t1 + 1, :], x_sb[:, t0:t1 + 1, :],
                                   bo_bc[:, 0:1, :].broadcast_to([P, 2, D]), ALU.add).then_inc(S["xb_ready"], 1)
            pool.memset(maskf[:], 0.0).then_inc(S["c_maskf"], 1)
            pool.memset(selD[:], 0.0).then_inc(S["c_selD0"], 1)
            pool.wait_ge(S["c_maskf"], 1)
            pool.affine_select(out=maskf[:, 0, :], in_=maskf[:, 0, :], compare_op=ALU.is_ge, fill=NEG, base=0,
                               pattern=[[-1, P]], channel_multiplier=1).then_inc(S["c_maskf"], 1)
            pool.affine_select(out=maskf[:, 1, :], in_=maskf[:, 1, :], compare_op=ALU.is_ge, fill=NEG, base=0,
                               pattern=[[1, P]], channel_multiplier=-1).then_inc(S["c_maskf"], 1)
            pool.wait_ge(S["c_selD0"], 1)
            sd = selD[:].rearrange("p (w c) -> p w c", c=32)
            pool.affine_select(out=sd, in_=sd, compare_op=ALU.not_equal, fill=1.0, base=-DH,
                               pattern=[[-32, G], [0, 32]], channel_multiplier=1).then_inc(S["c_selD"], 1)
            pool.memset(mmA[:], 0.0).then_inc(S["c_mm0"], 1)
            pool.memset(mmB[:], 0.0).then_inc(S["c_mm0"], 1)
            pool.memset(va[:], 0.0).then_inc(S["c_va0"], 1)
            pool.wait_ge(S["c_va0"], 1)
            pool.memset(va[:, :, :, :, DH:DH + 1], 1.0).then_inc(S["va_ready"], 1)
            pool.wait_ge(S["vx_ready"], 2)
            for b in range(B):
                for c, n in enumerate((P, C2)):
                    pool.tensor_copy(va[0:n, b, c, :, 0:DH].rearrange("p (v g) d -> p v g d", v=G),
                                     vx[0:n, b, c, :].rearrange("p (g v d) -> p v g d", g=G, v=G))\
                    .then_inc(S["va_ready"], 1)
            for g in range(G):
                pool.wait_ge(S["kst_full"], g + 1)
                pool.wait_ge(S["lomask_ready"], 2)
                pool.tensor_scalar(hisk[:, g, :], fullk[:, g, :], lomask[:, 1:2], None, ALU.mult).then_inc(S["kst_his"], 1)
                pool.wait_ge(S["kst_his"], g + 1)
                pool.tensor_tensor(ks[:, g, :], fullk[:, g, :], hisk[:, g, :].bitcast(F32), ALU.subtract)\
                    .then_inc(S["ks_ready"], 1)
            pool.memset(on[:], 0.0).then_inc(S["c_on0"], 1)
            pool.memset(gate_sb[:, E:16], 0.0).then_inc(S["c_gate0"], 1)
            pool.memset(lg[:], PAD).then_inc(S["c_lg0"], 1)
            pool.memset(vals[:], PAD).then_inc(S["c_lg0"], 1)
            pool.memset(comb[:, :, E:16], 1.0).then_inc(S["c_comb0"], 1)

            for t in (0, 1, 4, 5):
                pool.wait_ge(S["cb_ready"], 1)
                pool.wait_ge(S["x1_ready"], POS[t] + 1)
                pool.tensor_tensor(y2[:, t, :], x1[:, t, :], cb[:, t // TPB, :], ALU.add).then_inc(S["y2a_ready"], 1)
            for n, t in enumerate((2, 3, 6, 7)):
                pool.wait_ge(S["x1_ready"], POS[t] + 1)
                pool.tensor_tensor(x1b[:, t, :], x1[:, t, :], bo_bc[:, 2, :], ALU.add).then_inc(S["x1b_ready"], 1)

            def w1lo_stage(n, u, r):
                pool.wait_ge(S["w1hi_ready"], n + 1)
                pool.tensor_tensor(w1lo[:, r % R, 0:WSPLIT], w1_sb[:, bass.ds(u, 1), 0:WSPLIT].rearrange("p a n -> p (a n)"),
                                   w1hi[:, r % R, 0:WSPLIT].bitcast(F32), ALU.subtract).then_inc(S["w1lo_ready"], 1)

            pool.wait_ge(S["ld_w1"], 16)
            for n in range(R):
                w1lo_stage(n, n, n)
            pool.wait_ge(S["pv_mm"], 8)
            for s in range(B):
                pool.memset(comb_bc[:, s, 0, :], 1.0).then_inc(slot_filled[s][0], 16)

            def pool_item(n, s, u, r):
                pool.wait_ge(S["gelu_done"], n + 1)
                if isinstance(n, int):
                    j, fill = (u - 1) % UPL * (u > 0), (u - 1) // UPL * (u > 0)
                    pool.wait_ge(slot_filled[s][j], 16 * (fill + 1))
                else:
                    j = (r - U * s - 1) % UPL
                    pool.wait_ge(slot_filled[s][j], 4 * u - 4 * (j + 1) + 16)
                pool.tensor_tensor(gl[:, r % 2, :], gl[:, r % 2, :], comb_bc[:, s, j, :], ALU.mult).then_inc(S["gc_ready"], 1)
                if r >= 2 and (not isinstance(n, int) or n + 2 < 2 * U):
                    m, _, mu = back(n, s, u, -2)
                    w1lo_stage(m, mu, r + 2)

            walk(pool, pool_item, lambda n: None)

        @block.vector
        def _(dve):
            sub_, add_, mul_ = ALU.subtract, ALU.add, ALU.mult
            for i in range(4):
                dve.wait_ge(S["ek_done"], i + 1)
                dve.tensor_scalar(ek[:, i, :, :], ek[:, i, :, :], 1.0, None, ALU.min).then_inc(S["ekmin_done"], 1)
                dve.wait_ge(S["ekmin_done"], i + 1)
                dve.wait_ge(S["v_ready"], i + 1)
                dve.scalar_tensor_tensor(out=ksb[:, 2 * i:2 * i + 2, :],
                                         in0=bank[i][:].rearrange("p (t n) -> p t n", t=2)[:, :, 0:P], scalar=0.0,
                                         in1=ek[:, i, :, :], op0=ALU.max, op1=add_).then_inc(S["k_ready"], 1)
            for b in range(B):
                dve.wait_ge(S["eq_done"], b + 1)
                dve.tensor_scalar(eq[:, b, :], eq[:, b, :], 1.0, None, ALU.min).then_inc(S["eqmin_done"], 1)
                dve.wait_ge(S["eqmin_done"], b + 1)
                dve.scalar_tensor_tensor(out=qT[:, b, :], in0=bank[4 + b][:], scalar=0.0, in1=eq[:, b, :],
                                         op0=ALU.max, op1=add_).then_inc(S["q_ready"], 1)
            dve.wait_ge(S["c_headmask"], 3)
            for b in range(B):
                dve.wait_ge(S["kvs_mm"], b + 1)
                dve.tensor_tensor(bd[:, b, 0:P], bank[b][:, 0:P], headmask[:], mul_).then_inc(S["bd_ready"], 1)
                dve.tensor_scalar(bd[:, b, P:P + H], headmask[:, 0:P:DH], bank[b][:, P:P + 1], None, mul_)\
                    .then_inc(S["bdk_ready"], 1)
            dve.wait_ge(S["vx_mm"], 1)
            dve.wait_ge(S["ld_bias"], 80)
            v6 = bank[6][:].rearrange("p (b c d) -> p b c d", b=B, c=2)
            for c, n in enumerate((P, C2)):
                dve.tensor_tensor(vx[0:n, :, c, :], v6[0:n, :, c, :], bo_bc[0:n, 1:2, :].broadcast_to([n, B, D]), add_)\
                    .then_inc(S["vx_ready"], 1)
            hw = headmask[:].rearrange("p (w c d) -> p w c d", w=G, c=4)
            dve.tensor_reduce(lomask[:, 0:1], hw[:, :, 2:4, 0], AX.XY, add_).then_inc(S["lomask_ready"], 1)
            dve.tensor_reduce(lomask[:, 1:2], hw[:, :, 1, 0], AX.X, add_).then_inc(S["lomask_ready"], 1)

            def normalise(i):
                dve.wait_ge(S["num_mm"], i + 1)
                o = bank[NUMBANK[i]][:].rearrange("p (t n) -> p t n", t=2)
                dve.tensor_scalar(rden[:, i, :, :], o[:, :, P:P + H], EPS, None, add_).then_inc(S["den_ready"], 1)
                dve.wait_ge(S["den_ready"], i + 1)
                dve.reciprocal(rden[:, i, :, :], rden[:, i, :, :]).then_inc(S["rden_ready"], 1)
                dve.wait_ge(S["rden_ready"], i + 1)
                dve.tensor_tensor(osb[:, i, :, :].rearrange("p t (h d) -> p t h d", h=H),
                                  o[:, :, 0:P].rearrange("p t (h d) -> p t h d", h=H),
                                  rden[:, i, :, :].unsqueeze(3).broadcast_to([P, 2, H, DH]), mul_).then_inc(S["o_ready"], 1)

            normalise(0)
            normalise(1)
            normalise(2)
            normalise(3)

            def stats(src, st_, mv_, tiles, n0, s_st, s_mv):
                for t in tiles:
                    dve.bn_stats(st_[:, t, :], src(t)).then_inc(S[s_st], 1)
                for n, t in enumerate(tiles):
                    dve.wait_ge(S[s_st], n0 + n + 1)
                    dve.bn_aggr(mv_[:, t, :], st_[:, t, :]).then_inc(S[s_mv], 1)

            def apply(dst, src, mv_, rs, tiles, signal):
                for t in tiles:
                    dve.tensor_scalar(dst[:, t, :], src(t), mv_[:, t, 0:1], rs[:, t:t + 1], sub_, mul_).then_inc(S[signal], 1)

            def first_norm(h):
                dve.wait_ge(S["wo_mm"], h + 1)
                for q in range(2):
                    i = 2 * h + q
                    t = PAIRS[i][0]
                    dve.wait_ge(S["xb_ready"], i + 1)
                    dve.tensor_tensor(y[:, t:t + 2, :], bank[WOBANK[h]][:, q * 256:(q + 1) * 256].rearrange("p (t d) -> p t d", t=2),
                                      xb[:, t:t + 2, :], add_).then_inc(S["y_ready"], 1)
                dve.wait_ge(S["y_ready"], 2 * h + 2)
                stats(lambda t: y[:, t, :], st, mv, PAIRS[2 * h] + PAIRS[2 * h + 1], 4 * h, "st_done", "mv_ready")

            def first_apply(h):
                dve.wait_ge(S["rstd_ready"], h + 1)
                apply(x1, lambda t: y[:, t, :], mv, rstd, PAIRS[2 * h] + PAIRS[2 * h + 1], "x1_ready")

            first_norm(0)
            dve.wait_ge(S["cb_mm"], 1)
            dve.tensor_tensor(cb[:], bank[7][:, P:P + B * D].rearrange("p (b d) -> p b d", b=B),
                              bo_bc[:, 2:3, :].broadcast_to([P, B, D]), add_).then_inc(S["cb_ready"], 1)
            first_apply(0)
            first_norm(1)
            dve.wait_ge(S["c_ident"], 1)
            dve.wait_ge(S["c_maskf"], 3)
            dve.tensor_copy(ident16[:], ident[:]).then_inc(S["c_ident16"], 1)
            dve.tensor_copy(maskS[:], maskf[:, 0, :]).then_inc(S["c_mask16"], 1)
            dve.tensor_copy(maskT[:], maskf[:, 1, :]).then_inc(S["c_mask16"], 1)
            dve.wait_ge(S["ks_ready"], G)
            for g in range(G + 1):
                if g < G:
                    dve.wait_ge(S["qst_mm"], g + 1)
                    dve.tensor_scalar(fullq[:, g, :], bank[g][:, 0:B * NS], bqk_sb[:, 0, g:g + 1], SCALE, add_, mul_)\
                        .then_inc(S["qst_full"], 1)
                if g:
                    dve.wait_ge(S["qst_his"], g)
                    dve.tensor_tensor(qs[:, g - 1, :], fullq[:, g - 1, :], hisq[:, g - 1, :].bitcast(F32), sub_).then_inc(S["qs_ready"], 1)

            def maxima(n):
                b, c = n // 8, CHUNKS[n % 8]
                bk = bank[sbank(n)]
                dve.wait_ge(S["s_mm"], n + 1)
                dve.tensor_reduce(mA[:, b, 2 * c:2 * c + 2], bk[:, 0:2 * NS].rearrange("p (h n) -> p h n", h=2), AX.X, ALU.max)\
                    .then_inc(S["m_ready"], 1)
                dve.tensor_reduce(mB[0:QB, b, 2 * c:2 * c + 2], bk[0:QB, 2 * NS:2 * NS + 2 * C2].rearrange("p (h n) -> p h n", h=2),
                                  AX.X, ALU.max).then_inc(S["m_ready"], 1)

            def maxima_split(b, part):
                if part:
                    dve.wait_ge(S["mt_mm"], b + 1)
                    for hf in range(2):
                        q = qs[:, 2 * hf:2 * hf + 2, b * NS:(b + 1) * NS]
                        dve.tensor_tensor(q, bank[6 + hf][:, 0:2 * NS].rearrange("p (g n) -> p g n", g=2), q.bitcast(F32), add_)\
                            .then_inc(S["qm_ready"], 1)
                    return
                dve.wait_ge(S["m_ready"], 16 * (b + 1))
                dve.wait_ge(S["c_mm0"], 2)
                if b:
                    dve.wait_ge(S["mt_mm"], 1)
                views = [(t[0:r].rearrange("p g (v c) -> p g v c", v=G), m[0:r, b, :].rearrange("p (v g) -> p g v", v=G))
                         for t, m, r in ((mmA, mA, P), (mmB, mB, QB))]
                for to, m in views:
                    dve.tensor_scalar(to[:, :, :, 3 * DH].bitcast(F32R), m, -1.0, None, mul_).then_inc(S["mhi_ready"], 1)
                for n, (to, m) in enumerate(views):
                    dve.wait_ge(S["mhi_ready"], 2 * b + n + 1)
                    dve.scalar_tensor_tensor(out=to[:, :, :, 3 * DH + 1], in0=m, scalar=-1.0, in1=to[:, :, :, 3 * DH],
                                             op0=mul_, op1=sub_).then_inc(S["mlo_ready"], 1)

            def second_norm(tiles, n0):
                stats(lambda t: y2[:, t, :], st2, mv2, tiles, n0, "st2_done", "mv2_ready")

            def second_apply(tiles, n):
                dve.wait_ge(S["rstd2_ready"], n)
                apply(x2, lambda t: y2[:, t, :], mv2, rstd2, tiles, "x2_ready")

            def w1glo_stage(n, u, r):
                dve.wait_ge(S["w1hi_ready"], n + 1)
                dve.tensor_tensor(w1lo[:, r % R, WSPLIT:], w1_sb[:, bass.ds(u, 1), WSPLIT:].rearrange("p a n -> p (a n)"),
                                  w1hi[:, r % R, WSPLIT:].bitcast(F32), sub_).then_inc(S["w1glo_ready"], 1)

            def b1g_stage(n, u, r):
                dve.tensor_copy(b1g[:, r % R:r % R + 1], b1_sb[:, bass.ds(u, 1), 1:2].rearrange("p a b -> p (a b)"))\
                    .then_inc(S["b1g_ready"], 1)

            def w2lo_stage(n, u, r):
                dve.wait_ge(S["w2hi_ready"], n + 1)
                dve.scalar_tensor_tensor(out=w2lo[:, r % R, :], in0=w2_sb[:, bass.ds(u, 1), :].rearrange("p a n -> p (a n)"),
                                         scalar=mult_sb[:, bass.ds(u, 1)], in1=w2hi[:, r % R, :].bitcast(F32), op0=mul_, op1=sub_)\
                    .then_inc(S["w2lo_ready"], 1)

            def o_normalise(b):
                dve.wait_ge(S["c_on0"], 1)
                for hf in range(2):
                    dve.wait_ge(S["rdx_ready"], 2 * b + hf + 1)
                    dve.tensor_tensor(on[:, b, 2 * hf:2 * hf + 2, QB0:2 * P], oraw[:, b, 2 * hf:2 * hf + 2, :],
                                      rdx[:, b, 2 * hf:2 * hf + 2, :], mul_).then_inc(S["on_ready"], 1)

            def attended(b):
                dve.wait_ge(S["wox_mm"], b + 1)
                dve.wait_ge(S["x1b_ready"], 2 * b + 2)
                t = b * TPB + 2
                dve.tensor_tensor(y2[:, t:t + 2, :], bank[WOXBANK[b]][:, 0:2 * P].rearrange("p (t d) -> p t d", t=2), x1b[:, t:t + 2, :], add_)\
                    .then_inc(S["y2_ready"], 1)
                dve.wait_ge(S["y2_ready"], b + 1)
                second_norm((t, t + 1), 4 + 2 * b)

            def x2_split(b):
                dve.wait_ge(S["x2hi_ready"], b + 1)
                dve.tensor_tensor(x2lo[:, b, :], bank[X2BANK[b]][:], x2hi[:, b, :].bitcast(F32), sub_).then_inc(S["x2lo_ready"], 1)

            def gates_logits(b):
                T = slice(b * TPB, (b + 1) * TPB)
                dve.wait_ge(S["lg_mm"], b + 1)
                dve.wait_ge(S["c_lg0"], 2)
                dve.tensor_copy(lg[:, T, 0:E], bank[LGBANK[b]][:, 0:TPB * 16].rearrange("p (t e) -> p t e", e=16)[:, :, 0:E])\
                    .then_inc(S["lg_ready"], 1)

            def gates(b):
                T = slice(b * TPB, (b + 1) * TPB)
                dve.wait_ge(S["lg_ready"], b + 1)
                for t in range(b * TPB, (b + 1) * TPB):
                    dve.max(top[:, t, :], lg[:, t, 0:E]).then_inc(S["top_ready"], 1)
                dve.wait_ge(S["top_ready"], TPB * (b + 1))
                dve.tensor_copy(vals[:, T, 0:3], top[:, T, 0:3]).then_inc(S["vals_ready"], 1)
                dve.tensor_tensor(dl[:, T, :], lg[:, T, 0:E], top[:, T, 0:1].broadcast_to([P, TPB, E]), sub_).then_inc(S["dl_ready"], 1)
                dve.wait_ge(S["vals_ready"], b + 1)
                for t in range(b * TPB, (b + 1) * TPB):
                    dve.match_replace(rep[:, t, :], vals[:, t, :], lg[:, t, :], PAD).then_inc(S["rep_ready"], 1)
                dve.wait_ge(S["rep_ready"], TPB * (b + 1))
                dve.tensor_tensor(sel[:, T, :], rep[:, T, 0:E], lg[:, T, 0:E], ALU.not_equal).then_inc(S["sel_ready"], 1)
                dve.wait_ge(S["el_ready"], b + 1)
                dve.wait_ge(S["sel_ready"], b + 1)
                dve.tensor_tensor(em[:, T, :], el[:, T, :], sel[:, T, :], mul_).then_inc(S["em_ready"], 1)
                dve.tensor_reduce(zs[:, T], el[:, T, :], AX.X, add_).then_inc(S["zs_ready"], 1)
                dve.wait_ge(S["em_ready"], b + 1)
                dve.tensor_reduce(s3[:, T], em[:, T, :], AX.X, add_).then_inc(S["s3_ready"], 1)
                dve.wait_ge(S["s3_ready"], b + 1)
                dve.wait_ge(S["zs_ready"], b + 1)
                dve.scalar_tensor_tensor(out=dn[:, T], in0=zs[:, T], scalar=1e-20, in1=s3[:, T], op0=mul_, op1=add_)\
                    .then_inc(S["dn_ready"], 1)
                dve.wait_ge(S["dn_ready"], b + 1)
                dve.reciprocal(rd[:, T], dn[:, T]).then_inc(S["rd_ready"], 1)
                dve.wait_ge(S["rd_ready"], b + 1)
                dve.wait_ge(S["c_comb0"], 1)
                dve.tensor_tensor(comb[:, T, 0:E], em[:, T, :], rd[:, T].unsqueeze(2).broadcast_to([P, TPB, E]), mul_)\
                    .then_inc(S["comb_ready"], 1)

            for n in range(8):
                maxima(n)
                if n == 4:
                    dve.wait_ge(S["ld_gate"], 16)
                    dve.wait_ge(S["c_gate0"], 1)
                    dve.tensor_copy(ghi[:], gate_sb[:]).then_inc(S["g_hi"], 1)
                    dve.wait_ge(S["g_hi"], 1)
                    dve.tensor_tensor(glo[:], gate_sb[:], ghi[:].bitcast(F32), sub_).then_inc(S["g_lo"], 1)
                    dve.tensor_copy(identr[:], ident[:]).then_inc(S["c_ident16"], 1)
            maxima_split(0, 0)
            maxima(8)
            first_apply(1)
            maxima_split(0, 1)
            for n in range(9, 16):
                maxima(n)
                if n == 11:
                    dve.wait_ge(S["y2a_ready"], 4)
                    second_norm((0, 1, 4, 5), 0)
                if n == 12:
                    second_apply((0, 1, 4, 5), 1)
            maxima_split(1, 0)
            maxima_split(1, 1)
            x2_split(0)
            dve.wait_ge(S["ld_small"], 48)
            dve.wait_ge(S["ld_w1"], 16)
            dve.wait_ge(S["ld_w2"], 16)
            b1g_stage(0, 0, 0)
            b1g_stage(1, 1, 1)
            for n in range(R):
                w1glo_stage(n, n, n)
                w2lo_stage(n, n, n)
            gates_logits(0)
            gates(0)
            o_normalise(0)
            attended(0)
            second_apply((2, 3), 2)
            o_normalise(1)

            def act_product(n, u, r):
                dve.wait_ge(S["gc_ready"], n + 1)
                dve.wait_ge(S["h_mm"], n + 1)
                if r >= 2:
                    dve.wait_ge(S["alo_ready"], n - 1)
                dve.scalar_tensor_tensor(out=a[:, r % 2, :], in0=bank[2 + r % 2][:],
                                         scalar=b1_sb[:, bass.ds(u, 1), 0:1].rearrange("p a b -> p (a b)"),
                                         in1=gl[:, r % 2, :], op0=add_, op1=mul_).then_inc(S["a_ready"], 1)

            def act_lo(n, r):
                dve.wait_ge(S["ahi_ready"], n + 1)
                dve.tensor_tensor(alo[:, r % R, :], a[:, r % 2, :], ahi[:, r % R, :].bitcast(F32), sub_)\
                    .then_inc(S["alo_ready"], 1)

            def dve_item(n, s, u, r):
                static = isinstance(n, int)
                if r >= 1:
                    m, _, mu = back(n, s, u, 1)
                    act_product(m, mu, r - 1)
                if r >= 2:
                    m, _, mu = back(n, s, u, 2)
                    act_lo(m, r - 2)
                if r >= 2:
                    m, _, mu = back(n, s, u, 2)
                    if r - 2 >= R:
                        w2lo_stage(m, mu, r - 2)
                    if not static or n + 2 < 2 * U:
                        m, _, mu = back(n, s, u, -2)
                        w1glo_stage(m, mu, r + 2)
                        dve.wait_ge(S["gelu_done"], n - 1)
                if not static or n + 2 < 2 * U:
                    m, _, mu = back(n, s, u, -2)
                    b1g_stage(m, mu, r + 2)

            def third_norm(b):
                dve.wait_ge(S["yt_mm"], b + 1)
                T = range(b * TPB, (b + 1) * TPB)
                src = lambda t: bank[6 + t // TPB][:, (t % TPB) * P:(t % TPB + 1) * P]
                stats(src, st3, mv3, T, 4 * b, "st3_done", "mv3_ready")

            def third_apply(b):
                T = range(b * TPB, (b + 1) * TPB)
                src = lambda t: bank[6 + t // TPB][:, (t % TPB) * P:(t % TPB + 1) * P]
                dve.wait_ge(S["rstd3_ready"], b + 1)
                apply(res, src, mv3, rstd3, T, "res_ready")


            def after_item(n):
                if n == 1:
                    attended(1)
                if n == 2:
                    second_apply((6, 7), 3)
                if n == 3:
                    x2_split(1)
                if n == 6:
                    gates_logits(1)
                    gates(1)
                if n == 21:
                    third_norm(0)

            walk(dve, dve_item, after_item)
            n = 2 * U - 1
            act_lo(n - 1, n - 1)
            act_product(n, U - 1, n)
            w2lo_stage(n - 1, U - 2, n - 1)
            w2lo_stage(n, U - 1, n)
            act_lo(n, n)
            third_apply(0)
            third_norm(1)
            third_apply(1)

        @block.scalar
        def _(act):
            def A(out, in_, f, **kw):
                return nc.scalar.activation(out, in_, f, **kw)

            for b in range(B):
                act.dma_start(xT_sb[:, b * N:(b + 1) * N], xT[:, b * N:(b + 1) * N]).then_inc(S[f"ld_xT{b}"], 16)
            act.preload_act_table_set("natural_log_exp_and_others")
            for i in range(4):
                o = bank[i][:].rearrange("p (t n) -> p t n", t=2)
                act.wait_ge(S["kv_mm"], i + 1)
                A(ek[:, i, :, :], o[:, :, 0:P], ACT.Exp).then_inc(S["ek_done"], 1)
                A(vsb[:, 2 * i:2 * i + 2, 0:P], o[:, :, P:2 * P], ACT.Copy).then_inc(S["v_ready"], 1)
            for b in range(B):
                act.wait_ge(S["q_mm"], b + 1)
                A(eq[:, b, :], bank[4 + b][:], ACT.Exp).then_inc(S["eq_done"], 1)

            def rsqrt(mv_view, ln_view, rs_view, n, names):
                act.wait_ge(S["c_misc"], 3)
                A(ln_view, mv_view, ACT.Ln, bias=epsc[:, 0:1]).then_inc(S[names[0]], 1)
                act.wait_ge(S[names[0]], n)
                A(rs_view, ln_view, ACT.Exp, scale=-0.5).then_inc(S[names[1]], 1)

            def tiles_of(tensor, k0):
                return tensor[:].rearrange("p (b k) -> p b k", b=B)[:, :, k0:k0 + 2]

            def var_of(tensor, k0):
                return tensor[:].rearrange("p (b k) s -> p b k s", b=B)[:, :, k0:k0 + 2, 1]

            act.wait_ge(S["ld_bias"], 80)
            for g in range(G):
                act.wait_ge(S["kst_mm"], g + 1)
                A(fullk[:, g, :], bank[KSTBANK[g]][:, 0:B * NS], ACT.Identity, bias=bqk_sb[:, 1, g:g + 1]).then_inc(S["kst_full"], 1)
            for h in range(2):
                act.wait_ge(S["oT_mm"], h + 1)
                A(oT[:, h, :, :].rearrange("p c n -> p (c n)"), bank[2 + h][:], ACT.Copy).then_inc(S["oT_ready"], 1)
                if h == 0:
                    act.wait_ge(S["mean_mm"], 1)
                    act.wait_ge(S["c_mvt0"], 1)
                    for b in range(B):
                        A(mv_bc[:, b, :], bank[7][:, b:b + 1].broadcast_to([P, P]), ACT.Copy).then_inc(S["mvbc_ready"], 1)
                        A(mv_t2[:, b, 0:QB0], bank[7][:, b:b + 1].broadcast_to([P, QB0]), ACT.Copy).then_inc(S["mvbc_ready"], 1)
            act.wait_ge(S["mv_ready"], 4)
            rsqrt(var_of(mv, 2), tiles_of(lnv, 2), tiles_of(rstd, 2), 1, ("lnv_done", "rstd_ready"))
            for b in range(B):
                act.wait_ge(S["x1T_mm"], b + 1)
                A(x1T[:, b, :], bank[4 + b][:, QB0:2 * P], ACT.Copy).then_inc(S["x1T_ready"], 1)
            act.wait_ge(S["mv_ready"], 8)
            rsqrt(var_of(mv, 0), tiles_of(lnv, 0), tiles_of(rstd, 0), 2, ("lnv_done", "rstd_ready"))
            act.wait_ge(S["lomask_ready"], 2)
            for g in range(G):
                act.wait_ge(S["qst_full"], g + 1)
                A(hisq[:, g, :], fullq[:, g, :], ACT.Copy, scale=lomask[:, 0:1]).then_inc(S["qst_his"], 1)

            def probabilities(n):
                b, c = divmod(n, 8)
                bk = bank[2 + n % 2]
                act.wait_ge(S["sT_mm"], n + 1)
                A(pT1[:, b, 2 * c:2 * c + 2, :], bk[:, 0:2 * NS].rearrange("p (h n) -> p h n", h=2), ACT.Exp).then_inc(S["p_ready"], 1)
                A(pT2[0:C2, b, 2 * c:2 * c + 2, :], bk[0:C2, 2 * NS:2 * NS + 2 * C2].rearrange("p (h n) -> p h n", h=2), ACT.Exp)\
                    .then_inc(S["p_ready"], 1)

            def o_copy(b, hf):
                act.wait_ge(S["pv_mm"], 4 * b + 2 * hf + 2)
                A(oraw[:, b, 2 * hf:2 * hf + 2, :], bank[4 + hf][:, 0:2 * NS].rearrange("p (u n) -> p u n", u=2), ACT.Copy)\
                    .then_inc(S["oraw_ready"], 1)

            def attended_rsqrt(b):
                t = slice(b * TPB + 2, b * TPB + 4)
                act.wait_ge(S["mv2_ready"], 6 + 2 * b)
                rsqrt(mv2[:, t, 1], lnv2[:, t], rstd2[:, t], 2 + b, ("lnv2_done", "rstd2_ready"))

            def x2_hi(b):
                act.wait_ge(S["x2T_mm"], b + 1)
                A(x2hi[:, b, :], bank[X2BANK[b]][:], ACT.Copy).then_inc(S["x2hi_ready"], 1)

            def gate_exp(b):
                T = slice(b * TPB, (b + 1) * TPB)
                act.wait_ge(S["dl_ready"], b + 1)
                A(el[:, T, :], dl[:, T, :], ACT.Exp).then_inc(S["el_ready"], 1)

            def comb_copy(s):
                act.wait_ge(S["cT_mm"], s + 1)
                A(combT[:, s, :], bank[CBANK[s]][0:16, :], ACT.Copy).then_inc(S["cT_ready"], 1)

            def den_inverse(b):
                for hf in range(2):
                    act.wait_ge(S["db_mm"], 2 * b + hf + 1)
                    if b == 0:
                        act.wait_ge(S["qs_ready"], G)
                    A(rdx[:, b, 2 * hf:2 * hf + 2, :], bank[6 + hf][:, 0:2 * NS].rearrange("p (u n) -> p u n", u=2), ACT.Ln)\
                        .then_inc(S["rln_ready"], 1)
                for hf in range(2):
                    act.wait_ge(S["rln_ready"], 2 * b + hf + 1)
                    A(rdx[:, b, 2 * hf:2 * hf + 2, :], rdx[:, b, 2 * hf:2 * hf + 2, :], ACT.Exp, scale=-1.0)\
                        .then_inc(S["rdx_ready"], 1)

            def w1hi_stage(u, r):
                A(w1hi[:, r % R, :], w1_sb[:, bass.ds(u, 1), :].rearrange("p a n -> p (a n)"), ACT.Copy).then_inc(S["w1hi_ready"], 1)

            def w2hi_stage(u, r):
                A(w2hi[:, r % R, :], w2_sb[:, bass.ds(u, 1), :].rearrange("p a n -> p (a n)"), ACT.Copy,
                  scale=mult_sb[:, bass.ds(u, 1)]).then_inc(S["w2hi_ready"], 1)

            for n in range(16):
                probabilities(n)
                if n == 1:
                    act.wait_ge(S["mv2_ready"], 4)
                    rsqrt(var_of(mv2, 0), tiles_of(lnv2, 0), tiles_of(rstd2, 0), 1, ("lnv2_done", "rstd2_ready"))
                if n == 6:
                    x2_hi(0)
                if n == 11:
                    gate_exp(0)
                if n == 14:
                    comb_copy(0)
                if n == 7:
                    o_copy(0, 0)
                if 5 <= n < 5 + R:
                    act.wait_ge(S["ld_w1"], 16)
                    act.wait_ge(S["ld_w2"], 16)
                    act.wait_ge(S["ld_small"], 48)
                    w1hi_stage(n - 5, n - 5)
                    w2hi_stage(n - 5, n - 5)
                if n == 9:
                    o_copy(0, 1)
                if n == 11:
                    den_inverse(0)
            o_copy(1, 0)
            o_copy(1, 1)
            attended_rsqrt(0)
            den_inverse(1)

            def gelu(n, r):
                act.wait_ge(S["g_mm"], n + 1)
                act.wait_ge(S["b1g_ready"], n + 1)
                A(gl[:, r % 2, :], bank[r % 2][:], ACT.Gelu, bias=b1g[:, r % R:r % R + 1]).then_inc(S["gelu_done"], 1)

            def act_hi(n, r):
                act.wait_ge(S["a_ready"], n + 1)
                if r >= R:
                    act.wait_ge(S["fc2_mm"], n - R + 1)
                A(ahi[:, r % R, :], a[:, r % 2, :], ACT.Copy).then_inc(S["ahi_ready"], 1)

            def act_item(n, s, u, r):
                if r >= 2:
                    m, _, mu = back(n, s, u, 2)
                    act_hi(m, r - 2)
                    if r - 2 >= R:
                        w2hi_stage(mu, r - 2)
                gelu(n, r)
                if r >= 2 and (not isinstance(n, int) or n + 2 < 2 * U):
                    _, _, mu = back(n, s, u, -2)
                    w1hi_stage(mu, r + 2)

            def yT_copy():
                act.wait_ge(S["fc2_mm"], U)
                A(yT[:, 0, :], bank[OUTBANK[0]][:], ACT.Copy).then_inc(S["yT0_ready"], 1)

            def third_rsqrt(b):
                t = slice(b * TPB, (b + 1) * TPB)
                act.wait_ge(S["mv3_ready"], 4 * b + 4)
                rsqrt(mv3[:, t, 1], lnv3[:, t], rstd3[:, t], b + 1, ("lnv3_done", "rstd3_ready"))

            def after_item(n):
                if n == 2:
                    act.preload_act_table_set("natural_log_exp_and_others")
                    attended_rsqrt(1)
                    act.preload_act_table_set("gelu_and_others")
                if n == 3:
                    x2_hi(1)
                if n == 6:
                    act.preload_act_table_set("natural_log_exp_and_others")
                    gate_exp(1)
                    act.preload_act_table_set("gelu_and_others")
                if n == 15:
                    comb_copy(1)
                if n == 20:
                    yT_copy()

            act.preload_act_table_set("gelu_and_others")
            walk(act, act_item, after_item)
            m = 2 * U - 1
            act_hi(m - 1, m - 1)
            w2hi_stage(U - 2, m - 1)
            w2hi_stage(U - 1, m)
            act.preload_act_table_set("natural_log_exp_and_others")
            act_hi(m, m)
            third_rsqrt(0)
            act.wait_ge(S["fc2_mm"], 2 * U)
            for hf in (slice(0, 2 * P), slice(2 * P, N)):
                A(yT[:, 1, hf], bank[OUTBANK[1]][:, hf], ACT.Copy).then_inc(S["yT1_ready"], 1)
            third_rsqrt(1)


def kernel(**inputs):
    import numpy as np
    import concourse.bacc as bacc
    from concourse.bass_utils import run_bass_kernel_spmd as run

    I = {k: np.asarray(v) for k, v in inputs.items()}
    c = np.ascontiguousarray

    def stacked(w, last):
        w = w.reshape(w.shape[:-1] + (G, G, 1, DH))
        w = np.concatenate([w, w, w, np.broadcast_to(np.asarray(last, w.dtype), w.shape)], axis=-2)
        return w.reshape(w.shape[:-4] + (G, P))

    none, ones = np.zeros(DH), np.arange(DH) < 2
    wq, wk = I["L0_xattn_Wq"], I["L0_xattn_Wk"]
    wo = I["L0_xattn_Wo"]
    wop = np.zeros((G, 32, G, D), wo.dtype)
    wop[:, 0:DH, :, :] = wo.reshape(G, G, DH, D).transpose(0, 2, 1, 3)
    f1, s1 = I["L0_ffn_fc1_w"], I["L0_ffn_s_fc1_w"]
    s1 = s1.reshape(2, 2, P, D).transpose(1, 0, 2, 3).reshape(2, 2 * P, D)
    sb1 = I["L0_ffn_s_fc1_b"].reshape(2, 2, P).transpose(1, 0, 2)
    f2, s2 = I["L0_ffn_fc2_w"], I["L0_ffn_s_fc2_w"]
    s2 = s2.reshape(D, 2, P).transpose(1, 0, 2)
    arrays = {
        "x": c(I["x"]),
        "xT": c(I["x"].transpose(2, 0, 1).reshape(D, B * N)),
        "ctxT": c(I["ctx_1024"].transpose(2, 0, 1).reshape(D, B * NS)),
        "wA": c(np.concatenate([I["L0_attn_W" + n].T for n in "qkvo"], axis=1)),
        "boA": c(I["L0_attn_bo"]),
        "wqs": c(stacked(wq, none)),
        "wks": c(stacked(wk, none)),
        "bqs": c(stacked(I["L0_xattn_bq"], none).T),
        "bks": c(stacked(I["L0_xattn_bk"], ones).T),
        "wv": c(I["L0_xattn_Wv"]),
        "bv": c(I["L0_xattn_bv"]),
        "wo": c(wo),
        "wop": c(wop.reshape(P, G, D)),
        "boX": c(I["L0_xattn_bo"]),
        "gateT": c(I["L0_ffn_gate_w"].T),
        "w1T": c(np.concatenate([s1, f1]).transpose(2, 0, 1)),
        "b1": c(np.concatenate([sb1, I["L0_ffn_fc1_b"].reshape(E, 2, P)]).transpose(2, 0, 1)),
        "mult": c(np.concatenate([I["L0_ffn_s_geglu_mult"].reshape(2, P), I["L0_ffn_geglu_mult"]]).T),
        "w2T": c(np.concatenate([s2, f2]).transpose(2, 0, 1)),
        "b2": c(np.concatenate([I["L0_ffn_fc2_b"], I["L0_ffn_s_fc2_b"][None]])),
    }
    nc = bacc.Bacc("TRN2", target_bir_lowering=False, num_devices=1)
    args = {n: nc.dram_tensor(n + "_d", v.shape, mybir.dt.from_np(v.dtype), kind="ExternalInput").ap() for n, v in arrays.items()}
    comb_dram = nc.dram_tensor("comb_d", (E, B, N), F32, kind="Internal").ap()
    out = nc.dram_tensor("out_d", (B, N, D), F32, kind="ExternalOutput").ap()
    build(nc, comb_dram=comb_dram, out=out, **args)
    r = run(nc, [{n + "_d": v for n, v in arrays.items()}], core_ids=[0])
    return r.results[0]["out_d"]
```
